# Optimizing a Trainium2 kernel written in Bass

```python
import numpy as np
import jax
import jax.numpy as jnp

def _softmax(x, axis=-1):
    return jax.nn.softmax(x, axis=axis)

def _gelu(x):
    return jax.nn.gelu(x, approximate=True)

def _silu(x):
    return jax.nn.silu(x)

def _sigmoid(x):
    return jax.nn.sigmoid(x)

def _layernorm(x, axis=-1, eps=1e-05):
    m = jnp.mean(x, axis=axis, keepdims=True)
    v = jnp.var(x, axis=axis, keepdims=True)
    return (x - m) / jnp.sqrt(v + eps)

def _scatter_add(tgt, idx, src, axis=0):
    return tgt.at[idx].add(src)

def _segment_sum(src, seg, n):
    return jax.ops.segment_sum(src, seg, n)
kernel_name = 'mk_perceiver_d1_seqx_r2_522e7c'

def setup_inputs(seed: int=0):
    np.random.seed(seed)
    _w = jnp.asarray

    def _rec_inputs():
        import jax
        import jax.numpy as jnp
        _rk = jax.random.key(seed)
        x = -0.0002928 + 1 * jax.random.normal(jax.random.fold_in(_rk, 1), (1, 256, 512), jnp.float32)
        _lenS = 256 - jax.random.randint(jax.random.fold_in(_rk, 7), (1,), 0, max(1, 256 // 4) + 1, jnp.int32)
        _lenS2 = 25088 - jax.random.randint(jax.random.fold_in(_rk, 8), (1,), 0, max(1, 25088 // 4) + 1, jnp.int32)
        _ctx_1024P = jax.random.normal(jax.random.fold_in(_rk, 11), (1, 16, 512), jnp.float32)
        _ctx_1024c = jax.random.dirichlet(jax.random.fold_in(_rk, 511), 0.3 * jnp.ones((16,), jnp.float32), (1, 25088))
        _ctx_1024t = jnp.einsum('bsk,bkd->bsd', _ctx_1024c, _ctx_1024P)
        _ctx_1024t = _ctx_1024t * jax.lax.rsqrt(jnp.mean(jnp.square(_ctx_1024t)) + 1e-12) * 0.953939
        ctx_1024 = -1.39393e-06 + 0.999914 * (_ctx_1024t + 0.3 * jax.random.normal(jax.random.fold_in(_rk, 611), (1, 25088, 512), jnp.float32))
        return (x, ctx_1024)
    x, ctx_1024 = _rec_inputs()

    def _L0_xattn_setup():
        import jax, jax.numpy as jnp
        import numpy as np
        NUM_HEADS = 16
        EPS = 1e-05

        def _layernorm(x, gamma, beta):
            mu = jnp.mean(x, axis=-1, keepdims=True)
            var = jnp.var(x, axis=-1, keepdims=True)
            return (x - mu) * jax.lax.rsqrt(var + EPS) * gamma + beta
        key = jax.random.key(seed)
        ks = jax.random.split(key, 10)
        B, L, C = (1, 2048, 512)
        D = C // NUM_HEADS
        s = 0.02
        return {'q': jax.random.normal(ks[0], (B, L, C), dtype=jnp.float32), 'k': jax.random.normal(ks[1], (B, L, C), dtype=jnp.float32), 'v': jax.random.normal(ks[2], (B, L, C), dtype=jnp.float32), 'Wq': jax.random.normal(ks[3], (C, C), dtype=jnp.float32) * s, 'Wk': jax.random.normal(ks[4], (C, C), dtype=jnp.float32) * s, 'Wv': jax.random.normal(ks[5], (C, C), dtype=jnp.float32) * s, 'gq': jnp.ones((D,), jnp.float32), 'bq': jnp.zeros((D,), jnp.float32), 'gk': jnp.ones((D,), jnp.float32), 'bk': jnp.zeros((D,), jnp.float32), 'Wp': jax.random.normal(ks[6], (C, C), dtype=jnp.float32) * s, 'bp': jnp.zeros((C,), jnp.float32)}
    _L0_xattn_all = _L0_xattn_setup()
    _L0_xattn_in = {k: v for k, v in _L0_xattn_all.items() if k in ('Wq', 'Wk', 'Wv', 'gq', 'bq', 'gk', 'bk', 'Wp', 'bp')}
    del _L0_xattn_all

    def _L0_attn_setup():
        import jax, jax.numpy as jnp
        import numpy as np
        B, L, E, H = (1, 2048, 512, 16)
        D = E // H
        EPS = 1e-06
        key = jax.random.key(seed)
        k1, k2, k3 = jax.random.split(key, 3)
        x = jax.random.normal(k1, (B, L, E), dtype=jnp.float32)
        qkv_w = jax.random.normal(k2, (E, 3 * E), dtype=jnp.float32) / np.sqrt(E)
        qkv_b = jnp.zeros((3 * E,), dtype=jnp.float32)
        out_w = jax.random.normal(k3, (E, E), dtype=jnp.float32) / np.sqrt(E)
        out_b = jnp.zeros((E,), dtype=jnp.float32)
        return {'x': x, 'qkv_w': qkv_w, 'qkv_b': qkv_b, 'out_w': out_w, 'out_b': out_b}
    _L0_attn_all = _L0_attn_setup()
    _L0_attn_in = {k: v for k, v in _L0_attn_all.items() if k in ('qkv_w', 'qkv_b', 'out_w', 'out_b')}
    del _L0_attn_all

    def _L0_ffn_setup():
        import jax, jax.numpy as jnp
        import numpy as np
        B, S, H, F, E, K = (2, 1024, 512, 2048, 8, 2)

        def _ln(x, g, b, eps=1e-05):
            m = jnp.mean(x, axis=-1, keepdims=True)
            v = jnp.var(x, axis=-1, keepdims=True)
            return (x - m) / jnp.sqrt(v + eps) * g + b

        def _gelu(x):
            return jax.nn.gelu(x, approximate=False)
        key = jax.random.key(seed)
        ks = jax.random.split(key, 12)
        F2 = F // 2
        return {'hidden_states': jax.random.normal(ks[0], (B, S, H), jnp.float32), 'ln_g': jnp.ones((H,), jnp.float32), 'ln_b': jnp.zeros((H,), jnp.float32), 'router_w': jax.random.normal(ks[1], (H, E), jnp.float32) * 0.01, 'up_W': jax.random.normal(ks[2], (E, H, F), jnp.float32) * 0.02, 'up_b': jnp.zeros((E, F), jnp.float32), 'down_W': jax.random.normal(ks[3], (E, F, H), jnp.float32) * 0.02, 'down_b': jnp.zeros((E, H), jnp.float32), 'spec0_W': jax.random.normal(ks[4], (2, F, F), jnp.float32) * 0.02, 'spec0_b': jnp.zeros((2, F), jnp.float32), 'ln0_g': jnp.ones((2, F), jnp.float32), 'ln0_b': jnp.zeros((2, F), jnp.float32), 'spec1a_W': jax.random.normal(ks[5], (2, F, F2), jnp.float32) * 0.02, 'spec1a_b': jnp.zeros((2, F2), jnp.float32), 'spec1b_W': jax.random.normal(ks[6], (2, F2, F), jnp.float32) * 0.02, 'spec1b_b': jnp.zeros((2, F), jnp.float32), 'ln1_g': jnp.ones((2, F), jnp.float32), 'ln1_b': jnp.zeros((2, F), jnp.float32), 'spec2_W': jax.random.normal(ks[7], (2, F, F), jnp.float32) * 0.02, 'spec2_b': jnp.zeros((2, F), jnp.float32)}
    _L0_ffn_all = _L0_ffn_setup()
    _L0_ffn_in = {k: v for k, v in _L0_ffn_all.items() if k in ('ln_g', 'ln_b', 'router_w', 'up_W', 'up_b', 'down_W', 'down_b', 'spec0_W', 'spec0_b', 'ln0_g', 'ln0_b', 'spec1a_W', 'spec1a_b', 'spec1b_W', 'spec1b_b', 'ln1_g', 'ln1_b', 'spec2_W', 'spec2_b')}
    del _L0_ffn_all
    return {'x': x, 'ctx_1024': ctx_1024, 'L0_xattn_Wq': _L0_xattn_in['Wq'], 'L0_xattn_Wk': _L0_xattn_in['Wk'], 'L0_xattn_Wv': _L0_xattn_in['Wv'], 'L0_xattn_gq': _L0_xattn_in['gq'], 'L0_xattn_bq': _L0_xattn_in['bq'], 'L0_xattn_gk': _L0_xattn_in['gk'], 'L0_xattn_bk': _L0_xattn_in['bk'], 'L0_xattn_Wp': _L0_xattn_in['Wp'], 'L0_xattn_bp': _L0_xattn_in['bp'], 'L0_attn_qkv_w': _L0_attn_in['qkv_w'], 'L0_attn_qkv_b': _L0_attn_in['qkv_b'], 'L0_attn_out_w': _L0_attn_in['out_w'], 'L0_attn_out_b': _L0_attn_in['out_b'], 'L0_ffn_ln_g': _L0_ffn_in['ln_g'], 'L0_ffn_ln_b': _L0_ffn_in['ln_b'], 'L0_ffn_router_w': _L0_ffn_in['router_w'], 'L0_ffn_up_W': _L0_ffn_in['up_W'], 'L0_ffn_up_b': _L0_ffn_in['up_b'], 'L0_ffn_down_W': _L0_ffn_in['down_W'], 'L0_ffn_down_b': _L0_ffn_in['down_b'], 'L0_ffn_spec0_W': _L0_ffn_in['spec0_W'], 'L0_ffn_spec0_b': _L0_ffn_in['spec0_b'], 'L0_ffn_ln0_g': _L0_ffn_in['ln0_g'], 'L0_ffn_ln0_b': _L0_ffn_in['ln0_b'], 'L0_ffn_spec1a_W': _L0_ffn_in['spec1a_W'], 'L0_ffn_spec1a_b': _L0_ffn_in['spec1a_b'], 'L0_ffn_spec1b_W': _L0_ffn_in['spec1b_W'], 'L0_ffn_spec1b_b': _L0_ffn_in['spec1b_b'], 'L0_ffn_ln1_g': _L0_ffn_in['ln1_g'], 'L0_ffn_ln1_b': _L0_ffn_in['ln1_b'], 'L0_ffn_spec2_W': _L0_ffn_in['spec2_W'], 'L0_ffn_spec2_b': _L0_ffn_in['spec2_b']}

def reference(x, ctx_1024, L0_xattn_Wq, L0_xattn_Wk, L0_xattn_Wv, L0_xattn_gq, L0_xattn_bq, L0_xattn_gk, L0_xattn_bk, L0_xattn_Wp, L0_xattn_bp, L0_attn_qkv_w, L0_attn_qkv_b, L0_attn_out_w, L0_attn_out_b, L0_ffn_ln_g, L0_ffn_ln_b, L0_ffn_router_w, L0_ffn_up_W, L0_ffn_up_b, L0_ffn_down_W, L0_ffn_down_b, L0_ffn_spec0_W, L0_ffn_spec0_b, L0_ffn_ln0_g, L0_ffn_ln0_b, L0_ffn_spec1a_W, L0_ffn_spec1a_b, L0_ffn_spec1b_W, L0_ffn_spec1b_b, L0_ffn_ln1_g, L0_ffn_ln1_b, L0_ffn_spec2_W, L0_ffn_spec2_b):
    import jax
    import jax.numpy as jnp

    def _L0_xattn_ref(q, k, v, Wq, Wk, Wv, gq, bq, gk, bk, Wp, bp):
        import jax, jax.numpy as jnp
        import numpy as np
        NUM_HEADS = 16
        EPS = 1e-05

        def _layernorm(x, gamma, beta):
            mu = jnp.mean(x, axis=-1, keepdims=True)
            var = jnp.var(x, axis=-1, keepdims=True)
            return (x - mu) * jax.lax.rsqrt(var + EPS) * gamma + beta
        B, Lq, C = q.shape
        Lk = k.shape[1]
        H = NUM_HEADS
        D = C // H
        scale = D ** (-0.5)
        qh = (q @ Wq.T).reshape(B, Lq, H, D).transpose(0, 2, 1, 3)
        kh = (k @ Wk.T).reshape(B, Lk, H, D).transpose(0, 2, 1, 3)
        vh = (v @ Wv.T).reshape(B, Lk, H, D).transpose(0, 2, 1, 3)
        qh = _layernorm(qh, gq, bq) * scale
        kh = _layernorm(kh, gk, bk)
        attn = jax.nn.sigmoid(jnp.einsum('bhqd,bhkd->bhqk', qh, kh))
        x = jnp.einsum('bhqk,bhkd->bhqd', attn, vh)
        x = x.transpose(0, 2, 1, 3).reshape(B, Lq, C)
        return x @ Wp.T + bp

    def _L0_attn_ref(x, qkv_w, qkv_b, out_w, out_b):
        import jax, jax.numpy as jnp
        import numpy as np
        B, L, E, H = (1, 2048, 512, 16)
        D = E // H
        EPS = 1e-06
        b, l, e = x.shape
        qkv = x @ qkv_w + qkv_b
        q, k, v = jnp.split(qkv, 3, axis=-1)
        q = q.reshape(b, l, H, D).transpose(0, 2, 1, 3)
        k = k.reshape(b, l, H, D).transpose(0, 2, 1, 3)
        v = v.reshape(b, l, H, D).transpose(0, 2, 1, 3)
        q_prime = jax.nn.elu(q) + 1.0
        k_prime = jax.nn.elu(k) + 1.0
        kv_prod = jnp.einsum('bhld,bhle->bhlde', k_prime, v)
        kv_cumsum = jnp.cumsum(kv_prod, axis=2)
        context = jnp.einsum('bhld,bhlde->bhle', q_prime, kv_cumsum)
        k_cumsum = jnp.cumsum(k_prime, axis=2)
        norm = jnp.einsum('bhld,bhld->bhl', q_prime, k_cumsum)
        output = context / (norm[..., None] + EPS)
        output = output.transpose(0, 2, 1, 3).reshape(b, l, e)
        return output @ out_w + out_b

    def _L0_ffn_ref(hidden_states, ln_g, ln_b, router_w, up_W, up_b, down_W, down_b, spec0_W, spec0_b, ln0_g, ln0_b, spec1a_W, spec1a_b, spec1b_W, spec1b_b, ln1_g, ln1_b, spec2_W, spec2_b):
        import jax, jax.numpy as jnp
        import numpy as np
        B, S, H, F, E, K = (2, 1024, 512, 2048, 8, 2)

        def _ln(x, g, b, eps=1e-05):
            m = jnp.mean(x, axis=-1, keepdims=True)
            v = jnp.var(x, axis=-1, keepdims=True)
            return (x - m) / jnp.sqrt(v + eps) * g + b

        def _gelu(x):
            return jax.nn.gelu(x, approximate=False)
        b, s, h = hidden_states.shape
        x = hidden_states.reshape(-1, h)
        nx = _ln(x, ln_g, ln_b)
        logits = nx @ router_w
        probs = jax.nn.softmax(logits, axis=-1)
        _, idx = jax.lax.top_k(probs, K)
        mask = jnp.sum(jax.nn.one_hot(idx, probs.shape[-1], dtype=probs.dtype), axis=1)
        w = probs * mask
        w = w / jnp.sum(w, axis=-1, keepdims=True)
        h1 = _gelu(jnp.einsum('th,ehf->etf', nx, up_W) + up_b[:, None, :])
        i0 = jnp.array([0, 4])
        i1 = jnp.array([1, 5])
        i2 = jnp.array([2, 6])
        s0 = _gelu(_ln(jnp.einsum('etf,efg->etg', h1[i0], spec0_W) + spec0_b[:, None, :], ln0_g[:, None, :], ln0_b[:, None, :]))
        t1 = _gelu(jnp.einsum('etf,efg->etg', h1[i1], spec1a_W) + spec1a_b[:, None, :])
        s1 = _ln(jnp.einsum('etg,egf->etf', t1, spec1b_W) + spec1b_b[:, None, :], ln1_g[:, None, :], ln1_b[:, None, :])
        s2 = _gelu(jnp.einsum('etf,efg->etg', h1[i2], spec2_W) + spec2_b[:, None, :])
        h2 = h1.at[i0].set(s0).at[i1].set(s1).at[i2].set(s2)
        out_e = jnp.einsum('etf,efh->eth', h2, down_W) + down_b[:, None, :]
        y = jnp.einsum('eth,te->th', out_e, w) + x
        return y.reshape(hidden_states.shape)
    x = x + _L0_xattn_ref(_layernorm(x, axis=-1), ctx_1024, ctx_1024, L0_xattn_Wq, L0_xattn_Wk, L0_xattn_Wv, L0_xattn_gq, L0_xattn_bq, L0_xattn_gk, L0_xattn_bk, L0_xattn_Wp, L0_xattn_bp)
    x = x + _L0_attn_ref(_layernorm(x, axis=-1), L0_attn_qkv_w, L0_attn_qkv_b, L0_attn_out_w, L0_attn_out_b)
    x = x + _L0_ffn_ref(_layernorm(x, axis=-1), L0_ffn_ln_g, L0_ffn_ln_b, L0_ffn_router_w, L0_ffn_up_W, L0_ffn_up_b, L0_ffn_down_W, L0_ffn_down_b, L0_ffn_spec0_W, L0_ffn_spec0_b, L0_ffn_ln0_g, L0_ffn_ln0_b, L0_ffn_spec1a_W, L0_ffn_spec1a_b, L0_ffn_spec1b_W, L0_ffn_spec1b_b, L0_ffn_ln1_g, L0_ffn_ln1_b, L0_ffn_spec2_W, L0_ffn_spec2_b)
    return x

_drawn_inputs = setup_inputs


def setup_inputs(seed=0):
    import zlib

    import numpy as np

    out = dict(_drawn_inputs(seed))
    spreads = {'L0_xattn_gq': (1.0, 0.2),
     'L0_xattn_bq': (0.0, 0.39),
     'L0_xattn_gk': (1.0, 0.2),
     'L0_xattn_bk': (0.0, 0.1),
     'L0_xattn_bp': (0.0, 0.8),
     'L0_attn_qkv_b': (0.0, 0.8),
     'L0_attn_out_b': (0.0, 0.8),
     'L0_ffn_ln_g': (1.0, 0.6),
     'L0_ffn_ln_b': (0.0, 0.8),
     'L0_ffn_up_b': (0.0, 0.8),
     'L0_ffn_down_b': (0.0, 0.8),
     'L0_ffn_spec0_b': (0.0, 0.1),
     'L0_ffn_ln0_g': (1.0, 0.2),
     'L0_ffn_ln0_b': (0.0, 0.1),
     'L0_ffn_spec1a_b': (0.0, 0.8),
     'L0_ffn_spec1b_b': (0.0, 0.8),
     'L0_ffn_ln1_g': (1.0, 0.6),
     'L0_ffn_ln1_b': (0.0, 0.8),
     'L0_ffn_spec2_b': (0.0, 0.8)}
    factors = {'L0_attn_qkv_w': 8.0,
     'L0_attn_out_w': 8.0,
     'L0_ffn_router_w': 8.0,
     'L0_ffn_up_W': 8.0,
     'L0_ffn_down_W': 8.0,
     'L0_ffn_spec1a_W': 8.0,
     'L0_ffn_spec1b_W': 8.0,
     'L0_ffn_spec2_W': 8.0}
    for name, (base, spread) in spreads.items():
        noise = np.random.default_rng([zlib.crc32(name.encode()), seed]).standard_normal(out[name].shape)
        drawn = base * np.exp(spread * noise) if base else spread * noise
        out[name] = jnp.asarray(drawn.astype(out[name].dtype))
    for name, factor in factors.items():
        out[name] = (out[name] * factor).astype(out[name].dtype)
    return out
```

```python
from contextlib import ExitStack

import concourse.bass as bass
from concourse import mybir

TOK, C, H, D = 256, 512, 16, 32
NK = 25088
P = 128
TT, CT = TOK // P, C // P
KT = NK // P
HG = P // D
NG = H // HG
F, E, HALVES = 2048, 8, 2
FT = F // P
UNROLL = 4
CHUNK = 2048
WR = 4
RAW = 2

LAYERS = [
    ("up0", "gelu", 4, "xn", "h1", 0, False),
    ("spec0", "norm", 16, "h1", "pre", 0, True),
    ("up1", "gelu", 4, "xn", "h1", 1, False),
    ("down0", "down", 16, "h2", "y", 0, False),
    ("spec1a", "gelu", 16, "h1", "h2", 1, False),
    ("spec1b", "norm", 8, "h2", "pre", 1, True),
    ("up2", "gelu", 4, "xn", "h2", 2, False),
    ("down1", "down", 16, "h1", "y", 1, False),
    ("spec2", "gelu", 16, "h2", "h1", 2, True),
    ("up3", "gelu", 4, "xn", "h2", 3, True),
    ("down2", "down", 16, "h1", "y", 2, False),
    ("down3", "down", 16, "h2", "y", 3, False),
]
OUT_TILES = {"up0": 16, "up1": 16, "up2": 16, "up3": 16, "spec0": 16, "spec1a": 8, "spec1b": 16,
             "spec2": 16, "down0": 0, "down1": 0, "down2": 0, "down3": 0}
NORM_OUT = {"spec0": "h2", "spec1b": "h1"}
NORM_AFTER = {"up1": "spec0", "up2": "spec1b"}


def layer_chunks(name, kt):
    return (E // HALVES) if name.startswith("down") else OUT_TILES[name] * kt * P // CHUNK


NORMS = ["spec0", "spec1b"]
CHUNKS = {n: layer_chunks(n, kt) for n, _, kt, *_ in LAYERS}
CHUNKS_HALF = sum(CHUNKS.values())
TILES_HALF = sum(OUT_TILES.values())
EARLY = {n: max(0, OUT_TILES[n] - CHUNKS[n]) for n in CHUNKS}
EARLY_HALF = sum(EARLY.values())
CHUNK_BASE, FILL_BASE, EARLY_BASE, STAGE_BASE, GATED_BASE = {}, {}, {}, {}, {}
_stage = _gated = 0
for _n, _kind, _kt, _src, _dst, _e, _last in LAYERS:
    CHUNK_BASE[_n] = sum(CHUNKS[m] for m in CHUNK_BASE)
    FILL_BASE[_n] = sum(OUT_TILES[m] for m in FILL_BASE)
    EARLY_BASE[_n] = sum(EARLY[m] for m in EARLY_BASE)
    for _m in ([_n] if _kind == "gelu" else []) + ([NORM_AFTER[_n]] if _n in NORM_AFTER else []):
        STAGE_BASE[_m] = _stage
        _stage += OUT_TILES[_m]
        if _last or _m in NORMS:
            GATED_BASE[_m] = _gated
            _gated += OUT_TILES[_m]
GATED_HALF = _gated
SOURCE = {"spec0": "up0", "spec1a": "up1", "spec1b": "spec1a", "spec2": "up2",
          "down0": "spec0", "down1": "spec1b", "down2": "spec2", "down3": "up3"}
COLS, BIAS_COLS = {}, 0
for _n, _per in (("up_b", 4 * FT), ("spec0_b", FT), ("ln0_g", FT), ("ln0_b", FT), ("spec1a_b", 8),
                 ("spec1b_b", FT), ("ln1_g", FT), ("ln1_b", FT), ("spec2_b", FT)):
    COLS[_n] = (BIAS_COLS, _per)
    BIAS_COLS += 2 * _per
BIAS = {"up0": ("up_b", 0), "up1": ("up_b", 1), "up2": ("up_b", 2), "up3": ("up_b", 3),
        "spec0": ("spec0_b", 0), "spec1a": ("spec1a_b", 0), "spec1b": ("spec1b_b", 0),
        "spec2": ("spec2_b", 0)}


def perceiver_block(nc, a, out, NKT=KT):
    f32, f32r = mybir.dt.float32, mybir.dt.float32r
    ALU, ACT, AX = mybir.AluOpType, mybir.ActivationFunctionType, mybir.AxisListType.X
    nq = (NKT - 4) // UNROLL
    life = ExitStack()
    with life:
        def sb(name, shape, dt=f32, scope=life):
            return scope.enter_context(nc.sbuf_tensor(name, shape, dt))

        def ps(name, shape, scope):
            return scope.enter_context(nc.psum_tensor(name, shape, f32))

        def sem(name):
            return life.enter_context(nc.semaphore(name))

        named = {}

        def once(name):
            if name not in named:
                named[name] = sem(name)
            return named[name]

        setup = ExitStack()
        wq = sb("wq", [P, CT, C], f32, setup)
        wk = sb("wk_rows", [P, CT, C], f32, setup)
        wv = sb("wv", [P, CT, C], f32, setup)
        centre = sb("centre", [P, P], f32, setup)
        head_vecs = sb("head_vecs", [P, 4, D], f32, setup)
        x_t = sb("x_t", [P, CT, TOK], f32, setup)
        big = [sb(f"setup_big{i}", [P, TT, C], f32, setup) for i in range(2)]
        q_parts = sb("q_parts", [P, TT, H, 4, D], f32, setup)
        setup.close()

        w_hi = [sb(f"w_hi{i}", [P, CHUNK], f32r) for i in range(WR)]
        w_lo = [sb(f"w_lo{i}", [P, CHUNK], f32r) for i in range(WR)]
        w_raw = [sb(f"w_raw{i}", [P, CHUNK]) for i in range(RAW)]
        x = sb("x_rows", [P, TT, C])
        xn = sb("x_norm", [P, TT, C])
        ident = sb("ident", [P, P])
        neg_half = sb("neg_half", [P, 1])
        stat = sb("stat", [P, 4, 32])

        attn = ExitStack()
        raw = [sb(f"ctx_raw{i}", [P, CT, P], f32, attn) for i in range(4)]
        ctx_hi = [sb(f"ctx_hi{i}", [P, CT, P], f32r, attn) for i in range(2)]
        ctx_lo = [sb(f"ctx_lo{i}", [P, CT, P], f32r, attn) for i in range(2)]
        wk_hi = sb("wk_hi", [P, CT, C], f32r, attn)
        wk_lo = sb("wk_lo", [P, CT, C], f32r, attn)
        wv_hi = sb("wv_hi", [P, CT, C], f32r, attn)
        wv_lo = sb("wv_lo", [P, CT, C], f32r, attn)
        q4 = sb("q4", [P, H, TOK], f32r, attn)
        k_sq = sb("k_sq", [P, H, D], f32, attn)
        k_var = sb("k_var", [P, 3, H], f32, attn)
        k_eps = sb("k_eps", [P, 1], f32, attn)
        k_n = sb("k_n", [P, H, D - 1], f32, attn)
        k_hl = [sb(f"k_hl{i}", [P, H, 4, D], f32, attn) for i in range(2)]
        kT = [sb(f"kT{g}", [P, HG * P], f32r, attn) for g in range(NG)]
        v_sb = [sb(f"v_sb{i}", [P, C], f32, attn) for i in range(2)]
        probs = [sb(f"probs{g}", [P, HG, TOK], f32, attn) for g in range(NG)]
        zeros = sb("zeros", [P, C], f32, attn)
        psum_a = ExitStack()
        o_ps = ps("o_ps", [P, NG, TOK], psum_a)
        kv_ps = ps("kv_ps", [P, 2, C], psum_a)
        s_ps = ps("s_ps", [P, HG, TOK], psum_a)
        t_ps = ps("t_ps", [P, 2, HG * P], psum_a)
        psum_a.close()
        attn.close()

        mid = ExitStack()
        o_t = sb("o_t", [P, NG, TOK], f32, mid)
        wp = sb("wp", [P, CT, C], f32, mid)
        qkv_w = sb("qkv_w", [P, CT, 3 * C], f32, mid)
        qkv = sb("qkv", [P, TT, 3 * C], f32, mid)
        rows = sb("bias_rows", [P, 5, C], f32, mid)
        out_w = sb("out_w", [P, CT, C], f32, mid)
        qk_min = sb("qk_min", [P, TT, 2 * C], f32, mid)
        qk_max = sb("qk_max", [P, TT, 2 * C], f32, mid)
        v_one = sb("v_one", [P, TT, H, D + 1], f32, mid)
        qk_t = sb("qk_t", [P, 2, NG, TOK], f32, mid)
        mid_t = sb("mid_t", [P, CT, TOK], f32, mid)
        causal = sb("causal", [P, TOK + P], f32, mid)
        masked = [sb(f"masked{i}", [P, TOK + P], f32, mid) for i in range(4)]
        mid_a = sb("mid_a", [P, TT, C], f32, mid)
        mid_b = sb("mid_b", [P, TT, C], f32, mid)
        mid.close()
        psum_m = ExitStack()
        pm = ps("pm", [P, 4, 512], psum_m)
        po = ps("po", [P, 4, 512], psum_m)
        psum_m.close()

        ffn = ExitStack()
        hid = {n: (sb(f"{n}_hi", [P, FT, TOK], f32r, ffn), sb(f"{n}_lo", [P, FT, TOK], f32r, ffn))
               for n in ("h1", "h2")}
        pre = sb("pre", [P, FT, TOK], f32, ffn)
        stage = [sb(f"stage{i}", [P, TOK], f32, ffn) for i in range(4)]
        sq = [sb(f"sq{i}", [P, 4, TOK], f32, ffn) for i in range(2)]
        hid["xn"] = (sb("xn_hi", [P, CT, TOK], f32r, ffn), sb("xn_lo", [P, CT, TOK], f32r, ffn))
        gate = sb("gate", [P, E, TOK], f32, ffn)
        gate_t = sb("gate_t", [E, TOK], f32, ffn)
        down_b = sb("down_b", [E, C], f32, ffn)
        mean_w = sb("mean_w", [P, P], f32, ffn)
        moment = sb("moment", [P, 2, TOK], f32, ffn)
        vec = sb("bias_cols", [P, BIAS_COLS], f32, ffn)
        router_w = sb("router_w", [P, CT, E], f32, ffn)
        rt = sb("router_tmp", [P, 8, TT, E], f32, ffn)
        cmp = [sb(f"router_cmp{i}", [P, TT, E, E], f32, ffn) for i in range(2)]
        lower = sb("lower", [P, E, E], f32, ffn)
        psum_f = ExitStack()
        y_ps = ps("y_ps", [P, TT, C], psum_f)
        f_ps = ps("f_ps", [P, 4, 512], psum_f)
        m_ps = ps("m_ps", [P, 2, 512], psum_f)
        psum_f.close()
        ffn.close()

        def as_rows(t):
            return t.rearrange("p a b -> p (a b)").rearrange("p (t c) -> p t c", t=TT)

        nx_t, nx, r_b = pre[:, 0:CT], as_rows(pre[:, 8:12]), as_rows(pre[:, 12:16])
        lnv, r_a = as_rows(sq[0][:]), as_rows(sq[1][:])

        raw_in = [sem(f"raw_in{i}") for i in range(4)]
        ctx_hi_made, ctx_lo_made = sem("ctx_hi_made"), sem("ctx_lo_made")
        k_made, v_made = sem("k_made"), sem("v_made")
        k_sq_made, k_sum_made = sem("k_sq_made"), sem("k_sum_made")
        k_var_made, k_dev_made = sem("k_var_made"), sem("k_dev_made")
        k_normed, k_hi_made, k_split = sem("k_normed"), sem("k_hi_made"), sem("k_split")
        t_made, kt_made = sem("t_made"), sem("kt_made")
        s_made, probs_made, av_made = sem("s_made"), sem("probs_made"), sem("av_made")
        v_copied = sem("v_copied")
        w_in = [sem(f"w_in{i}") for i in range(RAW)]
        w_hi_made, w_lo_made, w_used = sem("w_hi_made"), sem("w_lo_made"), sem("w_used")
        f_made = sem("f_made")
        f_read = sem("f_read")
        gated = sem("gated")
        h_hi_made, h_made = sem("h_hi_made"), sem("h_made")
        mean_made, mean_copied, centred = sem("mean_made"), sem("mean_copied"), sem("centred")
        sq_made, sq_used = sem("sq_made"), sem("sq_used")
        var_copied, dev_made, scaled = sem("var_copied"), sem("dev_made"), sem("scaled")
        applied = sem("applied")
        done = sem("done")

        def wait(eng, s, v):
            if not isinstance(v, int) or v > 0:
                eng.wait_ge(s, v)

        def n_of(it, r, per=1, more=0):
            if isinstance(it, int):
                return per * (4 * it + r) + more
            return it * (4 * per) + (per * r + more)

        def at(half, per_half, q, per_q, more):
            v = half * per_half + more
            return v if isinstance(q, int) and q == 0 else v + q * per_q

        def one(t, i):
            return t[:, i] if isinstance(i, int) else t[:, bass.ds(i, 1)].rearrange("p o t -> p (o t)")

        def per_row(ap2, n):
            return ap2.unsqueeze(2).to_broadcast([ap2.shape[0], ap2.shape[1], n])

        def repeat(ap2, n):
            return ap2.unsqueeze(1).to_broadcast([ap2.shape[0], n, ap2.shape[1]])

        def quads(eng, name, kt):
            n = layer_chunks(name, kt) // 4
            if n == 1:
                yield 0
            else:
                with eng.Fori(0, n) as q:
                    yield q

        block = life.enter_context(nc.Block())

        @block.sync
        def _(sp):
            for name, dst in (("x", x), ("wq", wq), ("wk", wk), ("wv", wv), ("head_vecs", head_vecs)):
                sp.dma_start(dst[:], a[name]).then_inc(once(name + "_in"), 16)

            def load_ctx(it, r):
                wait(sp, ctx_lo_made, n_of(it, r, 1, -3))
                t = n_of(it, r)
                tile = a["ctx"][t] if isinstance(t, int) else \
                    a["ctx"][bass.ds(t, 1)].rearrange("o p n -> (o p) n")
                sp.dma_start(raw[r][:].rearrange("p a b -> p (a b)"), tile).then_inc(raw_in[r], 16)

            for r in range(4):
                load_ctx(0, r)
            for i in range(RAW):
                sp.dma_start(w_raw[i][:], a["w"][i]).then_inc(w_in[i], 16)
            with sp.Fori(1, NKT // 4) as it:
                for r in range(4):
                    load_ctx(it, r)
            sp.wait_ge(av_made, NG * (NKT + 1))
            for name, dst in (("wp", wp), ("bias_rows", rows), ("qkv_w", qkv_w), ("out_w", out_w)):
                sp.dma_start(dst[:], a[name]).then_inc(once(name + "_in"), 16)
            sp.wait_ge(once("x2_made"), 1)
            for name, dst in (("ln_rows", lnv), ("router_w", router_w), ("down_b", down_b),
                              ("bias_cols", vec)):
                sp.dma_start(dst[:], a[name]).then_inc(once(name + "_in"), 16)
            with sp.Fori(1, HALVES * CHUNKS_HALF // RAW) as it:
                for i in range(RAW):
                    sp.wait_ge(w_lo_made, it * RAW + (i - RAW + 1))
                    sp.dma_start(w_raw[i][:], a["w"][bass.ds(it * RAW + i, 1)]
                                 .rearrange("o p n -> (o p) n")).then_inc(w_in[i], 16)
            sp.wait_ge(once("result"), 1)
            sp.dma_start(out, x[:]).then_inc(done, 16)
            sp.wait_ge(done, 16)

        @block.gpsimd
        def _(pool):
            g = nc.gpsimd
            own, count = sem("pool_own"), [0]

            def link(ins):
                count[0] += 1
                ins.then_inc(own, 1)
                pool.wait_ge(own, count[0])

            def deviations(n, tag):
                pool.wait_ge(once(tag + "_var"), 1)
                g.tensor_tensor(stat[:, 2, 0:n], stat[:, 3, 0:n], neg_half[:].to_broadcast([P, n]),
                                ALU.pow).then_inc(once(tag + "_dev"), 1)

            link(g.memset(neg_half[:], -0.5))
            link(g.memset(k_eps[:], 1e-5))
            link(g.memset(ident[:], 0.0))
            link(g.affine_select(out=ident[:], in_=ident[:], compare_op=ALU.not_equal, fill=1.0,
                                 base=0, pattern=[[-1, P]], channel_multiplier=1))
            c3 = centre[:].rearrange("p (b d) -> p b d", b=HG)
            link(g.memset(centre[:], -1.0 / D))
            link(g.affine_select(out=c3, in_=c3, compare_op=ALU.is_ge, fill=0.0, base=0,
                                 pattern=[[-D, HG], [0, D]], channel_multiplier=1))
            link(g.affine_select(out=c3, in_=c3, compare_op=ALU.is_ge, fill=0.0, base=D - 1,
                                 pattern=[[D, HG], [0, D]], channel_multiplier=-1))
            g.tensor_tensor(centre[:], centre[:], ident[:], ALU.add).then_inc(once("consts"), 1)
            for i in range(2):
                link(g.memset(k_hl[i][:], 0.0))
                link(g.memset(k_hl[i][:, :, 0:3:2, D - 1:D], 1.0))
            g.memset(zeros[:], 0.0).then_inc(once("zeros_made"), 1)
            deviations(TT, "x")
            deviations(TT * H, "q")

            def low_part(it, r):
                pool.wait_ge(ctx_hi_made, n_of(it, r, 1, 1))
                wait(pool, v_made, n_of(it, r, 1, -1))
                g.tensor_tensor(ctx_lo[r % 2][:], raw[r % 4][:], ctx_hi[r % 2][:].bitcast(f32),
                                ALU.subtract).then_inc(ctx_lo_made, 1)

            def deviation(it, r):
                pool.wait_ge(k_sum_made, n_of(it, r, 1, 1))
                g.tensor_tensor(k_var[:, 1], k_var[:, 0], k_eps[:].to_broadcast([P, H]), ALU.add)\
                    .then_inc(k_var_made, 1)
                pool.wait_ge(k_var_made, n_of(it, r, 1, 1))
                wait(pool, k_normed, n_of(it, r))
                g.tensor_tensor(k_var[:, 2], k_var[:, 1], neg_half[:].to_broadcast([P, H]), ALU.pow)\
                    .then_inc(k_dev_made, 1)

            def step(it, r, last=False):
                if not last:
                    low_part(it, r + 1)
                deviation(it, r)

            low_part(0, 0)
            step(0, 0)
            step(0, 1)
            with pool.Fori(0, nq) as it:
                for r in range(2, 6):
                    step(it, r)
            step(nq, 2)
            step(nq, 3, last=True)

            pool.wait_ge(once("attention_done"), 1)
            link(g.memset(causal[:], 1.0))
            for first, n in ((0, TOK), (TOK, P)):
                link(g.affine_select(out=causal[:, first:first + n], in_=causal[:, first:first + n],
                                     compare_op=ALU.is_ge, fill=0.0, base=0, pattern=[[1, n]],
                                     channel_multiplier=-1))
            g.memset(v_one[:, :, :, D:D + 1], 1.0).then_inc(once("mid_consts"), 1)
            deviations(TT, "x1")
            pool.wait_ge(once("x2_made"), 1)
            link(g.memset(mean_w[:], 1.0 / F))
            link(g.memset(lower[:], 1.0))
            g.affine_select(out=lower[:], in_=lower[:], compare_op=ALU.is_ge, fill=0.0, base=-1,
                            pattern=[[1, E], [-1, E]], channel_multiplier=0)\
                .then_inc(once("router_consts"), 1)
            deviations(TT, "x2")
            deviations(TT, "nx")
            pool.sem_inc(h_made, 4)

            def low_tiles(half, dst, base):
                def make(q):
                    for i in range(4):
                        pool.wait_ge(h_hi_made, at(half, TILES_HALF, q, 4, base + i + 1))
                        hi, lo = (one(t, q * 4 + i) for t in hid[dst])
                        g.tensor_tensor(lo, stage[i][:], hi.bitcast(f32), ALU.subtract)\
                            .then_inc(h_made, 1)
                return make

            with pool.Fori(0, HALVES) as half:
                for name, kind, kt, src, dst, e, last in LAYERS:
                    if kind == "gelu":
                        make = low_tiles(half, dst, STAGE_BASE[name])
                        with pool.Fori(0, OUT_TILES[name] // 4) as q:
                            make(q)
                    if name in NORM_AFTER:
                        norm = NORM_AFTER[name]
                        pool.wait_ge(var_copied, half * 2 + (NORMS.index(norm) + 1))
                        g.tensor_tensor(moment[:, 1], moment[:, 1],
                                        neg_half[:].to_broadcast([P, TOK]), ALU.pow)\
                            .then_inc(dev_made, 1)
                        make = low_tiles(half, NORM_OUT[norm], STAGE_BASE[norm])
                        with pool.Fori(0, FT // 4) as q:
                            make(q)

        @block.scalar
        def _(act):
            s = nc.scalar

            def sigmoid(it, r, grp):
                act.wait_ge(s_made, n_of(it, r, NG, grp + 1))
                act.wait_ge(av_made, n_of(it, r, NG, grp + 1))
                s.activation(probs[grp][:], s_ps[:], ACT.Sigmoid).then_inc(probs_made, 1)

            def square(it, r):
                act.wait_ge(k_made, n_of(it, r, 1, 1))
                wait(act, k_sum_made, n_of(it, r))
                s.activation(k_sq[:].rearrange("p h d -> p (h d)"), kv_ps[:, 0], ACT.Square,
                             scale=float(D) ** -0.5).then_inc(k_sq_made, 1)

            def step(it, r, first=False, last=False):
                if not first:
                    if not (isinstance(it, int) and 4 * it + r == 1):
                        sigmoid(it, r - 2, 3)
                    sigmoid(it, r - 1, 0)
                if not last:
                    square(it, r)
                if not first:
                    sigmoid(it, r - 1, 1)
                    sigmoid(it, r - 1, 2)

            step(0, 0, first=True)
            step(0, 1)
            with act.Fori(0, nq) as it:
                for r in range(2, 6):
                    step(it, r)
            step(nq, 2)
            step(nq, 3)
            step(nq, 4, last=True)
            sigmoid(nq, 3, 3)

            act.wait_ge(once("qk_min_made"), 1)
            s.activation(qk_min[:], qk_min[:], ACT.Exp).then_inc(once("qk_exp"), 1)
            act.wait_ge(once("logits_less_max"), 1)
            s.activation(rt[:, 1], rt[:, 0], ACT.Exp).then_inc(once("router_exp"), 1)
            act.sem_inc(f_read, 4)
            act.wait_ge(once("bias_cols_in"), 16)

            def high(half, q, base, i):
                act.wait_ge(w_in[i % RAW], at(half, 8 * CHUNKS_HALF, q, 32, 8 * base + 16 * (i // 2 + 1)))
                act.wait_ge(w_used, at(half, CHUNKS_HALF, q, 4, base + i + 1))
                s.activation(w_hi[i][:], w_raw[i % RAW][:], ACT.Copy).then_inc(w_hi_made, 1)

            def column(key, half, q, per_q, more):
                first, per = COLS[key]
                i = at(half, per, q, per_q, first + more)
                return vec[:, i:i + 1] if isinstance(i, int) else vec[:, bass.ds(i, 1)]

            with act.Fori(0, HALVES) as half:
                for i in range(4):
                    high(half, 0, 0, i)
                for name, kind, kt, src, dst, e, last in LAYERS:
                    if kind == "down" and name == LAYERS[-1][0]:
                        continue
                    per = OUT_TILES[name] // layer_chunks(name, kt)
                    for q in quads(act, name, kt):
                        for i in range(4):
                            for j in range(per):
                                n = i * per + j
                                slot = n % 4
                                if j < per - 1:
                                    act.wait_ge(f_made, at(half, EARLY_HALF, q, 4 * (per - 1),
                                                           EARLY_BASE[name] + i * (per - 1) + j + 1))
                                else:
                                    act.wait_ge(w_used, at(half, CHUNKS_HALF, q, 4,
                                                           CHUNK_BASE[name] + i + 1 + 4))
                                bias = column(BIAS[name][0], half, q, 4 * per, BIAS[name][1] * FT + n)
                                if kind == "gelu":
                                    act.wait_ge(h_made, at(half, TILES_HALF, q, 4 * per,
                                                           STAGE_BASE[name] + n + 1))
                                    s.activation(stage[slot][:], f_ps[:, slot, 0:TOK], ACT.Gelu,
                                                 bias=bias).then_inc(f_read, 1)
                                else:
                                    s.activation(one(pre, q * (4 * per) + n if not isinstance(q, int)
                                                     else n), f_ps[:, slot, 0:TOK],
                                                 ACT.Identity, bias=bias).then_inc(f_read, 1)
                            high(half, q, CHUNK_BASE[name] + 4, i)
                    if name in NORM_AFTER:
                        norm = NORM_AFTER[name]
                        k0 = NORMS.index(norm)
                        for k in range(4):
                            act.wait_ge(centred, half * 8 + (4 * k0 + k + 1))
                            act.wait_ge(sq_used, half * 8 + (4 * k0 + k + 1))
                            s.activation(sq[k % 2][:], pre[:, 4 * k:4 * k + 4], ACT.Square)\
                                .then_inc(sq_made, 1)
                        with act.Fori(0, 4) as q:
                            act.wait_ge(scaled, at(half, 8, q, 1, 4 * k0 + 1))
                            for i in range(4):
                                act.wait_ge(h_made, at(half, TILES_HALF, q, 4, STAGE_BASE[norm] + i + 1))
                                s.activation(stage[i][:], one(pre, q * 4 + i),
                                             ACT.Gelu if k0 == 0 else ACT.Identity,
                                             bias=column(f"ln{k0}_b", half, q, 4, i),
                                             scale=column(f"ln{k0}_g", half, q, 4, i))\
                                    .then_inc(applied, 1)

        @block.vector
        def _(dve):
            v = nc.vector
            own, count = sem("dve_own"), [0]

            def link(ins):
                count[0] += 1
                ins.then_inc(own, 1)
                dve.wait_ge(own, count[0])
                return ins

            def layernorm(dst, src, cen, sqr, eps, tag):
                n, w = dst.shape[1], dst.shape[2]
                link(v.tensor_reduce(stat[:, 1, 0:n], src, AX, ALU.add))
                link(v.tensor_scalar(stat[:, 0, 0:n], stat[:, 1, 0:n], 1.0 / w, None, ALU.mult))
                link(v.tensor_tensor(cen, src, per_row(stat[:, 0, 0:n], w), ALU.subtract))
                link(v.tensor_tensor(sqr, cen, cen, ALU.mult))
                link(v.tensor_reduce(stat[:, 1, 0:n], sqr, AX, ALU.add))
                v.tensor_scalar(stat[:, 3, 0:n], stat[:, 1, 0:n], 1.0 / w, eps, ALU.mult, ALU.add)\
                    .then_inc(once(tag + "_var"), 1)
                dve.wait_ge(once(tag + "_dev"), 1)
                link(v.tensor_tensor(dst, cen, per_row(stat[:, 2, 0:n], w), ALU.mult))

            dve.wait_ge(once("x_in"), 16)
            layernorm(xn[:], x[:], big[0][:], big[1][:], 1e-5, "x")
            dve.sem_inc(once("xn_made"), 1)
            dve.wait_ge(once("wv_in"), 16)
            link(v.tensor_copy(wv_hi[:], wv[:]))
            v.tensor_tensor(wv_lo[:], wv[:], wv_hi[:].bitcast(f32), ALU.subtract)\
                .then_inc(once("wv_split"), 1)
            dve.wait_ge(once("xn_turned"), 1)
            v.tensor_copy(x_t[:], s_ps[:]).then_inc(once("x_t_made"), 1)
            dve.wait_ge(once("wk_centred"), 1)
            for c in range(CT):
                wk_ps = (t_ps[:, c % 2] if c < 2 else
                         o_ps[:, 2 * (c % 2):2 * (c % 2) + 2].rearrange("p g t -> p (g t)"))
                link(v.tensor_copy(wk_hi[:, c], wk_ps))
                link(v.tensor_tensor(wk_lo[:, c], wk_ps, wk_hi[:, c].bitcast(f32), ALU.subtract))
            dve.sem_inc(once("wk_split"), 1)
            dve.wait_ge(once("q_made"), 1)
            heads = [b[:].rearrange("p t (h d) -> p (t h) d", h=H) for b in big]
            qn, tmp = heads
            layernorm(qn, kv_ps[:].rearrange("p t (h d) -> p (t h) d", h=H), qn, tmp, 1e-5, "q")
            dve.wait_ge(once("head_vecs_in"), 16)
            gq, bq, gk, bk = (repeat(head_vecs[:, i], TT * H) for i in range(4))
            link(v.tensor_tensor(qn, qn, gq, ALU.mult))
            link(v.tensor_tensor(qn, qn, bq, ALU.add))
            link(v.tensor_scalar(big[0][:], big[0][:], float(D) ** -0.5, None, ALU.mult))
            link(v.tensor_tensor(tmp, qn, bk, ALU.mult))
            link(v.tensor_reduce(stat[:, 0, 0:TT * H], tmp, AX, ALU.add))
            link(v.tensor_tensor(qn, qn, gk, ALU.mult))
            link(v.tensor_tensor(tmp[:, :, 0:D - 1], qn[:, :, 0:D - 1],
                                 qn[:, :, D - 1:D].to_broadcast([P, TT * H, D - 1]), ALU.subtract))
            link(v.tensor_copy(tmp[:, :, D - 1], stat[:, 0, 0:TT * H]))
            parts = q_parts[:].rearrange("p t h a d -> p (t h) a d")
            link(v.tensor_copy(parts[:, :, 0].bitcast(f32r), tmp))
            link(v.tensor_tensor(parts[:, :, 2], tmp, parts[:, :, 0], ALU.subtract))
            link(v.tensor_copy(parts[:, :, 1], parts[:, :, 0]))
            v.tensor_copy(parts[:, :, 3], parts[:, :, 2]).then_inc(once("q_split"), 1)
            for grp in range(NG):
                dve.wait_ge(once("q_turned"), grp + 1)
                v.tensor_copy(q4[:, HG * grp:HG * grp + HG], s_ps[:]).then_inc(once("q4_made"), 1)

            def high_part(it, r):
                if isinstance(it, int):
                    dve.wait_ge(raw_in[r % 4], 16 * (it + r // 4 + 1))
                else:
                    dve.wait_ge(raw_in[r % 4], it * 16 + 16 * (r // 4 + 1))
                wait(dve, v_made, n_of(it, r, 1, -1))
                v.tensor_copy(ctx_hi[r % 2][:], raw[r % 4][:]).then_inc(ctx_hi_made, 1)

            def copy_turned(it, r, grp):
                dve.wait_ge(t_made, n_of(it, r, NG, grp + 1))
                wait(dve, s_made, n_of(it, r, NG, grp - 3))
                v.tensor_copy(kT[grp][:], t_ps[:, grp % 2]).then_inc(kt_made, 1)

            def copy_values(it, r):
                dve.wait_ge(v_made, n_of(it, r, 1, 1))
                wait(dve, av_made, n_of(it, r, NG))
                v.tensor_copy(v_sb[r % 2][:], kv_ps[:, 1]).then_inc(v_copied, 1)

            def sum_squares(it, r):
                dve.wait_ge(k_sq_made, n_of(it, r, 1, 1))
                v.tensor_reduce(k_var[:, 0], k_sq[:], AX, ALU.add).then_inc(k_sum_made, 1)

            def normalise(it, r):
                dve.wait_ge(k_dev_made, n_of(it, r, 1, 1))
                keys = kv_ps[:, 0].rearrange("p (h d) -> p h d", h=H)[:, :, 0:D - 1]
                v.tensor_tensor(k_n[:], keys, per_row(k_var[:, 2], D - 1), ALU.mult)\
                    .then_inc(k_normed, 1)
                dve.wait_ge(k_normed, n_of(it, r, 1, 1))
                hi, lo = (k_hl[r % 2][:, :, i:i + 3:2, 0:D - 1] for i in range(2))
                twice = k_n[:].unsqueeze(2).to_broadcast([P, H, 2, D - 1])
                wait(dve, t_made, n_of(it, r, NG, -NG))
                v.tensor_copy(hi.bitcast(f32r), twice).then_inc(k_hi_made, 1)
                dve.wait_ge(k_hi_made, n_of(it, r, 1, 1))
                v.tensor_tensor(lo, twice, hi, ALU.subtract).then_inc(k_split, 1)

            def step(it, r, first=False, last=False):
                if not first:
                    copy_turned(it, r - 1, 0)
                    copy_values(it, r - 1)
                if not last:
                    high_part(it, r + 1)
                if not first:
                    copy_turned(it, r - 1, 1)
                sum_squares(it, r)
                if not first:
                    copy_turned(it, r - 1, 2)
                normalise(it, r)
                if not first:
                    copy_turned(it, r - 1, 3)

            high_part(0, 0)
            step(0, 0, first=True)
            step(0, 1)
            with dve.Fori(0, nq) as it:
                for r in range(2, 6):
                    step(it, r)
            step(nq, 2)
            step(nq, 3, last=True)
            copy_turned(nq, 3, 0)
            copy_values(nq, 3)
            for grp in range(1, NG):
                copy_turned(nq, 3, grp)

            dve.wait_ge(av_made, NG * (NKT + 1))
            v.tensor_copy(o_t[:], o_ps[:]).then_inc(once("attention_done"), 1)
            dve.wait_ge(once("cross_made"), 1)
            dve.wait_ge(once("bias_rows_in"), 16)
            link(v.tensor_tensor(x[:], x[:], pm[:, 0:TT], ALU.add))
            link(v.tensor_tensor(x[:], x[:], repeat(rows[:, 0], TT), ALU.add))
            layernorm(xn[:], x[:], mid_a[:], mid_b[:], 1e-5, "x1")
            dve.sem_inc(once("x1n_made"), 1)
            dve.wait_ge(once("x1n_turned"), 1)
            v.tensor_copy(mid_t[:], po[:, 0:2].rearrange("p a (b c) -> p (a b) c", b=2))\
                .then_inc(once("x1_t_made"), 1)
            for i in range(TT):
                dve.wait_ge(once("qkv_made"), i + 1)
                last = link(v.tensor_tensor(qkv[:, i], pm[:, 0:3].rearrange("p a b -> p (a b)"),
                                            rows[:, 2:5].rearrange("p a b -> p (a b)"), ALU.add))
                dve.sem_inc(once("qkv_copied"), 1)
            v.tensor_scalar(qk_min[:], qkv[:, :, 0:2 * C], 0.0, None, ALU.min)\
                .then_inc(once("qk_min_made"), 1)
            link(v.tensor_scalar(qk_max[:], qkv[:, :, 0:2 * C], 0.0, None, ALU.max))
            dve.wait_ge(once("mid_consts"), 1)
            for i in range(TT):
                link(v.tensor_copy(v_one[:, i, :, 0:D],
                                   qkv[:, i, 2 * C:3 * C].rearrange("p (h d) -> p h d", h=H)))
            dve.wait_ge(once("qk_exp"), 1)
            v.tensor_tensor(qk_max[:], qk_max[:], qk_min[:], ALU.add).then_inc(once("qk_made"), 1)
            for i in range(2):
                dve.wait_ge(once("qk_turned"), i + 1)
                v.tensor_copy(qk_t[:, i], pm[:, 2 * i:2 * i + 2].rearrange("p a (b c) -> p (a b) c", b=2))\
                    .then_inc(once("qk_t_made"), 1)
            for h in range(H):
                dve.wait_ge(once("lin_scores"), h + 1)
                wait(dve, once("lin_used"), h - 3)
                v.tensor_tensor(masked[h % 4][:], pm[:, h % 4, 0:TOK + P], causal[:], ALU.mult)\
                    .then_inc(once("lin_masked"), 1)
            dve.wait_ge(once("lin_used"), H)
            for i in range(TT):
                for k in range(2):
                    o = po[:, 2 * i + k, 0:8 * (D + 1)].rearrange("p (h d) -> p h d", h=8)
                    link(v.tensor_scalar(stat[:, 0, 0:8], o[:, :, D], 1e-6, None, ALU.add))
                    link(v.reciprocal(stat[:, 1, 0:8], stat[:, 0, 0:8]))
                    link(v.tensor_tensor(mid_a[:, i, k * 256:k * 256 + 256]
                                         .rearrange("p (h d) -> p h d", h=8),
                                         o[:, :, 0:D], per_row(stat[:, 1, 0:8], D), ALU.mult))
            dve.sem_inc(once("lin_made"), 1)
            dve.wait_ge(once("lin_turned"), 1)
            v.tensor_copy(mid_t[:], pm[:, 0:2].rearrange("p a (b c) -> p (a b) c", b=2))\
                .then_inc(once("lin_t_made"), 1)
            dve.wait_ge(once("self_made"), 1)
            link(v.tensor_tensor(x[:], x[:], pm[:, 2:4], ALU.add))
            v.tensor_tensor(x[:], x[:], repeat(rows[:, 1], TT), ALU.add).then_inc(once("x2_made"), 1)
            dve.wait_ge(once("x2_made"), 1)
            layernorm(xn[:], x[:], r_a, r_b, 1e-5, "x2")
            layernorm(nx, xn[:], r_a, r_b, 1e-5, "nx")
            dve.wait_ge(once("ln_rows_in"), 16)
            link(v.tensor_tensor(nx, nx, repeat(lnv[:, 0], TT), ALU.mult))
            v.tensor_tensor(nx, nx, repeat(lnv[:, 1], TT), ALU.add).then_inc(once("nx_made"), 1)
            dve.wait_ge(once("nx_turned"), 1)
            v.tensor_copy(nx_t, f_ps[:, 0:2].rearrange("p a (b c) -> p (a b) c", b=2))\
                .then_inc(once("nx_t_made"), 1)
            dve.wait_ge(once("nx_t_made"), 1)
            link(v.tensor_copy(hid["xn"][0][:], nx_t))
            v.tensor_tensor(hid["xn"][1][:], nx_t, hid["xn"][0][:].bitcast(f32), ALU.subtract)\
                .then_inc(once("xn_split"), 1)
            dve.wait_ge(once("logits"), 1)
            lg = m_ps[:, 0, 0:TT * E].rearrange("p (t e) -> p t e", t=TT)
            link(v.tensor_reduce(rt[:, 2, :, 0], lg, AX, ALU.max))
            v.tensor_tensor(rt[:, 0], lg, per_row(rt[:, 2, :, 0], E), ALU.subtract)\
                .then_inc(once("logits_less_max"), 1)
            dve.wait_ge(once("router_exp"), 1)
            link(v.tensor_reduce(rt[:, 2, :, 0], rt[:, 1], AX, ALU.add))
            link(v.reciprocal(rt[:, 2, :, 1], rt[:, 2, :, 0]))
            link(v.tensor_tensor(rt[:, 3], rt[:, 1], per_row(rt[:, 2, :, 1], E), ALU.mult))
            dve.wait_ge(once("router_consts"), 1)
            for i in range(TT):
                mine = per_row(rt[:, 3, i], E)
                others = repeat(rt[:, 3, i], E)
                link(v.tensor_tensor(cmp[0][:, i], others, mine, ALU.is_gt))
                link(v.tensor_tensor(cmp[1][:, i], others, mine, ALU.is_equal))
                link(v.tensor_tensor(cmp[1][:, i], cmp[1][:, i], lower[:], ALU.mult))
                link(v.tensor_tensor(cmp[0][:, i], cmp[0][:, i], cmp[1][:, i], ALU.add))
                link(v.tensor_reduce(rt[:, 4, i], cmp[0][:, i], AX, ALU.add))
            link(v.tensor_scalar(rt[:, 4], rt[:, 4], 2.0, None, ALU.is_lt))
            link(v.tensor_tensor(rt[:, 5], rt[:, 4], rt[:, 3], ALU.mult))
            link(v.tensor_reduce(rt[:, 2, :, 0], rt[:, 5], AX, ALU.add))
            link(v.reciprocal(rt[:, 2, :, 1], rt[:, 2, :, 0]))
            v.tensor_tensor(rt[:, 5], rt[:, 5], per_row(rt[:, 2, :, 1], E), ALU.mult)\
                .then_inc(once("gates"), 1)
            dve.wait_ge(once("gates_turned"), 1)
            v.tensor_copy(gate_t[:], m_ps[0:E, 1, 0:TOK]).then_inc(once("gate_t_made"), 1)
            for k in range(2):
                dve.wait_ge(once("gates_spread"), k + 1)
                v.tensor_copy(gate[:, 4 * k:4 * k + 4],
                              f_ps[:, 2 * k:2 * k + 2].rearrange("p a (b c) -> p (a b) c", b=2))\
                    .then_inc(once("gates_copied"), 1)
            dve.wait_ge(once("gates_copied"), 2)

            def low(half, q, base, i):
                dve.wait_ge(w_hi_made, at(half, CHUNKS_HALF, q, 4, base + i + 1))
                v.tensor_tensor(w_lo[i][:], w_raw[i % RAW][:], w_hi[i][:].bitcast(f32), ALU.subtract)\
                    .then_inc(w_lo_made, 1)

            def high_tile(half, q, per_q, name, dst, e, last, n, gates_before):
                if name in NORMS:
                    dve.wait_ge(applied, at(half, 2 * FT, q, per_q, FT * e + n + 1))
                else:
                    dve.wait_ge(f_read, at(half, TILES_HALF, q, per_q, FILL_BASE[name] + n + 1 + 4))
                tile = stage[n % 4][:]
                if last:
                    v.tensor_tensor(tile, tile, one(gate, half * (E // 2) + e), ALU.mult)\
                        .then_inc(gated, 1)
                    dve.wait_ge(gated, at(half, GATED_HALF, q, per_q, gates_before + n + 1))
                i = n if isinstance(q, int) else q * per_q + n
                v.tensor_copy(one(hid[dst][0], i), tile).then_inc(h_hi_made, 1)

            def free(half, dst, name):
                order = [l[0] for l in LAYERS]
                k = order.index(name)
                readers = [l[0] for l in LAYERS if l[3] == dst]
                before = [n for n in readers if order.index(n) < k]
                if before:
                    end = CHUNK_BASE[before[-1]] + CHUNKS[before[-1]]
                else:
                    end = CHUNK_BASE[readers[-1]] + CHUNKS[readers[-1]]
                    dve.wait_ge(w_used, half * end + 4)
                    return
                dve.wait_ge(w_used, half * CHUNKS_HALF + (4 + end))

            with dve.Fori(0, HALVES) as half:
                for i in range(4):
                    low(half, 0, 0, i)
                for name, kind, kt, src, dst, e, last in LAYERS:
                    if kind == "down" and name == LAYERS[-1][0]:
                        continue
                    per = OUT_TILES[name] // layer_chunks(name, kt)
                    for q in quads(dve, name, kt):
                        if kind == "gelu":
                            free(half, dst, name)
                        for i in range(4):
                            if kind == "gelu":
                                for j in range(per):
                                    high_tile(half, q, 4 * per, name, dst, e, last, i * per + j,
                                              GATED_BASE.get(name))
                            low(half, q, CHUNK_BASE[name] + 4, i)
                    if kind == "norm":
                        k0 = NORMS.index(name)
                        dve.wait_ge(mean_made, half * 2 + (k0 + 1))
                        v.tensor_copy(moment[:, 0], m_ps[:, 0, 0:TOK]).then_inc(mean_copied, 1)
                        dve.wait_ge(mean_copied, half * 2 + (k0 + 1))
                        for k in range(4):
                            part = pre[:, 4 * k:4 * k + 4]
                            v.tensor_tensor(part, part, repeat(moment[:, 0], 4), ALU.subtract)\
                                .then_inc(centred, 1)
                    if name in NORM_AFTER:
                        norm = NORM_AFTER[name]
                        k0 = NORMS.index(norm)
                        dve.wait_ge(sq_used, half * 8 + (4 * k0 + 4 + 2))
                        v.tensor_scalar(moment[:, 1], m_ps[:, 1, 0:TOK], 1e-5, None, ALU.add)\
                            .then_inc(var_copied, 1)
                        dve.wait_ge(dev_made, half * 2 + (k0 + 1))
                        for k in range(4):
                            part = pre[:, 4 * k:4 * k + 4]
                            v.tensor_tensor(part, part, repeat(moment[:, 1], 4), ALU.mult)\
                                .then_inc(scaled, 1)
                        with dve.Fori(0, 4) as q:
                            free(half, NORM_OUT[norm], name)
                            for i in range(4):
                                high_tile(half, q, 4, norm, NORM_OUT[norm], k0, True, i,
                                          GATED_BASE[norm])
            link(v.tensor_tensor(x[:], x[:], xn[:], ALU.add))
            dve.wait_ge(w_used, 4 + HALVES * CHUNKS_HALF)
            v.tensor_tensor(x[:], x[:], y_ps[:], ALU.add).then_inc(once("result"), 1)

        @block.tensor
        def _(pe):
            t = nc.tensor

            def turn_rows(dst, src_rows):
                for i in range(TT):
                    for c in range(CT):
                        ins = t.transpose(dst(c, i), src_rows[:, i, c * P:(c + 1) * P], ident[:])
                return ins

            pe.wait_ge(once("consts"), 1)
            pe.wait_ge(once("wk_in"), 16)
            for c in range(CT):
                for b in range(CT):
                    dst = (t_ps[:, c % 2, b * P:(b + 1) * P] if c < 2 else
                           o_ps[:, 2 * (c % 2) + b // 2, (b % 2) * P:(b % 2 + 1) * P])
                    ins = t.matmul(dst, wk[:, b, c * P:(c + 1) * P], centre[:], start=True, stop=True)
            ins.then_inc(once("wk_centred"), 1)
            pe.wait_ge(once("xn_made"), 1)
            turn_rows(lambda c, i: s_ps[:, c, i * P:(i + 1) * P], xn).then_inc(once("xn_turned"), 1)
            pe.wait_ge(once("x_t_made"), 1)
            pe.wait_ge(once("wq_in"), 16)
            for i in range(TT):
                for c in range(CT):
                    ins = t.matmul(kv_ps[:, i], x_t[:, c, i * P:(i + 1) * P], wq[:, c],
                                   start=(c == 0), stop=(c == CT - 1))
            ins.then_inc(once("q_made"), 1)
            pe.wait_ge(once("q_split"), 1)
            for grp in range(NG):
                wait(pe, once("q4_made"), grp)
                for h in range(HG):
                    for i in range(TT):
                        ins = t.transpose(s_ps[:, h, i * P:(i + 1) * P],
                                          q_parts[:, i, HG * grp + h].rearrange("p a d -> p (a d)"),
                                          ident[:])
                ins.then_inc(once("q_turned"), 1)
            pe.wait_ge(once("zeros_made"), 1)
            pe.wait_ge(once("wk_split"), 1)
            for i in range(2):
                ins = t.matmul(o_ps[:, 2 * i:2 * i + 2].rearrange("p g t -> p (g t)"), zeros[:, 0:P],
                               zeros[:], start=True, stop=True)
            ins.then_inc(av_made, NG)
            pe.wait_ge(once("wv_split"), 1)
            pe.wait_ge(once("q4_made"), NG)

            def project(it, r, which, c, n):
                hi, lo = ((wk_hi, wk_lo), (wv_hi, wv_lo))[which]
                left, right = ((ctx_hi, hi), (ctx_lo, hi), (ctx_hi, lo))[n]
                ins = t.matmul(kv_ps[:, which], left[r % 2][:, c], right[:, c],
                               start=(c == 0 and n == 0), stop=(c == CT - 1 and n == 2))
                if c == CT - 1 and n == 2:
                    ins.then_inc((k_made, v_made)[which], 1)

            def projection(it, r, first, last):
                for m in range(first, last):
                    if m == 0:
                        pe.wait_ge(ctx_lo_made, n_of(it, r, 1, 1))
                        wait(pe, k_normed, n_of(it, r))
                    if m == 12:
                        wait(pe, v_copied, n_of(it, r))
                    project(it, r, m // 12, m % 12 // 3, m % 3)

            def turn_keys(it, r, grp):
                if grp == 0:
                    pe.wait_ge(k_split, n_of(it, r, 1, 1))
                wait(pe, kt_made, n_of(it, r, NG, grp - 1))
                for h in range(HG):
                    parts = k_hl[r % 2][:, HG * grp + h].rearrange("p a d -> p (a d)")
                    ins = t.transpose(t_ps[:, grp % 2, h * P:(h + 1) * P], parts, ident[:])
                ins.then_inc(t_made, 1)

            def scores(it, r, grp):
                pe.wait_ge(kt_made, n_of(it, r, NG, grp + 1))
                wait(pe, probs_made, n_of(it, r, NG, grp))
                for h in range(HG):
                    ins = t.matmul(s_ps[:, h], kT[grp][:, h * P:(h + 1) * P], q4[:, HG * grp + h],
                                   start=True, stop=True)
                ins.then_inc(s_made, 1)

            def attend(it, r, grp):
                pe.wait_ge(probs_made, n_of(it, r, NG, grp + 1))
                pe.wait_ge(v_copied, n_of(it, r, 1, 1))
                for h in range(HG):
                    ins = t.matmul(o_ps[D * h:D * h + D, grp], v_sb[r % 2][:, P * grp + D * h:P * grp + D * h + D],
                                   probs[grp][:, h], start=False, stop=False, skip_group_check=True)
                ins.then_inc(av_made, 1)

            SPLIT = (0, 8, 14, 19, 24)

            def step(it, r, project_it=True):
                second = isinstance(it, int) and 4 * it + r == 1
                for q in range(4):
                    a0, a1 = SPLIT[q], SPLIT[q + 1]
                    half_way = (a0 + a1) // 2
                    if project_it:
                        projection(it, r, a0, half_way)
                    if q > 0:
                        scores(it, r - 1, q - 1)
                    elif not second:
                        scores(it, r - 2, 3)
                    if project_it:
                        projection(it, r, half_way, a1)
                    turn_keys(it, r - 1, q)
                    if q > 1:
                        attend(it, r - 1, q - 2)
                    elif not second:
                        attend(it, r - 2, q + 2)

            projection(0, 0, 0, 24)
            step(0, 1)
            with pe.Fori(0, nq) as it:
                for r in range(2, 6):
                    step(it, r)
            step(nq, 2)
            step(nq, 3)
            step(nq, 4, project_it=False)
            scores(nq, 3, 3)
            attend(nq, 3, 2)
            attend(nq, 3, 3)

            pe.wait_ge(once("attention_done"), 1)
            pe.wait_ge(once("wp_in"), 16)
            for i in range(TT):
                for c in range(CT):
                    ins = t.matmul(pm[:, i], o_t[:, c, i * P:(i + 1) * P], wp[:, c],
                                   start=(c == 0), stop=(c == CT - 1))
            ins.then_inc(once("cross_made"), 1)
            pe.wait_ge(once("x1n_made"), 1)
            turn_rows(lambda c, i: po[:, c // 2, (c % 2) * TOK + i * P:(c % 2) * TOK + (i + 1) * P], xn)\
                .then_inc(once("x1n_turned"), 1)
            pe.wait_ge(once("x1_t_made"), 1)
            pe.wait_ge(once("qkv_w_in"), 16)
            for i in range(TT):
                wait(pe, once("qkv_copied"), i)
                for k in range(3):
                    for c in range(CT):
                        ins = t.matmul(pm[:, k], mid_t[:, c, i * P:(i + 1) * P],
                                       qkv_w[:, c, k * C:(k + 1) * C], start=(c == 0), stop=(c == CT - 1))
                ins.then_inc(once("qkv_made"), 1)
            pe.wait_ge(once("qk_made"), 1)
            for k in range(2):
                for i in range(TT):
                    for grp in range(NG):
                        first = (grp % 2) * TOK + i * P
                        ins = t.transpose(pm[:, 2 * k + grp // 2, first:first + P],
                                          qk_max[:, i, k * C + grp * P:k * C + (grp + 1) * P], ident[:])
                ins.then_inc(once("qk_turned"), 1)

            def lin_scores(h):
                grp, first = h // HG, D * (h % HG)
                q, k = (qk_t[first:first + D, i, grp] for i in range(2))
                pe.wait_ge(once("qk_t_made"), 2)
                wait(pe, once("lin_masked"), h - 3)
                t.matmul(pm[:, h % 4, 0:TOK], k[:, 0:P], q, start=True, stop=True)
                t.matmul(pm[:, h % 4, TOK:TOK + P], k[:, P:TOK], q[:, P:TOK], start=True, stop=True)\
                    .then_inc(once("lin_scores"), 1)

            def lin_values(h):
                pe.wait_ge(once("lin_masked"), h + 1)
                m, first = masked[h % 4], (h % 8) * (D + 1)
                out_of = [po[:, 2 * i + h // 8, first:first + D + 1] for i in range(TT)]
                t.matmul(out_of[0], m[:, 0:P], v_one[:, 0, h], start=True, stop=True)
                t.matmul(out_of[1], m[:, P:TOK], v_one[:, 0, h], start=True, stop=False)
                t.matmul(out_of[1], m[:, TOK:TOK + P], v_one[:, 1, h], start=False, stop=True)\
                    .then_inc(once("lin_used"), 1)

            for h in range(3):
                lin_scores(h)
            for h in range(H):
                if h + 3 < H:
                    lin_scores(h + 3)
                lin_values(h)
            pe.wait_ge(once("lin_made"), 1)
            turn_rows(lambda c, i: pm[:, c // 2, (c % 2) * TOK + i * P:(c % 2) * TOK + (i + 1) * P], mid_a)\
                .then_inc(once("lin_turned"), 1)
            pe.wait_ge(once("lin_t_made"), 1)
            pe.wait_ge(once("out_w_in"), 16)
            for i in range(TT):
                for c in range(CT):
                    ins = t.matmul(pm[:, 2 + i], mid_t[:, c, i * P:(i + 1) * P], out_w[:, c],
                                   start=(c == 0), stop=(c == CT - 1))
            ins.then_inc(once("self_made"), 1)
            pe.wait_ge(once("nx_made"), 1)
            turn_rows(lambda c, i: f_ps[:, c // 2, (c % 2) * TOK + i * P:(c % 2) * TOK + (i + 1) * P], nx)\
                .then_inc(once("nx_turned"), 1)
            pe.wait_ge(once("nx_t_made"), 1)
            pe.wait_ge(once("router_w_in"), 16)
            for i in range(TT):
                for c in range(CT):
                    ins = t.matmul(m_ps[:, 0, i * E:(i + 1) * E], nx_t[:, c, i * P:(i + 1) * P],
                                   router_w[:, c], start=(c == 0), stop=(c == CT - 1))
            ins.then_inc(once("logits"), 1)
            pe.wait_ge(once("gates"), 1)
            for i in range(TT):
                ins = t.transpose(m_ps[0:E, 1, i * P:(i + 1) * P], rt[:, 5, i], ident[:])
            ins.then_inc(once("gates_turned"), 1)
            pe.wait_ge(once("gate_t_made"), 1)
            for e in range(E):
                ins = t.matmul(f_ps[:, e // 2, (e % 2) * TOK:(e % 2 + 1) * TOK],
                               ident[0:E, e:e + 1].to_broadcast([E, P]), gate_t[:], start=True, stop=True)
                if e % 4 == 3:
                    ins.then_inc(once("gates_spread"), 1)
            pe.wait_ge(once("down_b_in"), 16)
            for i in range(TT):
                ins = t.matmul(y_ps[:, i], gate_t[:, i * P:(i + 1) * P], down_b[:], start=True, stop=True)
            ins.then_inc(w_used, 4)
            pe.sem_inc(sq_used, 2)
            pe.wait_ge(once("gates_copied"), 2)

            with pe.Fori(0, HALVES) as half:
                for name, kind, kt, src, dst, e, last in LAYERS:
                    s_hi, s_lo = hid[src]
                    per = OUT_TILES[name] // layer_chunks(name, kt)
                    if src == "xn":
                        pe.wait_ge(once("xn_split"), 1)

                    def source(k):
                        if src != "xn":
                            made = STAGE_BASE[SOURCE[name]] + k + 1 + 4
                            pe.wait_ge(h_made, half * TILES_HALF + made)

                    for q in quads(pe, name, kt):
                        for i in range(4):
                            pe.wait_ge(w_lo_made, at(half, CHUNKS_HALF, q, 4, CHUNK_BASE[name] + i + 1))
                            if kind == "down":
                                hi, lo = (w[i][:].rearrange("p (f n) -> p f n", f=4) for w in (w_hi, w_lo))
                                for j in range(4):
                                    source(4 * i + j)
                                    for tt in range(TT):
                                        rows_ = slice(tt * P, (tt + 1) * P)
                                        for l, w in ((s_hi, hi), (s_lo, hi), (s_hi, lo)):
                                            ins = t.matmul(y_ps[:, tt], l[:, 4 * i + j, rows_], w[:, j],
                                                           start=False, stop=False, skip_group_check=True)
                            for j in range(per):
                                n = i * per + j
                                slot = n % 4
                                pe.wait_ge(f_read, at(half, TILES_HALF, q, 4 * per, FILL_BASE[name] + n + 1))
                                hi, lo = (w[i][:].rearrange("p (k n) -> p k n", k=kt) for w in (w_hi, w_lo))
                                cols = slice(j * P, (j + 1) * P)
                                for k in range(kt):
                                    if i == 0 and j == 0:
                                        source(k)
                                    for m, (w, r) in enumerate(((hi, s_hi), (hi, s_lo), (lo, s_hi))):
                                        ins = t.matmul(f_ps[:, slot, 0:TOK], w[:, k, cols], r[:, k],
                                                       start=(k == 0 and m == 0),
                                                       stop=(k == kt - 1 and m == 2))
                                if j < per - 1:
                                    ins.then_inc(f_made, 1)
                            ins.then_inc(w_used, 1)
                    if kind == "norm":
                        k0 = NORMS.index(name)
                        for k in range(FT):
                            pe.wait_ge(f_read, half * TILES_HALF + (FILL_BASE[name] + k + 1 + 4))
                            ins = t.matmul(m_ps[:, 0, 0:TOK], mean_w[:], pre[:, k],
                                           start=(k == 0), stop=(k == FT - 1))
                        ins.then_inc(mean_made, 1)
                    if name in NORM_AFTER:
                        k0 = NORMS.index(NORM_AFTER[name])
                        for k in range(FT):
                            pe.wait_ge(sq_made, half * 8 + (4 * k0 + k // 4 + 1))
                            ins = t.matmul(m_ps[:, 1, 0:TOK], mean_w[:], sq[k // 4 % 2][:, k % 4],
                                           start=(k == 0), stop=(k == FT - 1))
                            if k % 4 == 3:
                                ins.then_inc(sq_used, 1)


def kernel(**inputs):
    import numpy as np
    import concourse.bacc as bacc
    from concourse.bass_utils import run_bass_kernel_spmd as run

    i = {k: np.asarray(v) for k, v in inputs.items()}
    f = {k[len("L0_ffn_"):]: v for k, v in i.items() if k.startswith("L0_ffn_")}
    xa = {k[len("L0_xattn_"):]: v for k, v in i.items() if k.startswith("L0_xattn_")}

    def chunks(w):
        return w.reshape(-1, P, w.shape[1]).transpose(1, 0, 2)

    def stream(w, name):
        k, n = w.shape
        if name == "down":
            return w.reshape(E // HALVES, 4, P, n).transpose(0, 2, 1, 3).reshape(-1, P, CHUNK)
        kt = k // P
        return w.reshape(kt, P, -1, CHUNK // kt).transpose(2, 1, 0, 3).reshape(-1, P, CHUNK)

    def columns(v):
        return v.reshape(-1, P).T

    spec = {"spec0": "spec0_W", "spec1a": "spec1a_W", "spec1b": "spec1b_W", "spec2": "spec2_W"}
    w = []
    for half in range(HALVES):
        for name, kind, kt, src, dst, e, last in LAYERS:
            if name.startswith("up"):
                w.append(stream(f["up_W"][half * 4 + e], "up"))
            elif kind == "down":
                w.append(stream(f["down_W"][half * 4 + e], "down"))
            else:
                w.append(stream(f[spec[name]][half], name))
    arrays = {
        "x": chunks(i["x"][0]),
        "ctx": i["ctx_1024"][0].reshape(KT, P, CT, P).transpose(0, 3, 2, 1).reshape(KT, P, C),
        "wq": chunks(xa["Wq"].T),
        "wk": chunks(xa["Wk"]),
        "wv": chunks(xa["Wv"].T),
        "wp": chunks(xa["Wp"].T),
        "head_vecs": np.broadcast_to(np.stack([xa["gq"], xa["bq"], xa["gk"], xa["bk"]]), (P, 4, D)),
        "bias_rows": np.broadcast_to(
            np.concatenate([xa["bp"], i["L0_attn_out_b"], i["L0_attn_qkv_b"]]).reshape(5, C), (P, 5, C)),
        "qkv_w": chunks(i["L0_attn_qkv_w"]),
        "out_w": chunks(i["L0_attn_out_w"]),
        "ln_rows": np.broadcast_to(np.stack([f["ln_g"], f["ln_b"]]), (P, 2, C)),
        "router_w": chunks(f["router_w"]),
        "down_b": f["down_b"],
        "bias_cols": np.concatenate([columns(f[n]) for n in (
            "up_b", "spec0_b", "ln0_g", "ln0_b", "spec1a_b", "spec1b_b", "ln1_g", "ln1_b", "spec2_b")],
            axis=1),
        "w": np.concatenate(w),
    }
    arrays = {k: np.ascontiguousarray(v) for k, v in arrays.items()}
    nc = bacc.Bacc("TRN2", target_bir_lowering=False, num_devices=1)
    given = {k: nc.dram_tensor(k + "_dram", v.shape, mybir.dt.from_np(v.dtype), kind="ExternalInput").ap()
             for k, v in arrays.items()}
    out = nc.dram_tensor("out_dram", (P, TT, C), mybir.dt.float32, kind="ExternalOutput").ap()
    perceiver_block(nc, given, out)
    r = run(nc, [{k + "_dram": v for k, v in arrays.items()}], core_ids=[0])
    return r.results[0]["out_dram"].transpose(1, 0, 2).reshape(1, TOK, C)
```

```python
from contextlib import ExitStack

import concourse.bass as bass
from concourse import mybir

TOK, C, H, D = 256, 512, 16, 32
NK = 25088
P = 128
TT, CT = TOK // P, C // P
KT = NK // P
HG = P // D
NG = H // HG
F, E, HALVES = 2048, 8, 2
FT = F // P
UNROLL = 4
CHUNK = 2048
WR = 4
RAW = 2

LAYERS = [
    ("up0", "gelu", 4, "xn", "h1", 0, False),
    ("spec0", "norm", 16, "h1", "pre", 0, True),
    ("up1", "gelu", 4, "xn", "h1", 1, False),
    ("spec1a", "gelu", 16, "h1", "h2", 1, False),
    ("spec1b", "norm", 8, "h2", "pre", 1, True),
    ("down0", "down", 16, "h1", "y", 0, False),
    ("up2", "gelu", 4, "xn", "h2", 2, False),
    ("spec2", "gelu", 16, "h2", "h1", 2, True),
    ("down2", "down", 16, "h1", "y", 2, False),
    ("down1", "down", 16, "h2", "y", 1, False),
    ("up3", "gelu", 4, "xn", "h1", 3, True),
    ("down3", "down", 16, "h1", "y", 3, False),
]
OUT_TILES = {"up0": 16, "up1": 16, "up2": 16, "up3": 16, "spec0": 16, "spec1a": 8, "spec1b": 16,
             "spec2": 16, "down0": 0, "down1": 0, "down2": 0, "down3": 0}
NORMS = ["spec0", "spec1b"]
NORM_OUT = {"spec0": "h1", "spec1b": "h2"}
STEPS = {
    ("up1", "second"): ("mean", "spec0"), ("up1", "end"): ("squares", "spec0"),
    ("spec1a", "four"): ("variance", "spec0"), ("spec1a", "end"): ("apply", "spec0"),
    ("down0", "second"): ("mean", "spec1b"), ("down0", "end"): ("squares", "spec1b"),
    ("up2", "end"): ("variance", "spec1b"), ("spec2", "end"): ("apply", "spec1b"),
}
NORM_AFTER = {layer: norm for (layer, _), (step, norm) in STEPS.items() if step == "apply"}


def layer_chunks(name, kt):
    return (E // HALVES) if name.startswith("down") else OUT_TILES[name] * kt * P // CHUNK


ROOT_STEPS = 4
ROOT_OPS = 3 + 3 * ROOT_STEPS
CHUNKS = {n: layer_chunks(n, kt) for n, _, kt, *_ in LAYERS}
CHUNKS_HALF = sum(CHUNKS.values())
TILES_HALF = sum(OUT_TILES.values())
EARLY = {n: max(0, OUT_TILES[n] - CHUNKS[n]) for n in CHUNKS}
EARLY_HALF = sum(EARLY.values())
CHUNK_BASE, FILL_BASE, EARLY_BASE, STAGE_BASE, GATED_BASE = {}, {}, {}, {}, {}
_stage = _gated = 0
for _n, _kind, _kt, _src, _dst, _e, _last in LAYERS:
    CHUNK_BASE[_n] = sum(CHUNKS[m] for m in CHUNK_BASE)
    FILL_BASE[_n] = sum(OUT_TILES[m] for m in FILL_BASE)
    EARLY_BASE[_n] = sum(EARLY[m] for m in EARLY_BASE)
    for _m in ([_n] if _kind == "gelu" else []) + ([NORM_AFTER[_n]] if _n in NORM_AFTER else []):
        STAGE_BASE[_m] = _stage
        _stage += OUT_TILES[_m]
        if _last or _m in NORMS:
            GATED_BASE[_m] = _gated
            _gated += OUT_TILES[_m]
GATED_HALF = _gated
SOURCE = {"spec0": "up0", "spec1a": "up1", "spec1b": "spec1a", "spec2": "up2",
          "down0": "spec0", "down1": "spec1b", "down2": "spec2", "down3": "up3"}
COLS, BIAS_COLS = {}, 0
for _n, _per in (("up_b", 4 * FT), ("spec0_b", FT), ("ln0_g", FT), ("ln0_b", FT), ("spec1a_b", 8),
                 ("spec1b_b", FT), ("ln1_g", FT), ("ln1_b", FT), ("spec2_b", FT)):
    COLS[_n] = (BIAS_COLS, _per)
    BIAS_COLS += 2 * _per
BIAS = {"up0": ("up_b", 0), "up1": ("up_b", 1), "up2": ("up_b", 2), "up3": ("up_b", 3),
        "spec0": ("spec0_b", 0), "spec1a": ("spec1a_b", 0), "spec1b": ("spec1b_b", 0),
        "spec2": ("spec2_b", 0)}


def perceiver_block(nc, a, out, NKT=KT):
    f32, f32r = mybir.dt.float32, mybir.dt.float32r
    ALU, ACT, AX = mybir.AluOpType, mybir.ActivationFunctionType, mybir.AxisListType.X
    nq = (NKT - 4) // UNROLL
    life = ExitStack()
    with life:
        def sb(name, shape, dt=f32, scope=life):
            return scope.enter_context(nc.sbuf_tensor(name, shape, dt))

        def ps(name, shape, scope):
            return scope.enter_context(nc.psum_tensor(name, shape, f32))

        def sem(name):
            return life.enter_context(nc.semaphore(name))

        named = {}

        def once(name):
            if name not in named:
                named[name] = sem(name)
            return named[name]

        setup = ExitStack()
        wq = sb("wq", [P, CT, C], f32, setup)
        wk = sb("wk_rows", [P, CT, C], f32, setup)
        wv = sb("wv", [P, CT, C], f32, setup)
        centre = sb("centre", [P, P], f32, setup)
        head_vecs = sb("head_vecs", [P, 4, D], f32, setup)
        x_t = sb("x_t", [P, CT, TOK], f32, setup)
        big = [sb(f"setup_big{i}", [P, TT, C], f32, setup) for i in range(2)]
        q_parts = sb("q_parts", [P, TT, H, 4, D], f32, setup)
        setup.close()

        w_hi = [sb(f"w_hi{i}", [P, CHUNK], f32r) for i in range(WR)]
        w_lo = [sb(f"w_lo{i}", [P, CHUNK], f32r) for i in range(WR)]
        w_raw = [sb(f"w_raw{i}", [P, CHUNK]) for i in range(RAW)]
        x = sb("x_rows", [P, TT, C])
        xn = sb("x_norm", [P, TT, C])
        ident = sb("ident", [P, P])
        neg_half = sb("neg_half", [P, 1])
        stat = sb("stat", [P, 4, 32])

        attn = ExitStack()
        raw = [sb(f"ctx_raw{i}", [P, CT, P], f32, attn) for i in range(4)]
        ctx_hi = [sb(f"ctx_hi{i}", [P, CT, P], f32r, attn) for i in range(2)]
        ctx_lo = [sb(f"ctx_lo{i}", [P, CT, P], f32r, attn) for i in range(2)]
        wk_hi = sb("wk_hi", [P, CT, C], f32r, attn)
        wk_lo = sb("wk_lo", [P, CT, C], f32r, attn)
        wv_hi = sb("wv_hi", [P, CT, C], f32r, attn)
        wv_lo = sb("wv_lo", [P, CT, C], f32r, attn)
        q4 = sb("q4", [P, H, TOK], f32r, attn)
        k_c = sb("k_centred", [P, H, D], f32, attn)
        k_sq = sb("k_sq", [P, H, D], f32, attn)
        k_var = sb("k_var", [P, 3, H], f32, attn)
        k_eps = sb("k_eps", [P, 1], f32, attn)
        k_n = sb("k_n", [P, H, D - 1], f32, attn)
        k_hl = [sb(f"k_hl{i}", [P, H, 2, D], f32r, attn) for i in range(2)]
        kT = [sb(f"kT{g}", [P, HG // 2, 2, P], f32r, attn) for g in range(NG)]
        v_sb = [sb(f"v_sb{i}", [P, C], f32, attn) for i in range(2)]
        probs = [sb(f"probs{g}", [P, HG, TOK], f32, attn) for g in range(NG)]
        zeros = sb("zeros", [P, C], f32, attn)
        ident_r = sb("ident_r", [P, P], f32r, attn)
        psum_a = ExitStack()
        o_ps = ps("o_ps", [P, NG, TOK], psum_a)
        kv_ps = ps("kv_ps", [P, 2, C], psum_a)
        s_ps = ps("s_ps", [P, HG, TOK], psum_a)
        t_ps = ps("t_ps", [P, 2, C], psum_a)
        psum_a.close()
        attn.close()

        mid = ExitStack()
        o_t = sb("o_t", [P, NG, TOK], f32, mid)
        wp = sb("wp", [P, CT, C], f32, mid)
        qkv_w = sb("qkv_w", [P, CT, 3 * C], f32, mid)
        qkv = sb("qkv", [P, TT, 3 * C], f32, mid)
        rows = sb("bias_rows", [P, 5, C], f32, mid)
        out_w = sb("out_w", [P, CT, C], f32, mid)
        qk_min = sb("qk_min", [P, TT, 2 * C], f32, mid)
        qk_max = sb("qk_max", [P, TT, 2 * C], f32, mid)
        v_one = sb("v_one", [P, TT, H, D + 1], f32, mid)
        qk_t = sb("qk_t", [P, 2, NG, TOK], f32, mid)
        mid_t = sb("mid_t", [P, CT, TOK], f32, mid)
        causal = sb("causal", [P, TOK + P], f32, mid)
        masked = [sb(f"masked{i}", [P, TOK + P], f32, mid) for i in range(4)]
        mid_a = sb("mid_a", [P, TT, C], f32, mid)
        mid_b = sb("mid_b", [P, TT, C], f32, mid)
        mid.close()
        psum_m = ExitStack()
        pm = ps("pm", [P, 4, 512], psum_m)
        po = ps("po", [P, 4, 512], psum_m)
        psum_m.close()

        ffn = ExitStack()
        hid = {n: (sb(f"{n}_hi", [P, FT, TOK], f32r, ffn), sb(f"{n}_lo", [P, FT, TOK], f32r, ffn))
               for n in ("h1", "h2")}
        pre = sb("pre", [P, FT, TOK], f32, ffn)
        stage = [sb(f"stage{i}", [P, TOK], f32, ffn) for i in range(4)]
        sq = [sb(f"sq{i}", [P, 4, TOK], f32, ffn) for i in range(2)]
        hid["xn"] = (sb("xn_hi", [P, CT, TOK], f32r, ffn), sb("xn_lo", [P, CT, TOK], f32r, ffn))
        gate = sb("gate", [P, E, TOK], f32, ffn)
        gate_t = sb("gate_t", [E, TOK], f32, ffn)
        down_b = sb("down_b", [E, C], f32, ffn)
        mean_w = sb("mean_w", [P, P], f32, ffn)
        moment = sb("moment", [P, 4, TOK], f32, ffn)
        sums = sb("sums", [P, 5, TOK], f32, ffn)
        vec = sb("bias_cols", [P, BIAS_COLS], f32, ffn)
        router_w = sb("router_w", [P, CT, E], f32, ffn)
        rt = sb("router_tmp", [P, 8, TT, E], f32, ffn)
        lower = sb("lower", [P, E, E], f32, ffn)
        psum_f = ExitStack()
        y_ps = ps("y_ps", [P, TT, C], psum_f)
        f_ps = ps("f_ps", [P, 4, 512], psum_f)
        m_ps = ps("m_ps", [P, 2, 512], psum_f)
        psum_f.close()
        ffn.close()

        def as_rows(t):
            return t.rearrange("p a b -> p (a b)").rearrange("p (t c) -> p t c", t=TT)

        nx_t, nx, r_b = pre[:, 0:CT], as_rows(pre[:, 8:12]), as_rows(pre[:, 12:16])
        cmp = [pre[:, 4 + i, 0:TT * E * E].rearrange("p (t e f) -> p t e f", t=TT, e=E) for i in range(2)]
        lnv, r_a = as_rows(sq[0][:]), as_rows(sq[1][:])

        raw_in = [sem(f"raw_in{i}") for i in range(4)]
        ctx_hi_made, ctx_lo_made = sem("ctx_hi_made"), sem("ctx_lo_made")
        k_made, v_made = sem("k_made"), sem("v_made")
        k_sq_made, k_sum_made = sem("k_sq_made"), sem("k_sum_made")
        k_kept = sem("k_kept")
        k_var_made, k_dev_made = sem("k_var_made"), sem("k_dev_made")
        k_normed, k_hi_made, k_split = sem("k_normed"), sem("k_hi_made"), sem("k_split")
        t_made = sem("t_made")
        kt_even_made, kt_odd_made = sem("kt_even_made"), sem("kt_odd_made")
        s_made, probs_made, av_made = sem("s_made"), sem("probs_made"), sem("av_made")
        v_copied = sem("v_copied")
        w_in = [sem(f"w_in{i}") for i in range(RAW)]
        w_hi_made, w_lo_made, w_used = sem("w_hi_made"), sem("w_lo_made"), sem("w_used")
        f_made = sem("f_made")
        f_read = sem("f_read")
        gated = sem("gated")
        h_hi_made, h_made = sem("h_hi_made"), sem("h_made")
        pre_summed, mean_made = sem("pre_summed"), sem("mean_made")
        mean_copied, centred = sem("mean_copied"), sem("centred")
        sq_made, sq_summed, var_made = sem("sq_made"), sem("sq_summed"), sem("var_made")
        root_step, scaled = sem("root_step"), sem("scaled")
        applied = sem("applied")
        done = sem("done")

        def wait(eng, s, v):
            if not isinstance(v, int) or v > 0:
                eng.wait_ge(s, v)

        def n_of(it, r, per=1, more=0):
            if isinstance(it, int):
                return per * (4 * it + r) + more
            return it * (4 * per) + (per * r + more)

        def is_first(it, r, t):
            return isinstance(it, int) and 4 * it + r == t

        def at(half, per_half, q, per_q, more):
            v = half * per_half + more
            return v if isinstance(q, int) and q == 0 else v + q * per_q

        def one(t, i):
            return t[:, i] if isinstance(i, int) else t[:, bass.ds(i, 1)].rearrange("p o t -> p (o t)")

        def per_row(ap2, n):
            return ap2.unsqueeze(2).to_broadcast([ap2.shape[0], ap2.shape[1], n])

        def repeat(ap2, n):
            return ap2.unsqueeze(1).to_broadcast([ap2.shape[0], n, ap2.shape[1]])

        def quads(eng, name, kt):
            n = layer_chunks(name, kt) // 4
            if n <= 2:
                yield from range(n)
            else:
                with eng.Fori(0, n) as q:
                    yield q

        block = life.enter_context(nc.Block())

        @block.sync
        def _(sp):
            for name, dst in (("x", x), ("wq", wq), ("wk", wk), ("wv", wv), ("head_vecs", head_vecs)):
                sp.dma_start(dst[:], a[name]).then_inc(once(name + "_in"), 16)

            def load_ctx(it, r):
                wait(sp, ctx_lo_made, n_of(it, r, 1, -3))
                t = n_of(it, r)
                tile = a["ctx"][t] if isinstance(t, int) else \
                    a["ctx"][bass.ds(t, 1)].rearrange("o p n -> (o p) n")
                sp.dma_start(raw[r][:].rearrange("p a b -> p (a b)"), tile).then_inc(raw_in[r], 16)

            for r in range(4):
                load_ctx(0, r)
            for i in range(RAW):
                sp.dma_start(w_raw[i][:], a["w"][i]).then_inc(w_in[i], 16)
            with sp.Fori(1, NKT // 4) as it:
                for r in range(4):
                    load_ctx(it, r)
            sp.wait_ge(av_made, NG * (NKT + 1))
            for name, dst in (("wp", wp), ("bias_rows", rows), ("qkv_w", qkv_w), ("out_w", out_w)):
                sp.dma_start(dst[:], a[name]).then_inc(once(name + "_in"), 16)
            sp.wait_ge(once("x2_made"), 1)
            for name, dst in (("ln_rows", lnv), ("router_w", router_w), ("down_b", down_b),
                              ("bias_cols", vec)):
                sp.dma_start(dst[:], a[name]).then_inc(once(name + "_in"), 16)
            with sp.Fori(1, HALVES * CHUNKS_HALF // RAW) as it:
                for i in range(RAW):
                    sp.wait_ge(w_lo_made, it * RAW + (i - RAW + 1))
                    sp.dma_start(w_raw[i][:], a["w"][bass.ds(it * RAW + i, 1)]
                                 .rearrange("o p n -> (o p) n")).then_inc(w_in[i], 16)
            sp.wait_ge(once("result"), 1)
            sp.dma_start(out, x[:]).then_inc(done, 16)
            sp.wait_ge(done, 16)

        @block.gpsimd
        def _(pool):
            g = nc.gpsimd
            own, count = sem("pool_own"), [0]

            def link(ins):
                count[0] += 1
                ins.then_inc(own, 1)
                pool.wait_ge(own, count[0])

            def deviations(n, tag):
                pool.wait_ge(once(tag + "_var"), 1)
                g.tensor_tensor(stat[:, 2, 0:n], stat[:, 3, 0:n], neg_half[:].to_broadcast([P, n]),
                                ALU.pow).then_inc(once(tag + "_dev"), 1)

            link(g.memset(neg_half[:], -0.5))
            link(g.memset(k_eps[:], 1e-5))
            link(g.memset(ident[:], 0.0))
            link(g.affine_select(out=ident[:], in_=ident[:], compare_op=ALU.not_equal, fill=1.0,
                                 base=0, pattern=[[-1, P]], channel_multiplier=1))
            c3 = centre[:].rearrange("p (b d) -> p b d", b=HG)
            link(g.memset(centre[:], -1.0 / D))
            link(g.affine_select(out=c3, in_=c3, compare_op=ALU.is_ge, fill=0.0, base=0,
                                 pattern=[[-D, HG], [0, D]], channel_multiplier=1))
            link(g.affine_select(out=c3, in_=c3, compare_op=ALU.is_ge, fill=0.0, base=D - 1,
                                 pattern=[[D, HG], [0, D]], channel_multiplier=-1))
            g.tensor_tensor(centre[:], centre[:], ident[:], ALU.add).then_inc(once("consts"), 1)
            for i in range(2):
                link(g.memset(k_hl[i][:].bitcast(f32), 0.0))
                link(g.memset(k_hl[i][:, :, 0, D - 1:D].bitcast(f32), 1.0))
            g.memset(zeros[:], 0.0).then_inc(once("zeros_made"), 1)
            deviations(TT, "x")
            deviations(TT * H, "q")

            def low_part(it, r):
                pool.wait_ge(ctx_hi_made, n_of(it, r, 1, 1))
                wait(pool, v_made, n_of(it, r, 1, -1))
                g.tensor_tensor(ctx_lo[r % 2][:], raw[r % 4][:], ctx_hi[r % 2][:].bitcast(f32),
                                ALU.subtract).then_inc(ctx_lo_made, 1)

            def deviation(it, r):
                pool.wait_ge(k_sum_made, n_of(it, r, 1, 1))
                g.tensor_tensor(k_var[:, 1], k_var[:, 0], k_eps[:].to_broadcast([P, H]), ALU.add)\
                    .then_inc(k_var_made, 1)
                pool.wait_ge(k_var_made, n_of(it, r, 1, 1))
                wait(pool, k_normed, n_of(it, r))
                g.tensor_tensor(k_var[:, 2], k_var[:, 1], neg_half[:].to_broadcast([P, H]), ALU.pow)\
                    .then_inc(k_dev_made, 1)

            def step(it, r, last=False):
                if not last:
                    low_part(it, r + 1)
                deviation(it, r)

            low_part(0, 0)
            step(0, 0)
            step(0, 1)
            with pool.Fori(0, nq) as it:
                for r in range(2, 6):
                    step(it, r)
            step(nq, 2)
            step(nq, 3, last=True)

            pool.wait_ge(once("attention_done"), 1)
            link(g.memset(causal[:], 1.0))
            for first, n in ((0, TOK), (TOK, P)):
                link(g.affine_select(out=causal[:, first:first + n], in_=causal[:, first:first + n],
                                     compare_op=ALU.is_ge, fill=0.0, base=0, pattern=[[1, n]],
                                     channel_multiplier=-1))
            g.memset(v_one[:, :, :, D:D + 1], 1.0).then_inc(once("mid_consts"), 1)
            deviations(TT, "x1")
            pool.wait_ge(once("x2_made"), 1)
            link(g.memset(mean_w[:], 1.0 / F))
            link(g.memset(lower[:], 1.0))
            g.affine_select(out=lower[:], in_=lower[:], compare_op=ALU.is_ge, fill=0.0, base=-1,
                            pattern=[[1, E], [-1, E]], channel_multiplier=0)\
                .then_inc(once("router_consts"), 1)
            deviations(TT, "x2")
            deviations(TT, "nx")
            pool.sem_inc(h_made, 4)

            def low_tiles(half, dst, base):
                def make(q):
                    for i in range(4):
                        pool.wait_ge(h_hi_made, at(half, TILES_HALF, q, 4, base + i + 1))
                        hi, lo = (one(t, q * 4 + i) for t in hid[dst])
                        g.tensor_tensor(lo, stage[i][:], hi.bitcast(f32), ALU.subtract)\
                            .then_inc(h_made, 1)
                return make

            with pool.Fori(0, HALVES) as half:
                for name, kind, kt, src, dst, e, last in LAYERS:
                    if kind == "gelu":
                        make = low_tiles(half, dst, STAGE_BASE[name])
                        with pool.Fori(0, OUT_TILES[name] // 4) as q:
                            make(q)
                    if name in NORM_AFTER:
                        norm = NORM_AFTER[name]
                        make = low_tiles(half, NORM_OUT[norm], STAGE_BASE[norm])
                        with pool.Fori(0, FT // 4) as q:
                            make(q)

        @block.scalar
        def _(act):
            s = nc.scalar

            def sigmoid(it, r, grp):
                act.wait_ge(s_made, n_of(it, r, NG, grp + 1))
                act.wait_ge(av_made, n_of(it, r, NG, grp + 1))
                s.activation(probs[grp][:], s_ps[:], ACT.Sigmoid).then_inc(probs_made, 1)

            def copy_turned(it, r, grp):
                act.wait_ge(t_made, n_of(it, r, NG, grp + 1))
                wait(act, s_made, n_of(it, r, NG, grp - 3))
                pairs = t_ps[:, grp % 2, 0:HG // 2 * P].rearrange("p (n k) -> p n k", n=HG // 2)
                s.activation(kT[grp][0:P // 2, :, 1], pairs[P // 2:P], ACT.Copy).then_inc(kt_odd_made, 1)
                s.activation(kT[grp][P // 2:P, :, 1], pairs[P // 2:P], ACT.Copy).then_inc(kt_odd_made, 1)

            def square(it, r):
                act.wait_ge(k_made, n_of(it, r, 1, 1))
                wait(act, k_sum_made, n_of(it, r))
                s.activation(k_sq[:].rearrange("p h d -> p (h d)"), kv_ps[:, 0], ACT.Square,
                             scale=float(D) ** -0.5).then_inc(k_sq_made, 1)
                wait(act, k_normed, n_of(it, r))
                s.activation(k_c[:].rearrange("p h d -> p (h d)"), kv_ps[:, 0], ACT.Copy)\
                    .then_inc(k_kept, 1)

            def step(it, r, keys=True):
                if not (is_first(it, r, 0) or is_first(it, r, 1)):
                    sigmoid(it, r - 2, 2)
                    copy_turned(it, r - 2, 3)
                    sigmoid(it, r - 2, 3)
                if not is_first(it, r, 0):
                    copy_turned(it, r - 1, 0)
                if keys:
                    square(it, r)
                if not is_first(it, r, 0):
                    sigmoid(it, r - 1, 0)
                    copy_turned(it, r - 1, 1)
                    sigmoid(it, r - 1, 1)
                    copy_turned(it, r - 1, 2)

            step(0, 0)
            step(0, 1)
            with act.Fori(0, nq) as it:
                for r in range(2, 6):
                    step(it, r)
            step(nq, 2)
            step(nq, 3)
            step(nq, 4, keys=False)
            sigmoid(nq, 3, 2)
            copy_turned(nq, 3, 3)
            sigmoid(nq, 3, 3)

            act.wait_ge(once("qk_min_made"), 1)
            s.activation(qk_min[:], qk_min[:], ACT.Exp).then_inc(once("qk_exp"), 1)
            act.wait_ge(once("logits_less_max"), 1)
            s.activation(rt[:, 1], rt[:, 0], ACT.Exp).then_inc(once("router_exp"), 1)
            act.sem_inc(f_read, 4)
            act.wait_ge(once("bias_cols_in"), 16)

            def high(half, q, base, i):
                act.wait_ge(w_in[i % RAW], at(half, 8 * CHUNKS_HALF, q, 32, 8 * base + 16 * (i // 2 + 1)))
                act.wait_ge(w_used, at(half, CHUNKS_HALF, q, 4, base + i + 1))
                s.activation(w_hi[i][:], w_raw[i % RAW][:], ACT.Copy).then_inc(w_hi_made, 1)

            def column(key, half, q, per_q, more):
                first, per = COLS[key]
                i = at(half, per, q, per_q, first + more)
                return vec[:, i:i + 1] if isinstance(i, int) else vec[:, bass.ds(i, 1)]

            with act.Fori(0, HALVES) as half:
                for i in range(4):
                    high(half, 0, 0, i)
                for name, kind, kt, src, dst, e, last in LAYERS:
                    if kind == "down" and name == LAYERS[-1][0]:
                        continue
                    per = OUT_TILES[name] // layer_chunks(name, kt)
                    for q in quads(act, name, kt):
                        for i in range(4):
                            for j in range(per):
                                n = i * per + j
                                slot = n % 4
                                if j < per - 1:
                                    act.wait_ge(f_made, at(half, EARLY_HALF, q, 4 * (per - 1),
                                                           EARLY_BASE[name] + i * (per - 1) + j + 1))
                                else:
                                    act.wait_ge(w_used, at(half, CHUNKS_HALF, q, 4,
                                                           CHUNK_BASE[name] + i + 1 + 4))
                                bias = column(BIAS[name][0], half, q, 4 * per, BIAS[name][1] * FT + n)
                                if kind == "gelu":
                                    act.wait_ge(h_made, at(half, TILES_HALF, q, 4 * per,
                                                           STAGE_BASE[name] + n + 1))
                                    s.activation(stage[slot][:], f_ps[:, slot, 0:TOK], ACT.Gelu,
                                                 bias=bias).then_inc(f_read, 1)
                                else:
                                    s.activation(one(pre, q * (4 * per) + n), f_ps[:, slot, 0:TOK],
                                                 ACT.Identity, bias=bias).then_inc(f_read, 1)
                            high(half, q, CHUNK_BASE[name] + 4, i)
                    step, norm = STEPS.get((name, "end"), (None, None))
                    if step == "squares":
                        k0 = NORMS.index(norm)
                        for k in range(4):
                            act.wait_ge(centred, half * 8 + (4 * k0 + k + 1))
                            if k >= 2:
                                act.wait_ge(sq_summed, half * 8 + (4 * k0 + k - 1))
                            s.activation(sq[k % 2][:], pre[:, 4 * k:4 * k + 4], ACT.Square)\
                                .then_inc(sq_made, 1)
                    if step == "apply":
                        k0 = NORMS.index(norm)
                        with act.Fori(0, 4) as q:
                            act.wait_ge(scaled, at(half, 8, q, 1, 4 * k0 + 1))
                            for i in range(4):
                                act.wait_ge(h_made, at(half, TILES_HALF, q, 4, STAGE_BASE[norm] + i + 1))
                                s.activation(stage[i][:], one(pre, q * 4 + i),
                                             ACT.Gelu if k0 == 0 else ACT.Identity,
                                             bias=column(f"ln{k0}_b", half, q, 4, i),
                                             scale=column(f"ln{k0}_g", half, q, 4, i))\
                                    .then_inc(applied, 1)

        @block.vector
        def _(dve):
            v = nc.vector
            own, count = sem("dve_own"), [0]

            def link(ins):
                count[0] += 1
                ins.then_inc(own, 1)
                dve.wait_ge(own, count[0])
                return ins

            def layernorm(dst, src, cen, sqr, eps, tag):
                n, w = dst.shape[1], dst.shape[2]
                link(v.tensor_reduce(stat[:, 1, 0:n], src, AX, ALU.add))
                link(v.tensor_scalar(stat[:, 0, 0:n], stat[:, 1, 0:n], 1.0 / w, None, ALU.mult))
                link(v.tensor_tensor(cen, src, per_row(stat[:, 0, 0:n], w), ALU.subtract))
                link(v.tensor_tensor(sqr, cen, cen, ALU.mult))
                link(v.tensor_reduce(stat[:, 1, 0:n], sqr, AX, ALU.add))
                v.tensor_scalar(stat[:, 3, 0:n], stat[:, 1, 0:n], 1.0 / w, eps, ALU.mult, ALU.add)\
                    .then_inc(once(tag + "_var"), 1)
                dve.wait_ge(once(tag + "_dev"), 1)
                link(v.tensor_tensor(dst, cen, per_row(stat[:, 2, 0:n], w), ALU.mult))

            dve.wait_ge(once("consts"), 1)
            link(v.tensor_copy(ident_r[:], ident[:]))
            dve.wait_ge(once("x_in"), 16)
            layernorm(xn[:], x[:], big[0][:], big[1][:], 1e-5, "x")
            dve.sem_inc(once("xn_made"), 1)
            dve.wait_ge(once("wv_in"), 16)
            link(v.tensor_copy(wv_hi[:], wv[:]))
            v.tensor_tensor(wv_lo[:], wv[:], wv_hi[:].bitcast(f32), ALU.subtract)\
                .then_inc(once("wv_split"), 1)
            dve.wait_ge(once("xn_turned"), 1)
            v.tensor_copy(x_t[:], s_ps[:]).then_inc(once("x_t_made"), 1)
            dve.wait_ge(once("wk_centred"), 1)
            for c in range(CT):
                wk_ps = (t_ps[:, c % 2] if c < 2 else
                         o_ps[:, 2 * (c % 2):2 * (c % 2) + 2].rearrange("p g t -> p (g t)"))
                link(v.tensor_copy(wk_hi[:, c], wk_ps))
                link(v.tensor_tensor(wk_lo[:, c], wk_ps, wk_hi[:, c].bitcast(f32), ALU.subtract))
            dve.sem_inc(once("wk_split"), 1)
            dve.wait_ge(once("q_made"), 1)
            heads = [b[:].rearrange("p t (h d) -> p (t h) d", h=H) for b in big]
            qn, tmp = heads
            layernorm(qn, kv_ps[:].rearrange("p t (h d) -> p (t h) d", h=H), qn, tmp, 1e-5, "q")
            dve.wait_ge(once("head_vecs_in"), 16)
            gq, bq, gk, bk = (repeat(head_vecs[:, i], TT * H) for i in range(4))
            link(v.tensor_tensor(qn, qn, gq, ALU.mult))
            link(v.tensor_tensor(qn, qn, bq, ALU.add))
            link(v.tensor_scalar(big[0][:], big[0][:], float(D) ** -0.5, None, ALU.mult))
            link(v.tensor_tensor(tmp, qn, bk, ALU.mult))
            link(v.tensor_reduce(stat[:, 0, 0:TT * H], tmp, AX, ALU.add))
            link(v.tensor_tensor(qn, qn, gk, ALU.mult))
            link(v.tensor_tensor(tmp[:, :, 0:D - 1], qn[:, :, 0:D - 1],
                                 qn[:, :, D - 1:D].to_broadcast([P, TT * H, D - 1]), ALU.subtract))
            link(v.tensor_copy(tmp[:, :, D - 1], stat[:, 0, 0:TT * H]))
            parts = q_parts[:].rearrange("p t h a d -> p (t h) a d")
            link(v.tensor_copy(parts[:, :, 0].bitcast(f32r), tmp))
            link(v.tensor_tensor(parts[:, :, 2], tmp, parts[:, :, 0], ALU.subtract))
            link(v.tensor_copy(parts[:, :, 1], parts[:, :, 0]))
            v.tensor_copy(parts[:, :, 3], parts[:, :, 2]).then_inc(once("q_split"), 1)
            for grp in range(NG):
                dve.wait_ge(once("q_turned"), grp + 1)
                v.tensor_copy(q4[:, HG * grp:HG * grp + HG], s_ps[:]).then_inc(once("q4_made"), 1)

            def high_part(it, r):
                if isinstance(it, int):
                    dve.wait_ge(raw_in[r % 4], 16 * (it + r // 4 + 1))
                else:
                    dve.wait_ge(raw_in[r % 4], it * 16 + 16 * (r // 4 + 1))
                wait(dve, v_made, n_of(it, r, 1, -1))
                v.tensor_copy(ctx_hi[r % 2][:], raw[r % 4][:]).then_inc(ctx_hi_made, 1)

            def copy_turned(it, r, grp):
                dve.wait_ge(t_made, n_of(it, r, NG, grp + 1))
                wait(dve, s_made, n_of(it, r, NG, grp - 3))
                pairs = t_ps[:, grp % 2, 0:HG // 2 * P].rearrange("p (n k) -> p n k", n=HG // 2)
                v.tensor_copy(kT[grp][0:P // 2, :, 0], pairs[0:P // 2]).then_inc(kt_even_made, 1)
                v.tensor_copy(kT[grp][P // 2:P, :, 0], pairs[0:P // 2]).then_inc(kt_even_made, 1)

            def copy_values(it, r):
                dve.wait_ge(v_made, n_of(it, r, 1, 1))
                wait(dve, av_made, n_of(it, r, NG))
                v.tensor_copy(v_sb[r % 2][:], kv_ps[:, 1]).then_inc(v_copied, 1)

            def sum_squares(it, r):
                dve.wait_ge(k_sq_made, n_of(it, r, 1, 1))
                v.tensor_reduce(k_var[:, 0], k_sq[:], AX, ALU.add).then_inc(k_sum_made, 1)

            def normalise(it, r):
                dve.wait_ge(k_kept, n_of(it, r, 1, 1))
                dve.wait_ge(k_dev_made, n_of(it, r, 1, 1))
                v.tensor_tensor(k_n[:], k_c[:, :, 0:D - 1], per_row(k_var[:, 2], D - 1), ALU.mult)\
                    .then_inc(k_normed, 1)

            def split_keys(it, r):
                dve.wait_ge(k_normed, n_of(it, r, 1, 1))
                hi, lo = (k_hl[r % 2][:, :, i, 0:D - 1] for i in range(2))
                wait(dve, t_made, n_of(it, r, NG, -NG))
                v.tensor_copy(hi, k_n[:]).then_inc(k_hi_made, 1)
                dve.wait_ge(k_hi_made, n_of(it, r, 1, 1))
                v.tensor_tensor(lo, k_n[:], hi.bitcast(f32), ALU.subtract).then_inc(k_split, 1)

            def step(it, r, keys=True, more=True):
                if not is_first(it, r, 0):
                    normalise(it, r - 1)
                    split_keys(it, r - 1)
                if not (is_first(it, r, 0) or is_first(it, r, 1)):
                    copy_turned(it, r - 2, 3)
                if not is_first(it, r, 0):
                    copy_values(it, r - 1)
                if more:
                    high_part(it, r + 1)
                if not is_first(it, r, 0):
                    copy_turned(it, r - 1, 0)
                if keys:
                    sum_squares(it, r)
                if not is_first(it, r, 0):
                    copy_turned(it, r - 1, 1)
                    copy_turned(it, r - 1, 2)

            high_part(0, 0)
            step(0, 0)
            step(0, 1)
            with dve.Fori(0, nq) as it:
                for r in range(2, 6):
                    step(it, r)
            step(nq, 2)
            step(nq, 3, more=False)
            step(nq, 4, keys=False, more=False)
            copy_turned(nq, 3, 3)

            dve.wait_ge(av_made, NG * (NKT + 1))
            v.tensor_copy(o_t[:], o_ps[:]).then_inc(once("attention_done"), 1)
            dve.wait_ge(once("cross_made"), 1)
            dve.wait_ge(once("bias_rows_in"), 16)
            link(v.tensor_tensor(x[:], x[:], pm[:, 0:TT], ALU.add))
            link(v.tensor_tensor(x[:], x[:], repeat(rows[:, 0], TT), ALU.add))
            layernorm(xn[:], x[:], mid_a[:], mid_b[:], 1e-5, "x1")
            dve.sem_inc(once("x1n_made"), 1)
            dve.wait_ge(once("x1n_turned"), 1)
            v.tensor_copy(mid_t[:], po[:, 0:2].rearrange("p a (b c) -> p (a b) c", b=2))\
                .then_inc(once("x1_t_made"), 1)
            for i in range(TT):
                dve.wait_ge(once("qkv_made"), i + 1)
                last = link(v.tensor_tensor(qkv[:, i], pm[:, 0:3].rearrange("p a b -> p (a b)"),
                                            rows[:, 2:5].rearrange("p a b -> p (a b)"), ALU.add))
                dve.sem_inc(once("qkv_copied"), 1)
            v.tensor_scalar(qk_min[:], qkv[:, :, 0:2 * C], 0.0, None, ALU.min)\
                .then_inc(once("qk_min_made"), 1)
            link(v.tensor_scalar(qk_max[:], qkv[:, :, 0:2 * C], 0.0, None, ALU.max))
            dve.wait_ge(once("mid_consts"), 1)
            for i in range(TT):
                link(v.tensor_copy(v_one[:, i, :, 0:D],
                                   qkv[:, i, 2 * C:3 * C].rearrange("p (h d) -> p h d", h=H)))
            dve.wait_ge(once("qk_exp"), 1)
            v.tensor_tensor(qk_max[:], qk_max[:], qk_min[:], ALU.add).then_inc(once("qk_made"), 1)
            for i in range(2):
                dve.wait_ge(once("qk_turned"), i + 1)
                v.tensor_copy(qk_t[:, i], pm[:, 2 * i:2 * i + 2].rearrange("p a (b c) -> p (a b) c", b=2))\
                    .then_inc(once("qk_t_made"), 1)
            for h in range(H):
                dve.wait_ge(once("lin_scores"), h + 1)
                wait(dve, once("lin_used"), h - 3)
                v.tensor_tensor(masked[h % 4][:], pm[:, h % 4, 0:TOK + P], causal[:], ALU.mult)\
                    .then_inc(once("lin_masked"), 1)
            dve.wait_ge(once("lin_used"), H)
            for i in range(TT):
                for k in range(2):
                    o = po[:, 2 * i + k, 0:8 * (D + 1)].rearrange("p (h d) -> p h d", h=8)
                    link(v.tensor_scalar(stat[:, 0, 0:8], o[:, :, D], 1e-6, None, ALU.add))
                    link(v.reciprocal(stat[:, 1, 0:8], stat[:, 0, 0:8]))
                    link(v.tensor_tensor(mid_a[:, i, k * 256:k * 256 + 256]
                                         .rearrange("p (h d) -> p h d", h=8),
                                         o[:, :, 0:D], per_row(stat[:, 1, 0:8], D), ALU.mult))
            dve.sem_inc(once("lin_made"), 1)
            dve.wait_ge(once("lin_turned"), 1)
            v.tensor_copy(mid_t[:], pm[:, 0:2].rearrange("p a (b c) -> p (a b) c", b=2))\
                .then_inc(once("lin_t_made"), 1)
            dve.wait_ge(once("self_made"), 1)
            link(v.tensor_tensor(x[:], x[:], pm[:, 2:4], ALU.add))
            v.tensor_tensor(x[:], x[:], repeat(rows[:, 1], TT), ALU.add).then_inc(once("x2_made"), 1)
            dve.wait_ge(once("x2_made"), 1)
            layernorm(xn[:], x[:], r_a, r_b, 1e-5, "x2")
            layernorm(nx, xn[:], r_a, r_b, 1e-5, "nx")
            dve.wait_ge(once("ln_rows_in"), 16)
            link(v.tensor_tensor(nx, nx, repeat(lnv[:, 0], TT), ALU.mult))
            v.tensor_tensor(nx, nx, repeat(lnv[:, 1], TT), ALU.add).then_inc(once("nx_made"), 1)
            dve.wait_ge(once("nx_turned"), 1)
            v.tensor_copy(nx_t, f_ps[:, 0:2].rearrange("p a (b c) -> p (a b) c", b=2))\
                .then_inc(once("nx_t_made"), 1)
            dve.wait_ge(once("nx_t_made"), 1)
            link(v.tensor_copy(hid["xn"][0][:], nx_t))
            v.tensor_tensor(hid["xn"][1][:], nx_t, hid["xn"][0][:].bitcast(f32), ALU.subtract)\
                .then_inc(once("xn_split"), 1)
            dve.wait_ge(once("logits"), 1)
            lg = m_ps[:, 0, 0:TT * E].rearrange("p (t e) -> p t e", t=TT)
            link(v.tensor_reduce(rt[:, 2, :, 0], lg, AX, ALU.max))
            v.tensor_tensor(rt[:, 0], lg, per_row(rt[:, 2, :, 0], E), ALU.subtract)\
                .then_inc(once("logits_less_max"), 1)
            dve.wait_ge(once("router_exp"), 1)
            link(v.tensor_reduce(rt[:, 2, :, 0], rt[:, 1], AX, ALU.add))
            link(v.reciprocal(rt[:, 2, :, 1], rt[:, 2, :, 0]))
            link(v.tensor_tensor(rt[:, 3], rt[:, 1], per_row(rt[:, 2, :, 1], E), ALU.mult))
            dve.wait_ge(once("router_consts"), 1)
            for i in range(TT):
                mine = per_row(rt[:, 3, i], E)
                others = repeat(rt[:, 3, i], E)
                link(v.tensor_tensor(cmp[0][:, i], others, mine, ALU.is_gt))
                link(v.tensor_tensor(cmp[1][:, i], others, mine, ALU.is_equal))
                link(v.tensor_tensor(cmp[1][:, i], cmp[1][:, i], lower[:], ALU.mult))
                link(v.tensor_tensor(cmp[0][:, i], cmp[0][:, i], cmp[1][:, i], ALU.add))
                link(v.tensor_reduce(rt[:, 4, i], cmp[0][:, i], AX, ALU.add))
            link(v.tensor_scalar(rt[:, 4], rt[:, 4], 2.0, None, ALU.is_lt))
            link(v.tensor_tensor(rt[:, 5], rt[:, 4], rt[:, 3], ALU.mult))
            link(v.tensor_reduce(rt[:, 2, :, 0], rt[:, 5], AX, ALU.add))
            link(v.reciprocal(rt[:, 2, :, 1], rt[:, 2, :, 0]))
            v.tensor_tensor(rt[:, 5], rt[:, 5], per_row(rt[:, 2, :, 1], E), ALU.mult)\
                .then_inc(once("gates"), 1)
            dve.wait_ge(once("gates_turned"), 1)
            v.tensor_copy(gate_t[:], m_ps[0:E, 1, 0:TOK]).then_inc(once("gate_t_made"), 1)
            for k in range(2):
                dve.wait_ge(once("gates_spread"), k + 1)
                v.tensor_copy(gate[:, 4 * k:4 * k + 4],
                              f_ps[:, 2 * k:2 * k + 2].rearrange("p a (b c) -> p (a b) c", b=2))\
                    .then_inc(once("gates_copied"), 1)
            dve.wait_ge(once("gates_copied"), 2)

            def low(half, q, base, i):
                dve.wait_ge(w_hi_made, at(half, CHUNKS_HALF, q, 4, base + i + 1))
                v.tensor_tensor(w_lo[i][:], w_raw[i % RAW][:], w_hi[i][:].bitcast(f32), ALU.subtract)\
                    .then_inc(w_lo_made, 1)

            def high_tile(half, q, per_q, name, dst, e, last, n, gates_before):
                if name in NORMS:
                    dve.wait_ge(applied, at(half, 2 * FT, q, per_q, FT * e + n + 1))
                else:
                    dve.wait_ge(f_read, at(half, TILES_HALF, q, per_q, FILL_BASE[name] + n + 1 + 4))
                tile = stage[n % 4][:]
                if last:
                    v.tensor_tensor(tile, tile, one(gate, half * (E // 2) + e), ALU.mult)\
                        .then_inc(gated, 1)
                    dve.wait_ge(gated, at(half, GATED_HALF, q, per_q, gates_before + n + 1))
                v.tensor_copy(one(hid[dst][0], q * per_q + n), tile).then_inc(h_hi_made, 1)

            def free(half, dst, name):
                order = [l[0] for l in LAYERS]
                k = order.index(name)
                readers = [l[0] for l in LAYERS if l[3] == dst]
                before = [n for n in readers if order.index(n) <= k]
                if before:
                    end = CHUNK_BASE[before[-1]] + CHUNKS[before[-1]]
                else:
                    end = CHUNK_BASE[readers[-1]] + CHUNKS[readers[-1]]
                    dve.wait_ge(w_used, half * end + 4)
                    return
                dve.wait_ge(w_used, half * CHUNKS_HALF + (4 + end))

            def normalisation(half, what):
                if what is None:
                    return
                step, norm = what
                k0 = NORMS.index(norm)
                var, root, scratch = moment[:, 1], moment[:, 2], moment[:, 3]
                if step == "mean":
                    dve.wait_ge(mean_made, half * 2 + (k0 + 1))
                    v.tensor_copy(moment[:, 0], m_ps[:, 0, 0:TOK]).then_inc(mean_copied, 1)
                    dve.wait_ge(mean_copied, half * 2 + (k0 + 1))
                    for k in range(4):
                        part = pre[:, 4 * k:4 * k + 4]
                        v.tensor_tensor(part, part, repeat(moment[:, 0], 4), ALU.subtract)\
                            .then_inc(centred, 1)
                if step == "squares":
                    for k in range(4):
                        dve.wait_ge(sq_made, half * 8 + (4 * k0 + k + 1))
                        v.tensor_reduce(sums[:, 1 + k], sq[k % 2][:].rearrange("p f t -> p t f"), AX,
                                        ALU.add).then_inc(sq_summed, 1)
                if step == "variance":
                    done_before = [ROOT_OPS * k0]

                    def follow(ins):
                        done_before[0] += 1
                        ins.then_inc(root_step, 1)
                        dve.wait_ge(root_step, half * (2 * ROOT_OPS) + done_before[0])

                    i32 = mybir.dt.int32
                    dve.wait_ge(var_made, half * 2 + (k0 + 1))
                    follow(v.tensor_scalar(var, m_ps[:, 1, 0:TOK], 1e-5, None, ALU.add))
                    follow(v.tensor_scalar(root.bitcast(i32), var.bitcast(i32), 1, None,
                                           ALU.logical_shift_right))
                    follow(v.tensor_scalar(root.bitcast(i32), root.bitcast(i32), -1.0,
                                           float(0x5F3759DF), ALU.mult, ALU.add))
                    for _ in range(ROOT_STEPS):
                        follow(v.scalar_tensor_tensor(scratch, root, -0.5, root, ALU.mult, ALU.mult))
                        follow(v.tensor_tensor(scratch, scratch, var, ALU.mult))
                        follow(v.scalar_tensor_tensor(root, scratch, 1.5, root, ALU.add, ALU.mult))
                    for k in range(4):
                        part = pre[:, 4 * k:4 * k + 4]
                        v.tensor_tensor(part, part, repeat(root, 4), ALU.mult).then_inc(scaled, 1)
                if step == "apply":
                    after = next(layer for layer, n in NORM_AFTER.items() if n == norm)
                    with dve.Fori(0, 4) as q:
                        free(half, NORM_OUT[norm], after)
                        for i in range(4):
                            high_tile(half, q, 4, norm, NORM_OUT[norm], k0, True, i, GATED_BASE[norm])

            with dve.Fori(0, HALVES) as half:
                for i in range(4):
                    low(half, 0, 0, i)
                for name, kind, kt, src, dst, e, last in LAYERS:
                    if kind == "down" and name == LAYERS[-1][0]:
                        continue
                    per = OUT_TILES[name] // layer_chunks(name, kt)
                    for q in quads(dve, name, kt):
                        if kind == "gelu":
                            free(half, dst, name)
                        for i in range(4):
                            if kind == "gelu":
                                for j in range(per):
                                    high_tile(half, q, 4 * per, name, dst, e, last, i * per + j,
                                              GATED_BASE.get(name))
                            low(half, q, CHUNK_BASE[name] + 4, i)
                            if i == 1:
                                normalisation(half, STEPS.get((name, "second")))
                        if isinstance(q, int) and q == 0:
                            normalisation(half, STEPS.get((name, "four")))
                    if kind == "norm":
                        dve.wait_ge(f_read, half * TILES_HALF + (FILL_BASE[name] + FT + 4))
                        v.tensor_reduce(sums[:, 0], pre[:].rearrange("p f t -> p t f"), AX, ALU.add)\
                            .then_inc(pre_summed, 1)
                    normalisation(half, STEPS.get((name, "end")))
            link(v.tensor_tensor(x[:], x[:], xn[:], ALU.add))
            dve.wait_ge(w_used, 4 + HALVES * CHUNKS_HALF)
            v.tensor_tensor(x[:], x[:], y_ps[:], ALU.add).then_inc(once("result"), 1)

        @block.tensor
        def _(pe):
            t = nc.tensor

            def turn_rows(dst, src_rows):
                for i in range(TT):
                    for c in range(CT):
                        ins = t.transpose(dst(c, i), src_rows[:, i, c * P:(c + 1) * P], ident[:])
                return ins

            pe.wait_ge(once("consts"), 1)
            pe.wait_ge(once("wk_in"), 16)
            for c in range(CT):
                for b in range(CT):
                    dst = (t_ps[:, c % 2, b * P:(b + 1) * P] if c < 2 else
                           o_ps[:, 2 * (c % 2) + b // 2, (b % 2) * P:(b % 2 + 1) * P])
                    ins = t.matmul(dst, wk[:, b, c * P:(c + 1) * P], centre[:], start=True, stop=True)
            ins.then_inc(once("wk_centred"), 1)
            pe.wait_ge(once("xn_made"), 1)
            turn_rows(lambda c, i: s_ps[:, c, i * P:(i + 1) * P], xn).then_inc(once("xn_turned"), 1)
            pe.wait_ge(once("x_t_made"), 1)
            pe.wait_ge(once("wq_in"), 16)
            for i in range(TT):
                for c in range(CT):
                    ins = t.matmul(kv_ps[:, i], x_t[:, c, i * P:(i + 1) * P], wq[:, c],
                                   start=(c == 0), stop=(c == CT - 1))
            ins.then_inc(once("q_made"), 1)
            pe.wait_ge(once("q_split"), 1)
            for grp in range(NG):
                wait(pe, once("q4_made"), grp)
                for h in range(HG):
                    for i in range(TT):
                        ins = t.transpose(s_ps[:, h, i * P:(i + 1) * P],
                                          q_parts[:, i, HG * grp + h].rearrange("p a d -> p (a d)"),
                                          ident[:])
                ins.then_inc(once("q_turned"), 1)
            pe.wait_ge(once("zeros_made"), 1)
            pe.wait_ge(once("wk_split"), 1)
            for i in range(2):
                ins = t.matmul(o_ps[:, 2 * i:2 * i + 2].rearrange("p g t -> p (g t)"), zeros[:, 0:P],
                               zeros[:], start=True, stop=True)
            ins.then_inc(av_made, NG)
            pe.wait_ge(once("wv_split"), 1)
            pe.wait_ge(once("q4_made"), NG)

            def project(it, r, which, c, n):
                hi, lo = ((wk_hi, wk_lo), (wv_hi, wv_lo))[which]
                left, right = ((ctx_hi, hi), (ctx_lo, hi), (ctx_hi, lo))[n]
                ins = t.matmul(kv_ps[:, which], left[r % 2][:, c], right[:, c],
                               start=(c == 0 and n == 0), stop=(c == CT - 1 and n == 2))
                if c == CT - 1 and n == 2:
                    ins.then_inc((k_made, v_made)[which], 1)

            def projection(it, r, first, last):
                for m in range(first, last):
                    if m == 0:
                        pe.wait_ge(ctx_lo_made, n_of(it, r, 1, 1))
                        wait(pe, k_kept, n_of(it, r))
                    if m == 12:
                        wait(pe, v_copied, n_of(it, r))
                    project(it, r, m // 12, m % 12 // 3, m % 3)

            def turn_keys(it, r, grp):
                if grp == 0:
                    pe.wait_ge(k_split, n_of(it, r, 1, 1))
                wait(pe, kt_even_made, n_of(it, r, 2 * NG, 2 * (grp - 1)))
                wait(pe, kt_odd_made, n_of(it, r, 2 * NG, 2 * (grp - 1)))
                for n in range(HG // 2):
                    h = HG * grp + 2 * n
                    parts = k_hl[r % 2][:, h:h + 2].rearrange("p h a d -> p (h a d)")
                    ins = t.matmul(t_ps[:, grp % 2, n * P:(n + 1) * P], parts, ident_r[:],
                                   start=True, stop=True)
                ins.then_inc(t_made, 1)

            def scores(it, r, grp):
                pe.wait_ge(kt_even_made, n_of(it, r, 2 * NG, 2 * (grp + 1)))
                pe.wait_ge(kt_odd_made, n_of(it, r, 2 * NG, 2 * (grp + 1)))
                wait(pe, probs_made, n_of(it, r, NG, grp))
                for h in range(HG):
                    ins = t.matmul(s_ps[:, h], kT[grp][:, h // 2, h % 2], q4[:, HG * grp + h],
                                   start=True, stop=True)
                ins.then_inc(s_made, 1)

            def attend(it, r, grp):
                pe.wait_ge(probs_made, n_of(it, r, NG, grp + 1))
                pe.wait_ge(v_copied, n_of(it, r, 1, 1))
                for h in range(HG):
                    ins = t.matmul(o_ps[D * h:D * h + D, grp], v_sb[r % 2][:, P * grp + D * h:P * grp + D * h + D],
                                   probs[grp][:, h], start=False, stop=False, skip_group_check=True)
                ins.then_inc(av_made, 1)

            QUARTER, BEFORE = 6, 4

            def step(it, r, project_it=True):
                for q in range(4):
                    a0, a1 = QUARTER * q, QUARTER * (q + 1)
                    half_way = a0 + BEFORE
                    if project_it:
                        projection(it, r, a0, half_way)
                    if not too_early(it, r, q - 2):
                        scores(it, *group(r, q - 2))
                    if project_it:
                        projection(it, r, half_way, a1)
                    if not too_early(it, r, q - 1):
                        turn_keys(it, *group(r, q - 1))
                    if not too_early(it, r, q - 3):
                        attend(it, *group(r, q - 3))

            def group(r, q):
                return r - 1 + q // 4, q % 4

            def too_early(it, r, q):
                return isinstance(it, int) and 4 * it + r - 1 + q // 4 < 0

            projection(0, 0, 0, 24)
            step(0, 1)
            with pe.Fori(0, nq) as it:
                for r in range(2, 6):
                    step(it, r)
            step(nq, 2)
            step(nq, 3)
            step(nq, 4, project_it=False)
            turn_keys(nq, 3, 3)
            scores(nq, 3, 2)
            attend(nq, 3, 1)
            scores(nq, 3, 3)
            attend(nq, 3, 2)
            attend(nq, 3, 3)

            pe.wait_ge(once("attention_done"), 1)
            pe.wait_ge(once("wp_in"), 16)
            for i in range(TT):
                for c in range(CT):
                    ins = t.matmul(pm[:, i], o_t[:, c, i * P:(i + 1) * P], wp[:, c],
                                   start=(c == 0), stop=(c == CT - 1))
            ins.then_inc(once("cross_made"), 1)
            pe.wait_ge(once("x1n_made"), 1)
            turn_rows(lambda c, i: po[:, c // 2, (c % 2) * TOK + i * P:(c % 2) * TOK + (i + 1) * P], xn)\
                .then_inc(once("x1n_turned"), 1)
            pe.wait_ge(once("x1_t_made"), 1)
            pe.wait_ge(once("qkv_w_in"), 16)
            for i in range(TT):
                wait(pe, once("qkv_copied"), i)
                for k in range(3):
                    for c in range(CT):
                        ins = t.matmul(pm[:, k], mid_t[:, c, i * P:(i + 1) * P],
                                       qkv_w[:, c, k * C:(k + 1) * C], start=(c == 0), stop=(c == CT - 1))
                ins.then_inc(once("qkv_made"), 1)
            pe.wait_ge(once("qk_made"), 1)
            for k in range(2):
                for i in range(TT):
                    for grp in range(NG):
                        first = (grp % 2) * TOK + i * P
                        ins = t.transpose(pm[:, 2 * k + grp // 2, first:first + P],
                                          qk_max[:, i, k * C + grp * P:k * C + (grp + 1) * P], ident[:])
                ins.then_inc(once("qk_turned"), 1)

            def lin_scores(h):
                grp, first = h // HG, D * (h % HG)
                q, k = (qk_t[first:first + D, i, grp] for i in range(2))
                pe.wait_ge(once("qk_t_made"), 2)
                wait(pe, once("lin_masked"), h - 3)
                t.matmul(pm[:, h % 4, 0:TOK], k[:, 0:P], q, start=True, stop=True)
                t.matmul(pm[:, h % 4, TOK:TOK + P], k[:, P:TOK], q[:, P:TOK], start=True, stop=True)\
                    .then_inc(once("lin_scores"), 1)

            def lin_values(h):
                pe.wait_ge(once("lin_masked"), h + 1)
                m, first = masked[h % 4], (h % 8) * (D + 1)
                out_of = [po[:, 2 * i + h // 8, first:first + D + 1] for i in range(TT)]
                t.matmul(out_of[0], m[:, 0:P], v_one[:, 0, h], start=True, stop=True)
                t.matmul(out_of[1], m[:, P:TOK], v_one[:, 0, h], start=True, stop=False)
                t.matmul(out_of[1], m[:, TOK:TOK + P], v_one[:, 1, h], start=False, stop=True)\
                    .then_inc(once("lin_used"), 1)

            for h in range(3):
                lin_scores(h)
            for h in range(H):
                if h + 3 < H:
                    lin_scores(h + 3)
                lin_values(h)
            pe.wait_ge(once("lin_made"), 1)
            turn_rows(lambda c, i: pm[:, c // 2, (c % 2) * TOK + i * P:(c % 2) * TOK + (i + 1) * P], mid_a)\
                .then_inc(once("lin_turned"), 1)
            pe.wait_ge(once("lin_t_made"), 1)
            pe.wait_ge(once("out_w_in"), 16)
            for i in range(TT):
                for c in range(CT):
                    ins = t.matmul(pm[:, 2 + i], mid_t[:, c, i * P:(i + 1) * P], out_w[:, c],
                                   start=(c == 0), stop=(c == CT - 1))
            ins.then_inc(once("self_made"), 1)
            pe.wait_ge(once("nx_made"), 1)
            turn_rows(lambda c, i: f_ps[:, c // 2, (c % 2) * TOK + i * P:(c % 2) * TOK + (i + 1) * P], nx)\
                .then_inc(once("nx_turned"), 1)
            pe.wait_ge(once("nx_t_made"), 1)
            pe.wait_ge(once("router_w_in"), 16)
            for i in range(TT):
                for c in range(CT):
                    ins = t.matmul(m_ps[:, 0, i * E:(i + 1) * E], nx_t[:, c, i * P:(i + 1) * P],
                                   router_w[:, c], start=(c == 0), stop=(c == CT - 1))
            ins.then_inc(once("logits"), 1)
            pe.wait_ge(once("gates"), 1)
            for i in range(TT):
                ins = t.transpose(m_ps[0:E, 1, i * P:(i + 1) * P], rt[:, 5, i], ident[:])
            ins.then_inc(once("gates_turned"), 1)
            pe.wait_ge(once("gate_t_made"), 1)
            for e in range(E):
                ins = t.matmul(f_ps[:, e // 2, (e % 2) * TOK:(e % 2 + 1) * TOK],
                               ident[0:E, e:e + 1].to_broadcast([E, P]), gate_t[:], start=True, stop=True)
                if e % 4 == 3:
                    ins.then_inc(once("gates_spread"), 1)
            pe.wait_ge(once("down_b_in"), 16)
            for i in range(TT):
                ins = t.matmul(y_ps[:, i], gate_t[:, i * P:(i + 1) * P], down_b[:], start=True, stop=True)
            ins.then_inc(w_used, 4)
            pe.wait_ge(once("gates_copied"), 2)

            def moments(half, what):
                step, norm = what or (None, None)
                k0 = NORMS.index(norm) if norm else 0
                if step == "mean":
                    pe.wait_ge(pre_summed, half * 2 + (k0 + 1))
                    t.matmul(m_ps[:, 0, 0:TOK], mean_w[:], sums[:, 0], start=True, stop=True)\
                        .then_inc(mean_made, 1)
                if step == "variance":
                    for k in range(4):
                        pe.wait_ge(sq_summed, half * 8 + (4 * k0 + k + 1))
                        ins = t.matmul(m_ps[:, 1, 0:TOK], mean_w[:], sums[:, 1 + k], start=(k == 0),
                                       stop=(k == 3))
                    ins.then_inc(var_made, 1)

            with pe.Fori(0, HALVES) as half:
                for name, kind, kt, src, dst, e, last in LAYERS:
                    s_hi, s_lo = hid[src]
                    per = OUT_TILES[name] // layer_chunks(name, kt)
                    if src == "xn":
                        pe.wait_ge(once("xn_split"), 1)

                    def source(k):
                        if src != "xn":
                            made = STAGE_BASE[SOURCE[name]] + k + 1 + 4
                            pe.wait_ge(h_made, half * TILES_HALF + made)

                    for q in quads(pe, name, kt):
                        for i in range(4):
                            pe.wait_ge(w_lo_made, at(half, CHUNKS_HALF, q, 4, CHUNK_BASE[name] + i + 1))
                            if kind == "down":
                                hi, lo = (w[i][:].rearrange("p (f n) -> p f n", f=4) for w in (w_hi, w_lo))
                                for j in range(4):
                                    source(4 * i + j)
                                    for tt in range(TT):
                                        rows_ = slice(tt * P, (tt + 1) * P)
                                        for l, w in ((s_hi, hi), (s_lo, hi), (s_hi, lo)):
                                            ins = t.matmul(y_ps[:, tt], l[:, 4 * i + j, rows_], w[:, j],
                                                           start=False, stop=False, skip_group_check=True)
                            for j in range(per):
                                n = i * per + j
                                slot = n % 4
                                pe.wait_ge(f_read, at(half, TILES_HALF, q, 4 * per, FILL_BASE[name] + n + 1))
                                hi, lo = (w[i][:].rearrange("p (k n) -> p k n", k=kt) for w in (w_hi, w_lo))
                                cols = slice(j * P, (j + 1) * P)
                                for k in range(kt):
                                    if i == 0 and j == 0:
                                        source(k)
                                    for m, (w, r) in enumerate(((hi, s_hi), (hi, s_lo), (lo, s_hi))):
                                        ins = t.matmul(f_ps[:, slot, 0:TOK], w[:, k, cols], r[:, k],
                                                       start=(k == 0 and m == 0),
                                                       stop=(k == kt - 1 and m == 2))
                                if j < per - 1:
                                    ins.then_inc(f_made, 1)
                            ins.then_inc(w_used, 1)
                            if i == 1:
                                moments(half, STEPS.get((name, "second")))
                        if isinstance(q, int) and q == 0:
                            moments(half, STEPS.get((name, "four")))
                    moments(half, STEPS.get((name, "end")))


def kernel(**inputs):
    import numpy as np
    import concourse.bacc as bacc
    from concourse.bass_utils import run_bass_kernel_spmd as run

    i = {k: np.asarray(v) for k, v in inputs.items()}
    f = {k[len("L0_ffn_"):]: v for k, v in i.items() if k.startswith("L0_ffn_")}
    xa = {k[len("L0_xattn_"):]: v for k, v in i.items() if k.startswith("L0_xattn_")}

    def chunks(w):
        return w.reshape(-1, P, w.shape[1]).transpose(1, 0, 2)

    def stream(w, name):
        k, n = w.shape
        if name == "down":
            return w.reshape(E // HALVES, 4, P, n).transpose(0, 2, 1, 3).reshape(-1, P, CHUNK)
        kt = k // P
        return w.reshape(kt, P, -1, CHUNK // kt).transpose(2, 1, 0, 3).reshape(-1, P, CHUNK)

    def columns(v):
        return v.reshape(-1, P).T

    spec = {"spec0": "spec0_W", "spec1a": "spec1a_W", "spec1b": "spec1b_W", "spec2": "spec2_W"}
    w = []
    for half in range(HALVES):
        for name, kind, kt, src, dst, e, last in LAYERS:
            if name.startswith("up"):
                w.append(stream(f["up_W"][half * 4 + e], "up"))
            elif kind == "down":
                w.append(stream(f["down_W"][half * 4 + e], "down"))
            else:
                w.append(stream(f[spec[name]][half], name))
    arrays = {
        "x": chunks(i["x"][0]),
        "ctx": i["ctx_1024"][0].reshape(KT, P, CT, P).transpose(0, 3, 2, 1).reshape(KT, P, C),
        "wq": chunks(xa["Wq"].T),
        "wk": chunks(xa["Wk"]),
        "wv": chunks(xa["Wv"].T),
        "wp": chunks(xa["Wp"].T),
        "head_vecs": np.broadcast_to(np.stack([xa["gq"], xa["bq"], xa["gk"], xa["bk"]]), (P, 4, D)),
        "bias_rows": np.broadcast_to(
            np.concatenate([xa["bp"], i["L0_attn_out_b"], i["L0_attn_qkv_b"]]).reshape(5, C), (P, 5, C)),
        "qkv_w": chunks(i["L0_attn_qkv_w"]),
        "out_w": chunks(i["L0_attn_out_w"]),
        "ln_rows": np.broadcast_to(np.stack([f["ln_g"], f["ln_b"]]), (P, 2, C)),
        "router_w": chunks(f["router_w"]),
        "down_b": f["down_b"],
        "bias_cols": np.concatenate([columns(f[n]) for n in (
            "up_b", "spec0_b", "ln0_g", "ln0_b", "spec1a_b", "spec1b_b", "ln1_g", "ln1_b", "spec2_b")],
            axis=1),
        "w": np.concatenate(w),
    }
    arrays = {k: np.ascontiguousarray(v) for k, v in arrays.items()}
    nc = bacc.Bacc("TRN2", target_bir_lowering=False, num_devices=1,
                   dynamic_dma_scratch_size=1024)
    given = {k: nc.dram_tensor(k + "_dram", v.shape, mybir.dt.from_np(v.dtype), kind="ExternalInput").ap()
             for k, v in arrays.items()}
    out = nc.dram_tensor("out_dram", (P, TT, C), mybir.dt.float32, kind="ExternalOutput").ap()
    perceiver_block(nc, given, out)
    r = run(nc, [{k + "_dram": v for k, v in arrays.items()}], core_ids=[0])
    return r.results[0]["out_dram"].transpose(1, 0, 2).reshape(1, TOK, C)
```

```python
from contextlib import ExitStack

import concourse.bass as bass
from concourse import mybir

TOK, C, H, D = 256, 512, 16, 32
NK = 25088
P = 128
TT, CT = TOK // P, C // P
KT = NK // P
HG = P // D
NG = H // HG
F, E, HALVES = 2048, 8, 2
FT = F // P
UNROLL = 4
CHUNK = 2048
WR = 4
RAW = 2

LAYERS = [
    ("up0", "gelu", 4, "xn", "h1", 0, False),
    ("spec0", "norm", 16, "h1", "pre", 0, True),
    ("up1", "gelu", 4, "xn", "h1", 1, False),
    ("spec1a", "gelu", 16, "h1", "h2", 1, False),
    ("spec1b", "norm", 8, "h2", "pre", 1, True),
    ("down0", "down", 16, "h1", "y", 0, False),
    ("up2", "gelu", 4, "xn", "h2", 2, False),
    ("spec2", "gelu", 16, "h2", "h1", 2, True),
    ("down2", "down", 16, "h1", "y", 2, False),
    ("down1", "down", 16, "h2", "y", 1, False),
    ("up3", "gelu", 4, "xn", "h1", 3, True),
    ("down3", "down", 16, "h1", "y", 3, False),
]
OUT_TILES = {"up0": 16, "up1": 16, "up2": 16, "up3": 16, "spec0": 16, "spec1a": 8, "spec1b": 16,
             "spec2": 16, "down0": 0, "down1": 0, "down2": 0, "down3": 0}
NORMS = ["spec0", "spec1b"]
NORM_OUT = {"spec0": "h1", "spec1b": "h2"}
STEPS = {
    ("up1", "second"): ("mean", "spec0"), ("up1", "end"): ("squares", "spec0"),
    ("spec1a", "four"): ("variance", "spec0"), ("spec1b", "spread"): ("apply", "spec0"),
    ("down0", "second"): ("mean", "spec1b"), ("down0", "end"): ("squares", "spec1b"),
    ("up2", "end"): ("variance", "spec1b"), ("spec2", "end"): ("apply", "spec1b"),
}
NORM_AFTER = {layer: norm for (layer, _), (step, norm) in STEPS.items() if step == "apply"}


def layer_chunks(name, kt):
    return (E // HALVES) if name.startswith("down") else OUT_TILES[name] * kt * P // CHUNK


ROOT_STEPS = 4
ROOT_OPS = 3 + 3 * ROOT_STEPS
CHUNKS = {n: layer_chunks(n, kt) for n, _, kt, *_ in LAYERS}
CHUNKS_HALF = sum(CHUNKS.values())
TILES_HALF = sum(OUT_TILES.values())
EARLY = {n: max(0, OUT_TILES[n] - CHUNKS[n]) for n in CHUNKS}
EARLY_HALF = sum(EARLY.values())
CHUNK_BASE, FILL_BASE, EARLY_BASE, STAGE_BASE = {}, {}, {}, {}
_stage = 0
for _n, _kind, _kt, _src, _dst, _e, _last in LAYERS:
    CHUNK_BASE[_n] = sum(CHUNKS[m] for m in CHUNK_BASE)
    FILL_BASE[_n] = sum(OUT_TILES[m] for m in FILL_BASE)
    EARLY_BASE[_n] = sum(EARLY[m] for m in EARLY_BASE)
    for _m in ([_n] if _kind == "gelu" else []) + ([NORM_AFTER[_n]] if _n in NORM_AFTER else []):
        STAGE_BASE[_m] = _stage
        _stage += OUT_TILES[_m]
SOURCE = {"spec0": "up0", "spec1a": "up1", "spec1b": "spec1a", "spec2": "up2",
          "down0": "spec0", "down1": "spec1b", "down2": "spec2", "down3": "up3"}
COLS, BIAS_COLS = {}, 0
for _n, _per in (("up_b", 4 * FT), ("spec0_b", FT), ("ln0_g", FT), ("ln0_b", FT), ("spec1a_b", 8),
                 ("spec1b_b", FT), ("ln1_g", FT), ("ln1_b", FT), ("spec2_b", FT)):
    COLS[_n] = (BIAS_COLS, _per)
    BIAS_COLS += 2 * _per
BIAS = {"up0": ("up_b", 0), "up1": ("up_b", 1), "up2": ("up_b", 2), "up3": ("up_b", 3),
        "spec0": ("spec0_b", 0), "spec1a": ("spec1a_b", 0), "spec1b": ("spec1b_b", 0),
        "spec2": ("spec2_b", 0)}


def perceiver_block(nc, a, out, NKT=KT):
    f32, f32r = mybir.dt.float32, mybir.dt.float32r
    ALU, ACT, AX = mybir.AluOpType, mybir.ActivationFunctionType, mybir.AxisListType.X
    nq = (NKT - 4) // UNROLL
    life = ExitStack()
    with life:
        def sb(name, shape, dt=f32, scope=life):
            return scope.enter_context(nc.sbuf_tensor(name, shape, dt))

        def ps(name, shape, scope):
            return scope.enter_context(nc.psum_tensor(name, shape, f32))

        def sem(name):
            return life.enter_context(nc.semaphore(name))

        named = {}

        def once(name):
            if name not in named:
                named[name] = sem(name)
            return named[name]

        setup = ExitStack()
        wq = sb("wq", [P, CT, C], f32, setup)
        wk = sb("wk_rows", [P, CT, C], f32, setup)
        wv = sb("wv", [P, CT, C], f32, setup)
        centre = sb("centre", [P, P], f32, setup)
        head_vecs = sb("head_vecs", [P, 4, D], f32, setup)
        x_t = sb("x_t", [P, CT, TOK], f32, setup)
        big = [sb(f"setup_big{i}", [P, TT, C], f32, setup) for i in range(2)]
        q_parts = sb("q_parts", [P, TT, H, 4, D], f32, setup)
        setup.close()

        w_hi, w_lo = [], []
        for i in range(WR):
            if i == WR // 2:
                late_slots = ExitStack()
                qkv_w = sb("qkv_w", [P, CT, 3 * C], f32, late_slots)
                wp = sb("wp", [P, CT, C], f32, late_slots)
                late_slots.close()
            w_hi.append(sb(f"w_hi{i}", [P, CHUNK], f32r))
            w_lo.append(sb(f"w_lo{i}", [P, CHUNK], f32r))
        w_raw = [sb(f"w_raw{i}", [P, CHUNK]) for i in range(RAW)]
        x = sb("x_rows", [P, TT, C])
        xn = sb("x_norm", [P, TT, C])
        ident = sb("ident", [P, P])
        neg_half = sb("neg_half", [P, 1])
        stat = sb("stat", [P, 4, 32])
        row_stat = sb("row_stat", [P, TT, 6])
        row_mean = sb("row_mean", [P, TT, 2])
        down_b = sb("down_b", [E, C])
        vec = sb("bias_cols", [P, BIAS_COLS])
        router_w = sb("router_w", [P, CT, E])

        early = ExitStack()
        rows = sb("bias_rows", [P, 5, C], f32, early)
        out_w = sb("out_w", [P, CT, C], f32, early)
        lnv = sb("ln_rows", [P, 2, C], f32, early)

        attn = ExitStack()
        raw = [sb(f"ctx_raw{i}", [P, CT, P], f32, attn) for i in range(4)]
        ctx_hi = [sb(f"ctx_hi{i}", [P, CT, P], f32r, attn) for i in range(2)]
        ctx_lo = [sb(f"ctx_lo{i}", [P, CT, P], f32r, attn) for i in range(2)]
        wk_hi = sb("wk_hi", [P, CT, C], f32r, attn)
        wk_lo = sb("wk_lo", [P, CT, C], f32r, attn)
        wv_hi = sb("wv_hi", [P, CT, C], f32r, attn)
        wv_lo = sb("wv_lo", [P, CT, C], f32r, attn)
        q4 = sb("q4", [P, H, TOK], f32r, attn)
        k_c = sb("k_centred", [P, H, D], f32, attn)
        k_sq = sb("k_sq", [P, H, D], f32, attn)
        k_var = sb("k_var", [P, 3, H], f32, attn)
        k_eps = sb("k_eps", [P, 1], f32, attn)
        k_n = sb("k_n", [P, H, D - 1], f32, attn)
        k_hl = [sb(f"k_hl{i}", [P, H, 2, D], f32r, attn) for i in range(2)]
        kT = [sb(f"kT{g}", [P, HG // 2, 2, P], f32r, attn) for g in range(NG)]
        v_sb = [sb(f"v_sb{i}", [P, C], f32, attn) for i in range(2)]
        probs = [sb(f"probs{g}", [P, HG, TOK], f32, attn) for g in range(NG)]
        zeros = probs[-1][:, 0:2].rearrange("p h t -> p (h t)")
        ident_r = sb("ident_r", [P, P], f32r, attn)
        psum_a = ExitStack()
        o_ps = ps("o_ps", [P, NG, TOK], psum_a)
        kv_ps = ps("kv_ps", [P, 2, C], psum_a)
        s_ps = ps("s_ps", [P, HG, TOK], psum_a)
        t_ps = ps("t_ps", [P, 2, C], psum_a)
        psum_a.close()
        attn.close()

        mid = ExitStack()
        o_t = sb("o_t", [P, NG, TOK], f32, mid)
        qkv = sb("qkv", [P, TT, 3 * C], f32, mid)
        qk_min = sb("qk_min", [P, TT, 2 * C], f32, mid)
        qk_max = sb("qk_max", [P, TT, 2 * C], f32, mid)
        ones = sb("ones", [P, D], f32, mid)
        qk_t = sb("qk_t", [P, 2, NG, TOK], f32, mid)
        mid_t = sb("mid_t", [P, CT, TOK], f32, mid)
        causal = sb("causal", [P, TOK + P], f32, mid)
        masked = [sb(f"masked{i}", [P, TOK + P], f32, mid) for i in range(8)]
        lin_norm = sb("lin_norm", [P, CT, TOK], f32, mid)
        mid.close()
        early.close()
        psum_m = ExitStack()
        pm = ps("pm", [P, 4, 512], psum_m)
        po = ps("po", [P, 4, 512], psum_m)
        psum_m.close()

        ffn = ExitStack()
        hid = {n: (sb(f"{n}_hi", [P, FT, TOK], f32r, ffn), sb(f"{n}_lo", [P, FT, TOK], f32r, ffn))
               for n in ("h1", "h2")}
        pre = sb("pre", [P, FT, TOK], f32, ffn)
        stage = [sb(f"stage{i}", [P, TOK], f32, ffn) for i in range(4)]
        sq = [sb(f"sq{i}", [P, 4, TOK], f32, ffn) for i in range(2)]
        hid["xn"] = (sb("xn_hi", [P, CT, TOK], f32r, ffn), sb("xn_lo", [P, CT, TOK], f32r, ffn))
        gate = sb("gate", [P, E, TOK], f32, ffn)
        gate_t = sb("gate_t", [E, TOK], f32, ffn)
        gate_parts = sb("gate_parts", [E, 2, TOK], f32r, ffn)
        pick = sb("pick", [E, E], f32r, ffn)
        mean_w = sb("mean_w", [P, P], f32, ffn)
        moment = sb("moment", [P, 4, TOK], f32, ffn)
        sums = sb("sums", [P, 5, TOK], f32, ffn)
        rt = sb("router_tmp", [P, 8, TT, E], f32, ffn)
        lower = sb("lower", [P, E, E], f32, ffn)
        psum_f = ExitStack()
        y_ps = ps("y_ps", [P, TT, C], psum_f)
        f_ps = ps("f_ps", [P, 4, 512], psum_f)
        m_ps = ps("m_ps", [P, 2, 512], psum_f)
        psum_f.close()
        ffn.close()

        def as_rows(t):
            return t.rearrange("p a b -> p (a b)").rearrange("p (t c) -> p t c", t=TT)

        nx_t, nx = pre[:, 0:CT], as_rows(pre[:, 8:12])
        cmp = [pre[:, 4 + i, 0:TT * E * E].rearrange("p (t e f) -> p t e f", t=TT, e=E) for i in range(2)]

        q_turned_in = [s_ps[:], t_ps[:].rearrange("p a (b c) -> p (a b) c", b=2)]

        raw_in = [sem(f"raw_in{i}") for i in range(4)]
        ctx_hi_made, ctx_lo_made = sem("ctx_hi_made"), sem("ctx_lo_made")
        k_made, v_made = sem("k_made"), sem("v_made")
        k_sq_made, k_sum_made = sem("k_sq_made"), sem("k_sum_made")
        k_kept = sem("k_kept")
        k_var_made, k_dev_made = sem("k_var_made"), sem("k_dev_made")
        k_normed, k_hi_made, k_split = sem("k_normed"), sem("k_hi_made"), sem("k_split")
        t_made = sem("t_made")
        kt_even_made, kt_odd_made = sem("kt_even_made"), sem("kt_odd_made")
        s_made, probs_made, av_made = sem("s_made"), sem("probs_made"), sem("av_made")
        v_copied = sem("v_copied")
        w_in = [sem(f"w_in{i}") for i in range(RAW)]
        w_hi_made, w_lo_made, w_used = sem("w_hi_made"), sem("w_lo_made"), sem("w_used")
        f_made = sem("f_made")
        f_read = sem("f_read")
        h_hi_made, h_made = sem("h_hi_made"), sem("h_made")
        pre_summed, mean_made = sem("pre_summed"), sem("mean_made")
        mean_copied, centred = sem("mean_copied"), sem("centred")
        sq_made, sq_summed, var_made = sem("sq_made"), sem("sq_summed"), sem("var_made")
        root_step, scaled = sem("root_step"), sem("scaled")
        applied = sem("applied")
        done = sem("done")

        def wait(eng, s, v):
            if not isinstance(v, int) or v > 0:
                eng.wait_ge(s, v)

        def n_of(it, r, per=1, more=0):
            if isinstance(it, int):
                return per * (4 * it + r) + more
            return it * (4 * per) + (per * r + more)

        def is_first(it, r, t):
            return isinstance(it, int) and 4 * it + r == t

        def at(half, per_half, q, per_q, more):
            v = half * per_half + more
            return v if isinstance(q, int) and q == 0 else v + q * per_q

        def one(t, i):
            return t[:, i] if isinstance(i, int) else t[:, bass.ds(i, 1)].rearrange("p o t -> p (o t)")

        def per_row(ap2, n):
            return ap2.unsqueeze(2).to_broadcast([ap2.shape[0], ap2.shape[1], n])

        def repeat(ap2, n):
            return ap2.unsqueeze(1).to_broadcast([ap2.shape[0], n, ap2.shape[1]])

        def quads(eng, name, kt):
            n = layer_chunks(name, kt) // 4
            if n <= 2:
                yield from range(n)
            else:
                with eng.Fori(0, n) as q:
                    yield q

        def spread_tiles(name, q, i):
            if (name, "spread") not in STEPS:
                return ()
            per = FT // CHUNKS[name]
            return range(per * (4 * q + i), per * (4 * q + i + 1))

        block = life.enter_context(nc.Block())

        @block.sync
        def _(sp):
            for name, dst in (("x", x), ("wq", wq), ("wk", wk), ("wv", wv), ("head_vecs", head_vecs)):
                sp.dma_start(dst[:], a[name]).then_inc(once(name + "_in"), 16)

            def load_ctx(it, r):
                wait(sp, ctx_lo_made, n_of(it, r, 1, -3))
                t = n_of(it, r)
                tile = a["ctx"][t] if isinstance(t, int) else \
                    a["ctx"][bass.ds(t, 1)].rearrange("o p n -> (o p) n")
                sp.dma_start(raw[r][:].rearrange("p a b -> p (a b)"), tile).then_inc(raw_in[r], 16)

            for r in range(4):
                load_ctx(0, r)
            for i in range(RAW):
                sp.dma_start(w_raw[i][:], a["w"][i]).then_inc(w_in[i], 16)
            for name, dst in (("bias_rows", rows), ("out_w", out_w), ("ln_rows", lnv),
                              ("router_w", router_w), ("down_b", down_b), ("bias_cols", vec)):
                sp.dma_start(dst[:], a[name]).then_inc(once(name + "_in"), 16)
            sp.wait_ge(once("q4_made"), NG)
            for name, dst in (("wp", wp), ("qkv_w", qkv_w)):
                sp.dma_start(dst[:], a[name]).then_inc(once(name + "_in"), 16)
            with sp.Fori(1, NKT // 4) as it:
                for r in range(4):
                    load_ctx(it, r)
            with sp.Fori(1, HALVES * CHUNKS_HALF // RAW) as it:
                for i in range(RAW):
                    sp.wait_ge(w_lo_made, it * RAW + (i - RAW + 1))
                    sp.dma_start(w_raw[i][:], a["w"][bass.ds(it * RAW + i, 1)]
                                 .rearrange("o p n -> (o p) n")).then_inc(w_in[i], 16)
            for i in range(4):
                sp.wait_ge(w_lo_made, HALVES * CHUNKS_HALF + (i - RAW + 1))
                sp.sem_inc(w_in[i % RAW], 16)
            sp.wait_ge(once("result"), 1)
            sp.dma_start(out, x[:]).then_inc(done, 16)
            sp.wait_ge(done, 16)

        @block.gpsimd
        def _(pool):
            g = nc.gpsimd
            own, count = sem("pool_own"), [0]

            def link(ins):
                count[0] += 1
                ins.then_inc(own, 1)
                pool.wait_ge(own, count[0])

            def deviations(n, tag):
                pool.wait_ge(once(tag + "_var"), 1)
                g.tensor_tensor(stat[:, 2, 0:n], stat[:, 3, 0:n], neg_half[:].to_broadcast([P, n]),
                                ALU.pow).then_inc(once(tag + "_dev"), 1)

            link(g.memset(neg_half[:], -0.5))
            link(g.memset(k_eps[:], 1e-5))
            link(g.memset(ident[:], 0.0))
            link(g.affine_select(out=ident[:], in_=ident[:], compare_op=ALU.not_equal, fill=1.0,
                                 base=0, pattern=[[-1, P]], channel_multiplier=1))
            c3 = centre[:].rearrange("p (b d) -> p b d", b=HG)
            link(g.memset(centre[:], -1.0 / D))
            link(g.affine_select(out=c3, in_=c3, compare_op=ALU.is_ge, fill=0.0, base=0,
                                 pattern=[[-D, HG], [0, D]], channel_multiplier=1))
            link(g.affine_select(out=c3, in_=c3, compare_op=ALU.is_ge, fill=0.0, base=D - 1,
                                 pattern=[[D, HG], [0, D]], channel_multiplier=-1))
            g.tensor_tensor(centre[:], centre[:], ident[:], ALU.add).then_inc(once("consts"), 1)
            for i in range(2):
                link(g.memset(k_hl[i][:].bitcast(f32), 0.0))
                link(g.memset(k_hl[i][:, :, 0, D - 1:D].bitcast(f32), 1.0))
            g.memset(zeros, 0.0).then_inc(once("zeros_made"), 1)
            deviations(TT, "x")

            def low_part(it, r):
                pool.wait_ge(ctx_hi_made, n_of(it, r, 1, 1))
                wait(pool, v_made, n_of(it, r, 1, -1))
                g.tensor_tensor(ctx_lo[r % 2][:], raw[r % 4][:], ctx_hi[r % 2][:].bitcast(f32),
                                ALU.subtract).then_inc(ctx_lo_made, 1)

            def deviation(it, r):
                pool.wait_ge(k_sum_made, n_of(it, r, 1, 1))
                g.tensor_tensor(k_var[:, 1], k_var[:, 0], k_eps[:].to_broadcast([P, H]), ALU.add)\
                    .then_inc(k_var_made, 1)
                pool.wait_ge(k_var_made, n_of(it, r, 1, 1))
                wait(pool, k_normed, n_of(it, r))
                g.tensor_tensor(k_var[:, 2], k_var[:, 1], neg_half[:].to_broadcast([P, H]), ALU.pow)\
                    .then_inc(k_dev_made, 1)

            def step(it, r, last=False):
                if not last:
                    low_part(it, r + 1)
                deviation(it, r)

            low_part(0, 0)
            low_part(0, 1)
            deviations(TT * H, "q")
            deviation(0, 0)
            step(0, 1)
            with pool.Fori(0, nq) as it:
                for r in range(2, 6):
                    step(it, r)
            step(nq, 2)
            step(nq, 3, last=True)
            pool.wait_ge(once("xn_made"), TT)
            pool.wait_ge(once("bias_rows_in"), 16)
            g.tensor_tensor(x[:], x[:], repeat(rows[:, 0], TT), ALU.add).then_inc(once("x_offset"), 1)

            pool.wait_ge(once("attention_done"), 2)
            link(g.memset(causal[:], 1.0))
            for first, n in ((0, TOK), (TOK, P)):
                link(g.affine_select(out=causal[:, first:first + n], in_=causal[:, first:first + n],
                                     compare_op=ALU.is_ge, fill=0.0, base=0, pattern=[[1, n]],
                                     channel_multiplier=-1))
            g.memset(ones[:], 1.0).then_inc(once("mid_consts"), 1)
            deviations(TT, "x1")
            pool.wait_ge(once("x1n_made"), TT)
            g.tensor_tensor(x[:], x[:], repeat(rows[:, 1], TT), ALU.add).then_inc(once("x1_offset"), 1)
            pool.wait_ge(once("x2_made"), TT)
            link(g.memset(mean_w[:], 1.0 / F))
            link(g.memset(lower[:], 1.0))
            g.affine_select(out=lower[:], in_=lower[:], compare_op=ALU.is_ge, fill=0.0, base=-1,
                            pattern=[[1, E], [-1, E]], channel_multiplier=0)\
                .then_inc(once("router_consts"), 1)
            deviations(TT, "x2")
            deviations(TT, "nx")
            pool.sem_inc(h_made, 4)

            def low_tiles(half, dst, base):
                def make(q):
                    for i in range(4):
                        pool.wait_ge(h_hi_made, at(half, TILES_HALF, q, 4, base + i + 1))
                        hi, lo = (one(t, q * 4 + i) for t in hid[dst])
                        g.tensor_tensor(lo, stage[i][:], hi.bitcast(f32), ALU.subtract)\
                            .then_inc(h_made, 1)
                return make

            with pool.Fori(0, HALVES) as half:
                for name, kind, kt, src, dst, e, last in LAYERS:
                    if kind == "gelu":
                        make = low_tiles(half, dst, STAGE_BASE[name])
                        with pool.Fori(0, OUT_TILES[name] // 4) as q:
                            make(q)
                    if name in NORM_AFTER:
                        norm = NORM_AFTER[name]
                        make = low_tiles(half, NORM_OUT[norm], STAGE_BASE[norm])
                        with pool.Fori(0, FT // 4) as q:
                            make(q)

        @block.scalar
        def _(act):
            s = nc.scalar

            def sigmoid(it, r, grp):
                act.wait_ge(s_made, n_of(it, r, NG, grp + 1))
                act.wait_ge(av_made, n_of(it, r, NG, grp + 1))
                s.activation(probs[grp][:], s_ps[:], ACT.Sigmoid).then_inc(probs_made, 1)

            def copy_turned(it, r, grp):
                act.wait_ge(t_made, n_of(it, r, NG, grp + 1))
                wait(act, s_made, n_of(it, r, NG, grp - 3))
                pairs = t_ps[:, grp % 2, 0:HG // 2 * P].rearrange("p (n k) -> p n k", n=HG // 2)
                s.activation(kT[grp][0:P // 2, :, 1], pairs[P // 2:P], ACT.Copy).then_inc(kt_odd_made, 1)
                s.activation(kT[grp][P // 2:P, :, 1], pairs[P // 2:P], ACT.Copy).then_inc(kt_odd_made, 1)

            def square(it, r):
                act.wait_ge(k_made, n_of(it, r, 1, 1))
                wait(act, k_sum_made, n_of(it, r))
                s.activation(k_sq[:].rearrange("p h d -> p (h d)"), kv_ps[:, 0], ACT.Square,
                             scale=float(D) ** -0.5).then_inc(k_sq_made, 1)
                wait(act, k_normed, n_of(it, r))
                s.activation(k_c[:].rearrange("p h d -> p (h d)"), kv_ps[:, 0], ACT.Copy)\
                    .then_inc(k_kept, 1)

            def step(it, r, keys=True):
                if not (is_first(it, r, 0) or is_first(it, r, 1)):
                    sigmoid(it, r - 2, 2)
                    copy_turned(it, r - 2, 3)
                    sigmoid(it, r - 2, 3)
                if not is_first(it, r, 0):
                    copy_turned(it, r - 1, 0)
                if keys:
                    square(it, r)
                if not is_first(it, r, 0):
                    sigmoid(it, r - 1, 0)
                    copy_turned(it, r - 1, 1)
                    sigmoid(it, r - 1, 1)
                    copy_turned(it, r - 1, 2)

            step(0, 0)
            step(0, 1)
            with act.Fori(0, nq) as it:
                for r in range(2, 6):
                    step(it, r)
            step(nq, 2)
            step(nq, 3)
            step(nq, 4, keys=False)
            sigmoid(nq, 3, 2)
            copy_turned(nq, 3, 3)
            sigmoid(nq, 3, 3)

            act.wait_ge(av_made, NG * (NKT + 1))
            s.activation(o_t[:, 2:4], o_ps[:, 2:4], ACT.Copy).then_inc(once("attention_done"), 1)

            def high(half, q, base, i):
                act.wait_ge(w_in[i % RAW], at(half, 8 * CHUNKS_HALF, q, 32, 8 * base + 16 * (i // 2 + 1)))
                act.wait_ge(w_used, at(half, CHUNKS_HALF, q, 4, base + i + 1))
                s.activation(w_hi[i][:], w_raw[i % RAW][:], ACT.Copy).then_inc(w_hi_made, 1)

            high(0, 0, 0, 0)
            high(0, 0, 0, 1)
            for i in range(TT):
                act.wait_ge(once("qk_min_made"), i + 1)
                s.activation(qk_min[:, i], qk_min[:, i], ACT.Exp).then_inc(once("qk_exp"), 1)
            high(0, 0, 0, 2)
            high(0, 0, 0, 3)
            act.wait_ge(once("logits_less_max"), 1)
            s.activation(rt[:, 1], rt[:, 0], ACT.Exp).then_inc(once("router_exp"), 1)
            act.sem_inc(f_read, 4)
            act.wait_ge(once("bias_cols_in"), 16)

            def column(key, half, q, per_q, more):
                first, per = COLS[key]
                i = at(half, per, q, per_q, first + more)
                return vec[:, i:i + 1] if isinstance(i, int) else vec[:, bass.ds(i, 1)]

            def apply(half, q, norm, n):
                k0 = NORMS.index(norm)
                act.wait_ge(scaled, at(half, 8, q, 1, 4 * k0 + n // 4 + 1))
                act.wait_ge(h_made, at(half, TILES_HALF, q, 4, STAGE_BASE[norm] + n + 1))
                s.activation(stage[n % 4][:], one(pre, q * 4 + n),
                             ACT.Gelu if k0 == 0 else ACT.Identity,
                             bias=column(f"ln{k0}_b", half, q, 4, n),
                             scale=column(f"ln{k0}_g", half, q, 4, n)).then_inc(applied, 1)

            with act.Fori(0, HALVES) as half:
                for name, kind, kt, src, dst, e, last in LAYERS:
                    per = OUT_TILES[name] // layer_chunks(name, kt)
                    for q in quads(act, name, kt):
                        for i in range(4):
                            for n in spread_tiles(name, q, i):
                                apply(half, 0, STEPS[name, "spread"][1], n)
                            for j in range(per):
                                n = i * per + j
                                slot = n % 4
                                if j < per - 1:
                                    act.wait_ge(f_made, at(half, EARLY_HALF, q, 4 * (per - 1),
                                                           EARLY_BASE[name] + i * (per - 1) + j + 1))
                                else:
                                    act.wait_ge(w_used, at(half, CHUNKS_HALF, q, 4,
                                                           CHUNK_BASE[name] + i + 1 + 4))
                                bias = column(BIAS[name][0], half, q, 4 * per, BIAS[name][1] * FT + n)
                                if kind == "gelu":
                                    act.wait_ge(h_made, at(half, TILES_HALF, q, 4 * per,
                                                           STAGE_BASE[name] + n + 1))
                                    s.activation(stage[slot][:], f_ps[:, slot, 0:TOK], ACT.Gelu,
                                                 bias=bias).then_inc(f_read, 1)
                                else:
                                    if (name, "spread") in STEPS:
                                        act.wait_ge(applied, half * (2 * FT) + (q * (4 * per) + n + 1))
                                    s.activation(one(pre, q * (4 * per) + n), f_ps[:, slot, 0:TOK],
                                                 ACT.Identity, bias=bias).then_inc(f_read, 1)
                            high(half, q, CHUNK_BASE[name] + 4, i)
                    step, norm = STEPS.get((name, "end"), (None, None))
                    if step == "squares":
                        k0 = NORMS.index(norm)
                        for k in range(4):
                            act.wait_ge(centred, half * 8 + (4 * k0 + k + 1))
                            if k >= 2:
                                act.wait_ge(sq_summed, half * 8 + (4 * k0 + k - 1))
                            s.activation(sq[k % 2][:], pre[:, 4 * k:4 * k + 4], ACT.Square)\
                                .then_inc(sq_made, 1)
                    if step == "apply":
                        with act.Fori(0, 4) as q:
                            for i in range(4):
                                apply(half, q, norm, i)

        @block.vector
        def _(dve):
            v = nc.vector
            own, count = sem("dve_own"), [0]

            def link(ins):
                count[0] += 1
                ins.then_inc(own, 1)
                dve.wait_ge(own, count[0])
                return ins

            def low(half, q, base, i):
                dve.wait_ge(w_hi_made, at(half, CHUNKS_HALF, q, 4, base + i + 1))
                v.tensor_tensor(w_lo[i][:], w_raw[i % RAW][:], w_hi[i][:].bitcast(f32), ALU.subtract)\
                    .then_inc(w_lo_made, 1)

            def row_stats(src, tag):
                for i in range(TT):
                    link(v.bn_stats(row_stat[:, i], src[:, i]))
                    link(v.bn_aggr(row_mean[:, i], row_stat[:, i]))
                v.tensor_scalar(stat[:, 3, 0:TT], row_mean[:, :, 1], 1e-5, None, ALU.add)\
                    .then_inc(once(tag + "_var"), 1)
                dve.wait_ge(once(tag + "_dev"), 1)

            def layernorm_rows(dst, src, tag):
                row_stats(src, tag)
                for i in range(TT):
                    v.tensor_scalar(dst[:, i], src[:, i], row_mean[:, i, 0:1], stat[:, 2, i:i + 1],
                                    ALU.subtract, ALU.mult).then_inc(once(tag + "n_made"), 1)

            def layernorm(dst, src, cen, sqr, eps, tag, meanwhile):
                n, w = dst.shape[1], dst.shape[2]
                link(v.tensor_reduce(stat[:, 1, 0:n], src, AX, ALU.add))
                link(v.tensor_scalar(stat[:, 0, 0:n], stat[:, 1, 0:n], 1.0 / w, None, ALU.mult))
                link(v.tensor_tensor(cen, src, per_row(stat[:, 0, 0:n], w), ALU.subtract))
                dve.sem_inc(once(tag + "_read"), 1)
                link(v.tensor_tensor(sqr, cen, cen, ALU.mult))
                link(v.tensor_reduce(stat[:, 1, 0:n], sqr, AX, ALU.add))
                v.tensor_scalar(stat[:, 3, 0:n], stat[:, 1, 0:n], 1.0 / w, eps, ALU.mult, ALU.add)\
                    .then_inc(once(tag + "_var"), 1)
                meanwhile()
                dve.wait_ge(once(tag + "_dev"), 1)
                link(v.tensor_tensor(dst, cen, per_row(stat[:, 2, 0:n], w), ALU.mult))

            def high_part(it, r):
                if isinstance(it, int):
                    dve.wait_ge(raw_in[r % 4], 16 * (it + r // 4 + 1))
                else:
                    dve.wait_ge(raw_in[r % 4], it * 16 + 16 * (r // 4 + 1))
                wait(dve, v_made, n_of(it, r, 1, -1))
                v.tensor_copy(ctx_hi[r % 2][:], raw[r % 4][:]).then_inc(ctx_hi_made, 1)

            def copy_turned(it, r, grp):
                dve.wait_ge(t_made, n_of(it, r, NG, grp + 1))
                wait(dve, s_made, n_of(it, r, NG, grp - 3))
                pairs = t_ps[:, grp % 2, 0:HG // 2 * P].rearrange("p (n k) -> p n k", n=HG // 2)
                v.tensor_copy(kT[grp][0:P // 2, :, 0], pairs[0:P // 2]).then_inc(kt_even_made, 1)
                v.tensor_copy(kT[grp][P // 2:P, :, 0], pairs[0:P // 2]).then_inc(kt_even_made, 1)

            def copy_values(it, r):
                dve.wait_ge(v_made, n_of(it, r, 1, 1))
                wait(dve, av_made, n_of(it, r, NG))
                v.tensor_copy(v_sb[r % 2][:], kv_ps[:, 1]).then_inc(v_copied, 1)

            def sum_squares(it, r):
                dve.wait_ge(k_sq_made, n_of(it, r, 1, 1))
                v.tensor_reduce(k_var[:, 0], k_sq[:], AX, ALU.add).then_inc(k_sum_made, 1)

            def normalise(it, r):
                dve.wait_ge(k_kept, n_of(it, r, 1, 1))
                dve.wait_ge(k_dev_made, n_of(it, r, 1, 1))
                v.tensor_tensor(k_n[:], k_c[:, :, 0:D - 1], per_row(k_var[:, 2], D - 1), ALU.mult)\
                    .then_inc(k_normed, 1)

            def split_keys(it, r):
                dve.wait_ge(k_normed, n_of(it, r, 1, 1))
                hi, lo = (k_hl[r % 2][:, :, i, 0:D - 1] for i in range(2))
                wait(dve, t_made, n_of(it, r, NG, -NG))
                v.tensor_copy(hi, k_n[:]).then_inc(k_hi_made, 1)
                dve.wait_ge(k_hi_made, n_of(it, r, 1, 1))
                v.tensor_tensor(lo, k_n[:], hi.bitcast(f32), ALU.subtract).then_inc(k_split, 1)

            def step(it, r, keys=True, more=True):
                if not is_first(it, r, 0):
                    normalise(it, r - 1)
                    split_keys(it, r - 1)
                if not (is_first(it, r, 0) or is_first(it, r, 1)):
                    copy_turned(it, r - 2, 3)
                if not is_first(it, r, 0):
                    copy_values(it, r - 1)
                if more:
                    high_part(it, r + 1)
                if not is_first(it, r, 0):
                    copy_turned(it, r - 1, 0)
                if keys:
                    sum_squares(it, r)
                if not is_first(it, r, 0):
                    copy_turned(it, r - 1, 1)
                    copy_turned(it, r - 1, 2)

            dve.wait_ge(once("consts"), 1)
            link(v.tensor_copy(ident_r[:], ident[:]))
            dve.wait_ge(once("x_in"), 16)
            layernorm_rows(xn, x, "x")
            dve.wait_ge(once("wv_in"), 16)
            link(v.tensor_copy(wv_hi[:], wv[:]))
            v.tensor_tensor(wv_lo[:], wv[:], wv_hi[:].bitcast(f32), ALU.subtract)\
                .then_inc(once("wv_split"), 1)
            dve.wait_ge(once("xn_turned"), TT)
            v.tensor_copy(x_t[:], s_ps[:]).then_inc(once("x_t_made"), 1)
            dve.wait_ge(once("wk_centred"), 1)
            for c in range(CT):
                wk_ps = (t_ps[:, c % 2] if c < 2 else
                         o_ps[:, 2 * (c % 2):2 * (c % 2) + 2].rearrange("p g t -> p (g t)"))
                link(v.tensor_copy(wk_hi[:, c], wk_ps))
                link(v.tensor_tensor(wk_lo[:, c], wk_ps, wk_hi[:, c].bitcast(f32), ALU.subtract))
            dve.sem_inc(once("wk_split"), 1)
            high_part(0, 0)
            high_part(0, 1)
            dve.wait_ge(once("q_made"), 1)
            heads = [b[:].rearrange("p t (h d) -> p (t h) d", h=H) for b in big]
            qn, tmp = heads
            layernorm(qn, kv_ps[:].rearrange("p t (h d) -> p (t h) d", h=H), qn, tmp, 1e-5, "q",
                      lambda: sum_squares(0, 0))
            dve.wait_ge(once("head_vecs_in"), 16)
            gq, bq, gk, bk = (repeat(head_vecs[:, i], TT * H) for i in range(4))
            link(v.tensor_tensor(qn, qn, gq, ALU.mult))
            link(v.tensor_tensor(qn, qn, bq, ALU.add))
            link(v.tensor_scalar(big[0][:], big[0][:], float(D) ** -0.5, None, ALU.mult))
            link(v.tensor_tensor(tmp, qn, bk, ALU.mult))
            link(v.tensor_reduce(stat[:, 0, 0:TT * H], tmp, AX, ALU.add))
            link(v.tensor_tensor(qn, qn, gk, ALU.mult))
            link(v.tensor_tensor(tmp[:, :, 0:D - 1], qn[:, :, 0:D - 1],
                                 qn[:, :, D - 1:D].to_broadcast([P, TT * H, D - 1]), ALU.subtract))
            link(v.tensor_copy(tmp[:, :, D - 1], stat[:, 0, 0:TT * H]))
            parts = q_parts[:].rearrange("p t h a d -> p (t h) a d")
            link(v.tensor_copy(parts[:, :, 0].bitcast(f32r), tmp))
            link(v.tensor_tensor(parts[:, :, 2], tmp, parts[:, :, 0], ALU.subtract))
            link(v.tensor_copy(parts[:, :, 1], parts[:, :, 0]))
            v.tensor_copy(parts[:, :, 3], parts[:, :, 2]).then_inc(once("q_split"), 1)
            for grp in range(NG):
                dve.wait_ge(once("q_turned"), grp + 1)
                v.tensor_copy(q4[:, HG * grp:HG * grp + HG], q_turned_in[grp % 2]).then_inc(once("q4_made"), 1)

            step(0, 1)
            with dve.Fori(0, nq) as it:
                for r in range(2, 6):
                    step(it, r)
            step(nq, 2)
            step(nq, 3, more=False)
            step(nq, 4, keys=False, more=False)
            copy_turned(nq, 3, 3)

            dve.wait_ge(av_made, NG * (NKT + 1))
            v.tensor_copy(o_t[:, 0:2], o_ps[:, 0:2]).then_inc(once("attention_done"), 1)
            dve.wait_ge(once("x_offset"), 1)
            for i in range(TT):
                dve.wait_ge(once("cross_made"), i + 1)
                link(v.tensor_tensor(x[:, i], x[:, i], pm[:, i], ALU.add))
            layernorm_rows(xn, x, "x1")
            for i in range(TT):
                dve.wait_ge(once("x1n_turned"), i + 1)
                v.tensor_copy(mid_t[:, :, i * P:(i + 1) * P],
                              po[:, i].rearrange("p (c t) -> p c t", c=CT)).then_inc(once("x1_t_made"), 1)
            low(0, 0, 0, 0)
            low(0, 0, 0, 1)
            for i in range(TT):
                dve.wait_ge(once("qkv_made"), i + 1)
                link(v.tensor_tensor(qkv[:, i], pm[:, 0:3].rearrange("p a b -> p (a b)"),
                                     rows[:, 2:5].rearrange("p a b -> p (a b)"), ALU.add))
                dve.sem_inc(once("qkv_copied"), 1)
                v.tensor_scalar(qk_min[:, i], qkv[:, i, 0:2 * C], 0.0, None, ALU.min)\
                    .then_inc(once("qk_min_made"), 1)
                link(v.tensor_scalar(qk_max[:, i], qkv[:, i, 0:2 * C], 0.0, None, ALU.max))
                dve.wait_ge(once("qk_exp"), i + 1)
                v.tensor_tensor(qk_max[:, i], qk_max[:, i], qk_min[:, i], ALU.add)\
                    .then_inc(once("qk_made"), 1)
            for i in range(TT):
                dve.wait_ge(once("qk_turned"), i + 1)
                for k in range(2):
                    v.tensor_copy(qk_t[:, k, :, i * P:(i + 1) * P],
                                  po[:, 2 * i + k].rearrange("p (g t) -> p g t", g=NG))\
                        .then_inc(once("qk_t_made"), 1)
            dve.wait_ge(once("mid_consts"), 1)
            for h in range(H):
                dve.wait_ge(once("lin_scores"), h + 1)
                wait(dve, once("lin_used"), h // HG - 1)
                v.tensor_tensor(masked[h % 8][:], pm[:, h % 4, 0:TOK + P], causal[:], ALU.mult)\
                    .then_inc(once("lin_masked"), 1)
            for grp in range(NG):
                dve.wait_ge(once("lin_used"), grp + 1)
                values, weights = po[:, grp, 0:TOK], po[:, grp, TOK:2 * TOK]
                link(v.tensor_scalar(lin_norm[:, grp], weights, 1e-6, None, ALU.add))
                link(v.reciprocal(lin_norm[:, grp], lin_norm[:, grp]))
                v.tensor_tensor(mid_t[:, grp], values, lin_norm[:, grp], ALU.mult)\
                    .then_inc(once("lin_t_made"), 1)
            low(0, 0, 0, 2)
            low(0, 0, 0, 3)
            dve.wait_ge(once("x1_offset"), 1)
            for i in range(TT):
                dve.wait_ge(once("self_made"), i + 1)
                v.tensor_tensor(x[:, i], x[:, i], pm[:, 2 + i], ALU.add).then_inc(once("x2_made"), 1)
            dve.wait_ge(once("x2_made"), TT)
            layernorm_rows(xn, x, "x2")
            dve.wait_ge(once("x2n_made"), TT)
            row_stats(xn, "nx")
            dve.wait_ge(once("ln_rows_in"), 16)
            for i in range(TT):
                link(v.scalar_tensor_tensor(nx[:, i], xn[:, i], row_mean[:, i, 0:1], lnv[:, 0],
                                            ALU.subtract, ALU.mult))
                v.scalar_tensor_tensor(nx[:, i], nx[:, i], stat[:, 2, i:i + 1], lnv[:, 1],
                                       ALU.mult, ALU.add).then_inc(once("nx_made"), 1)
            for i in range(TT):
                dve.wait_ge(once("nx_turned"), i + 1)
                v.tensor_copy(nx_t[:, :, i * P:(i + 1) * P],
                              f_ps[:, i].rearrange("p (c t) -> p c t", c=CT)).then_inc(once("nx_t_made"), 1)
            dve.wait_ge(once("nx_t_made"), TT)
            link(v.tensor_copy(hid["xn"][0][:], nx_t))
            v.tensor_tensor(hid["xn"][1][:], nx_t, hid["xn"][0][:].bitcast(f32), ALU.subtract)\
                .then_inc(once("xn_split"), 1)
            dve.wait_ge(once("logits"), 1)
            lg = m_ps[:, 0, 0:TT * E].rearrange("p (t e) -> p t e", t=TT)
            link(v.tensor_reduce(rt[:, 2, :, 0], lg, AX, ALU.max))
            v.tensor_tensor(rt[:, 0], lg, per_row(rt[:, 2, :, 0], E), ALU.subtract)\
                .then_inc(once("logits_less_max"), 1)
            dve.wait_ge(once("router_exp"), 1)
            link(v.tensor_reduce(rt[:, 2, :, 0], rt[:, 1], AX, ALU.add))
            link(v.reciprocal(rt[:, 2, :, 1], rt[:, 2, :, 0]))
            link(v.tensor_tensor(rt[:, 3], rt[:, 1], per_row(rt[:, 2, :, 1], E), ALU.mult))
            dve.wait_ge(once("router_consts"), 1)
            v.tensor_copy(pick[:], ident[0:E, 0:E])
            shape = [P, TT, E, E]
            mine = rt[:, 3].unsqueeze(3).to_broadcast(shape)
            others = rt[:, 3].unsqueeze(2).to_broadcast(shape)
            link(v.tensor_tensor(cmp[0], others, mine, ALU.is_gt))
            link(v.tensor_tensor(cmp[1], others, mine, ALU.is_equal))
            link(v.tensor_tensor(cmp[1], cmp[1], lower[:].unsqueeze(1).to_broadcast(shape), ALU.mult))
            link(v.tensor_tensor(cmp[0], cmp[0], cmp[1], ALU.add))
            link(v.tensor_reduce(rt[:, 4], cmp[0], AX, ALU.add))
            link(v.tensor_scalar(rt[:, 4], rt[:, 4], 2.0, None, ALU.is_lt))
            link(v.tensor_tensor(rt[:, 5], rt[:, 4], rt[:, 3], ALU.mult))
            link(v.tensor_reduce(rt[:, 2, :, 0], rt[:, 5], AX, ALU.add))
            link(v.reciprocal(rt[:, 2, :, 1], rt[:, 2, :, 0]))
            v.tensor_tensor(rt[:, 5], rt[:, 5], per_row(rt[:, 2, :, 1], E), ALU.mult)\
                .then_inc(once("gates"), 1)
            dve.wait_ge(once("gates_turned"), 1)
            link(v.tensor_copy(gate_parts[:, 0], m_ps[0:E, 1, 0:TOK]))
            v.tensor_tensor(gate_parts[:, 1], m_ps[0:E, 1, 0:TOK], gate_parts[:, 0].bitcast(f32),
                            ALU.subtract).then_inc(once("gate_split"), 1)
            v.tensor_copy(gate_t[:], m_ps[0:E, 1, 0:TOK]).then_inc(once("gate_t_made"), 1)
            for k in range(2):
                dve.wait_ge(once("gates_spread"), k + 1)
                v.tensor_copy(gate[:, 4 * k:4 * k + 4],
                              f_ps[:, 2 * k:2 * k + 2].rearrange("p a (b c) -> p (a b) c", b=2))\
                    .then_inc(once("gates_copied"), 1)
            dve.wait_ge(once("gates_copied"), 2)

            def high_tile(half, q, per_q, name, dst, e, last, n):
                if name in NORMS:
                    dve.wait_ge(applied, at(half, 2 * FT, q, per_q, FT * e + n + 1))
                else:
                    dve.wait_ge(f_read, at(half, TILES_HALF, q, per_q, FILL_BASE[name] + n + 1 + 4))
                tile, high = stage[n % 4][:], one(hid[dst][0], q * per_q + n)
                if last:
                    factor = one(gate, half * (E // 2) + e)
                    v.tensor_tensor(high, tile, factor, ALU.mult)
                    v.tensor_tensor(tile, tile, factor, ALU.mult).then_inc(h_hi_made, 1)
                else:
                    v.tensor_copy(high, tile).then_inc(h_hi_made, 1)

            def free(half, dst, name):
                order = [l[0] for l in LAYERS]
                k = order.index(name)
                readers = [l[0] for l in LAYERS if l[3] == dst]
                before = [n for n in readers if order.index(n) <= k]
                if before:
                    end = CHUNK_BASE[before[-1]] + CHUNKS[before[-1]]
                else:
                    end = CHUNK_BASE[readers[-1]] + CHUNKS[readers[-1]]
                    dve.wait_ge(w_used, half * end + 4)
                    return
                dve.wait_ge(w_used, half * CHUNKS_HALF + (4 + end))

            def normalisation(half, what):
                if what is None:
                    return
                step, norm = what
                k0 = NORMS.index(norm)
                var, root, scratch = moment[:, 1], moment[:, 2], moment[:, 3]
                if step == "mean":
                    dve.wait_ge(mean_made, half * 2 + (k0 + 1))
                    v.tensor_copy(moment[:, 0], m_ps[:, 0, 0:TOK]).then_inc(mean_copied, 1)
                    dve.wait_ge(mean_copied, half * 2 + (k0 + 1))
                    for k in range(4):
                        part = pre[:, 4 * k:4 * k + 4]
                        v.tensor_tensor(part, part, repeat(moment[:, 0], 4), ALU.subtract)\
                            .then_inc(centred, 1)
                if step == "squares":
                    for k in range(4):
                        dve.wait_ge(sq_made, half * 8 + (4 * k0 + k + 1))
                        v.tensor_reduce(sums[:, 1 + k], sq[k % 2][:].rearrange("p f t -> p t f"), AX,
                                        ALU.add).then_inc(sq_summed, 1)
                if step == "variance":
                    done_before = [ROOT_OPS * k0]

                    def follow(ins):
                        done_before[0] += 1
                        ins.then_inc(root_step, 1)
                        dve.wait_ge(root_step, half * (2 * ROOT_OPS) + done_before[0])

                    i32 = mybir.dt.int32
                    dve.wait_ge(var_made, half * 2 + (k0 + 1))
                    follow(v.tensor_scalar(var, m_ps[:, 1, 0:TOK], 1e-5, None, ALU.add))
                    follow(v.tensor_scalar(root.bitcast(i32), var.bitcast(i32), 1, None,
                                           ALU.logical_shift_right))
                    follow(v.tensor_scalar(root.bitcast(i32), root.bitcast(i32), -1.0,
                                           float(0x5F3759DF), ALU.mult, ALU.add))
                    for _ in range(ROOT_STEPS):
                        follow(v.scalar_tensor_tensor(scratch, root, -0.5, root, ALU.mult, ALU.mult))
                        follow(v.tensor_tensor(scratch, scratch, var, ALU.mult))
                        follow(v.scalar_tensor_tensor(root, scratch, 1.5, root, ALU.add, ALU.mult))
                    for k in range(4):
                        part = pre[:, 4 * k:4 * k + 4]
                        v.tensor_tensor(part, part, repeat(root, 4), ALU.mult).then_inc(scaled, 1)
                if step == "apply":
                    after = next(layer for layer, n in NORM_AFTER.items() if n == norm)
                    with dve.Fori(0, 4) as q:
                        free(half, NORM_OUT[norm], after)
                        for i in range(4):
                            high_tile(half, q, 4, norm, NORM_OUT[norm], k0, True, i)

            with dve.Fori(0, HALVES) as half:
                for name, kind, kt, src, dst, e, last in LAYERS:
                    per = OUT_TILES[name] // layer_chunks(name, kt)
                    for q in quads(dve, name, kt):
                        if kind == "gelu":
                            free(half, dst, name)
                        for i in range(4):
                            if kind == "gelu":
                                for j in range(per):
                                    high_tile(half, q, 4 * per, name, dst, e, last, i * per + j)
                            low(half, q, CHUNK_BASE[name] + 4, i)
                            for n in spread_tiles(name, q, i):
                                norm = STEPS[name, "spread"][1]
                                if n == 0:
                                    free(half, NORM_OUT[norm], name)
                                high_tile(half, 0, 4, norm, NORM_OUT[norm], NORMS.index(norm), True, n)
                            if i == 1:
                                normalisation(half, STEPS.get((name, "second")))
                        if isinstance(q, int) and q == 0:
                            normalisation(half, STEPS.get((name, "four")))
                    if kind == "norm":
                        dve.wait_ge(f_read, half * TILES_HALF + (FILL_BASE[name] + FT + 4))
                        v.tensor_reduce(sums[:, 0], pre[:].rearrange("p f t -> p t f"), AX, ALU.add)\
                            .then_inc(pre_summed, 1)
                    normalisation(half, STEPS.get((name, "end")))
            link(v.tensor_tensor(x[:], x[:], xn[:], ALU.add))
            dve.wait_ge(w_used, 4 + HALVES * CHUNKS_HALF)
            v.tensor_tensor(x[:], x[:], y_ps[:], ALU.add).then_inc(once("result"), 1)

        @block.tensor
        def _(pe):
            t = nc.tensor

            def turn_rows(dst, src_rows, made, turned):
                for i in range(TT):
                    pe.wait_ge(once(made), i + 1)
                    for c in range(CT):
                        ins = t.transpose(dst(c, i), src_rows[:, i, c * P:(c + 1) * P], ident[:])
                    ins.then_inc(once(turned), 1)

            pe.wait_ge(once("consts"), 1)
            pe.wait_ge(once("wk_in"), 16)
            for c in range(CT):
                for b in range(CT):
                    dst = (t_ps[:, c % 2, b * P:(b + 1) * P] if c < 2 else
                           o_ps[:, 2 * (c % 2) + b // 2, (b % 2) * P:(b % 2 + 1) * P])
                    ins = t.matmul(dst, wk[:, b, c * P:(c + 1) * P], centre[:], start=True, stop=True)
            ins.then_inc(once("wk_centred"), 1)
            turn_rows(lambda c, i: s_ps[:, c, i * P:(i + 1) * P], xn, "xn_made", "xn_turned")
            pe.wait_ge(once("x_t_made"), 1)
            pe.wait_ge(once("wq_in"), 16)
            for i in range(TT):
                for c in range(CT):
                    ins = t.matmul(kv_ps[:, i], x_t[:, c, i * P:(i + 1) * P], wq[:, c],
                                   start=(c == 0), stop=(c == CT - 1))
            ins.then_inc(once("q_made"), 1)
            def project(it, r, which, c, n):
                hi, lo = ((wk_hi, wk_lo), (wv_hi, wv_lo))[which]
                left, right = ((ctx_hi, hi), (ctx_lo, hi), (ctx_hi, lo))[n]
                ins = t.matmul(kv_ps[:, which], left[r % 2][:, c], right[:, c],
                               start=(c == 0 and n == 0), stop=(c == CT - 1 and n == 2))
                if c == CT - 1 and n == 2:
                    ins.then_inc((k_made, v_made)[which], 1)

            def projection(it, r, first, last):
                for m in range(first, last):
                    if m == 0:
                        pe.wait_ge(ctx_lo_made, n_of(it, r, 1, 1))
                        wait(pe, k_kept, n_of(it, r))
                    if m == 12:
                        wait(pe, v_copied, n_of(it, r))
                    project(it, r, m // 12, m % 12 // 3, m % 3)

            def turn_keys(it, r, grp):
                if grp == 0:
                    pe.wait_ge(k_split, n_of(it, r, 1, 1))
                wait(pe, kt_even_made, n_of(it, r, 2 * NG, 2 * (grp - 1)))
                wait(pe, kt_odd_made, n_of(it, r, 2 * NG, 2 * (grp - 1)))
                for n in range(HG // 2):
                    h = HG * grp + 2 * n
                    parts = k_hl[r % 2][:, h:h + 2].rearrange("p h a d -> p (h a d)")
                    ins = t.matmul(t_ps[:, grp % 2, n * P:(n + 1) * P], parts, ident_r[:],
                                   start=True, stop=True)
                ins.then_inc(t_made, 1)

            def scores(it, r, grp):
                pe.wait_ge(kt_even_made, n_of(it, r, 2 * NG, 2 * (grp + 1)))
                pe.wait_ge(kt_odd_made, n_of(it, r, 2 * NG, 2 * (grp + 1)))
                wait(pe, probs_made, n_of(it, r, NG, grp))
                for h in range(HG):
                    ins = t.matmul(s_ps[:, h], kT[grp][:, h // 2, h % 2], q4[:, HG * grp + h],
                                   start=True, stop=True)
                ins.then_inc(s_made, 1)

            def attend(it, r, grp):
                pe.wait_ge(probs_made, n_of(it, r, NG, grp + 1))
                pe.wait_ge(v_copied, n_of(it, r, 1, 1))
                for h in range(HG):
                    ins = t.matmul(o_ps[D * h:D * h + D, grp], v_sb[r % 2][:, P * grp + D * h:P * grp + D * h + D],
                                   probs[grp][:, h], start=False, stop=False, skip_group_check=True)
                ins.then_inc(av_made, 1)

            QUARTER, BEFORE = 6, 4

            def step(it, r, project_it=True):
                for q in range(4):
                    a0, a1 = QUARTER * q, QUARTER * (q + 1)
                    half_way = a0 + BEFORE
                    if project_it:
                        projection(it, r, a0, half_way)
                    if not too_early(it, r, q - 2):
                        scores(it, *group(r, q - 2))
                    if project_it:
                        projection(it, r, half_way, a1)
                    if not too_early(it, r, q - 1):
                        turn_keys(it, *group(r, q - 1))
                    if not too_early(it, r, q - 3):
                        attend(it, *group(r, q - 3))

            def group(r, q):
                return r - 1 + q // 4, q % 4

            def too_early(it, r, q):
                return isinstance(it, int) and 4 * it + r - 1 + q // 4 < 0

            pe.wait_ge(once("zeros_made"), 1)
            pe.wait_ge(once("wk_split"), 1)
            for i in range(2):
                ins = t.matmul(o_ps[:, 2 * i:2 * i + 2].rearrange("p g t -> p (g t)"), zeros[:, 0:P],
                               zeros, start=True, stop=True)
            ins.then_inc(av_made, NG)
            pe.wait_ge(once("wv_split"), 1)
            pe.wait_ge(once("q_read"), 1)
            projection(0, 0, 0, 24)
            pe.wait_ge(once("q_split"), 1)
            for grp in range(NG):
                wait(pe, once("q4_made"), grp - 1)
                for h in range(HG):
                    for i in range(TT):
                        ins = t.transpose(q_turned_in[grp % 2][:, h, i * P:(i + 1) * P],
                                          q_parts[:, i, HG * grp + h].rearrange("p a d -> p (a d)"),
                                          ident[:])
                ins.then_inc(once("q_turned"), 1)
            pe.wait_ge(once("q4_made"), NG)
            pe.sem_inc(w_used, 2)
            step(0, 1)
            with pe.Fori(0, nq) as it:
                for r in range(2, 6):
                    step(it, r)
            step(nq, 2)
            step(nq, 3)
            step(nq, 4, project_it=False)
            turn_keys(nq, 3, 3)
            scores(nq, 3, 2)
            attend(nq, 3, 1)
            scores(nq, 3, 3)
            attend(nq, 3, 2)
            attend(nq, 3, 3)

            pe.wait_ge(once("attention_done"), 2)
            pe.wait_ge(once("wp_in"), 16)
            for i in range(TT):
                for c in range(CT):
                    ins = t.matmul(pm[:, i], o_t[:, c, i * P:(i + 1) * P], wp[:, c],
                                   start=(c == 0), stop=(c == CT - 1))
                ins.then_inc(once("cross_made"), 1)
            turn_rows(lambda c, i: po[:, i, c * P:(c + 1) * P], xn, "x1n_made", "x1n_turned")
            pe.wait_ge(once("qkv_w_in"), 16)
            for i in range(TT):
                pe.wait_ge(once("x1_t_made"), i + 1)
                wait(pe, once("qkv_copied"), i)
                for k in range(3):
                    for c in range(CT):
                        ins = t.matmul(pm[:, k], mid_t[:, c, i * P:(i + 1) * P],
                                       qkv_w[:, c, k * C:(k + 1) * C], start=(c == 0), stop=(c == CT - 1))
                ins.then_inc(once("qkv_made"), 1)
            pe.sem_inc(w_used, 2)
            for i in range(TT):
                pe.wait_ge(once("qk_made"), i + 1)
                for k in range(2):
                    for grp in range(NG):
                        ins = t.transpose(po[:, 2 * i + k, grp * P:(grp + 1) * P],
                                          qk_max[:, i, k * C + grp * P:k * C + (grp + 1) * P], ident[:])
                ins.then_inc(once("qk_turned"), 1)

            def lin_scores(h):
                grp, first = h // HG, D * (h % HG)
                q, k = (qk_t[first:first + D, i, grp] for i in range(2))
                pe.wait_ge(once("qk_t_made"), 2 * TT)
                wait(pe, once("lin_masked"), h - 3)
                t.matmul(pm[:, h % 4, 0:TOK], k[:, 0:P], q, start=True, stop=True)
                t.matmul(pm[:, h % 4, TOK:TOK + P], k[:, P:TOK], q[:, P:TOK], start=True, stop=True)\
                    .then_inc(once("lin_scores"), 1)

            def lin_values(grp):
                pe.wait_ge(once("lin_masked"), HG * (grp + 1))
                for j in range(2):
                    for i in range(TT):
                        for h in range(HG):
                            head = HG * grp + h
                            left = ones[:] if j else qkv[:, i, 2 * C + D * head:2 * C + D * (head + 1)]
                            ins = t.matmul(po[D * h:D * h + D, grp, j * TOK + i * P:(j + 1) * TOK],
                                           left, masked[head % 8][:, i * TOK:TOK + i * P],
                                           start=(i == 0), stop=(i == TT - 1), skip_group_check=True)
                ins.then_inc(once("lin_used"), 1)

            pe.wait_ge(once("mid_consts"), 1)
            for h in range(HG):
                lin_scores(h)
            for grp in range(NG):
                if grp + 1 < NG:
                    for h in range(HG):
                        lin_scores(HG * (grp + 1) + h)
                lin_values(grp)
            pe.wait_ge(once("lin_t_made"), NG)
            pe.wait_ge(once("out_w_in"), 16)
            for i in range(TT):
                for c in range(CT):
                    ins = t.matmul(pm[:, 2 + i], mid_t[:, c, i * P:(i + 1) * P], out_w[:, c],
                                   start=(c == 0), stop=(c == CT - 1))
                ins.then_inc(once("self_made"), 1)
            turn_rows(lambda c, i: f_ps[:, i, c * P:(c + 1) * P], nx, "nx_made", "nx_turned")
            pe.wait_ge(once("nx_t_made"), TT)
            pe.wait_ge(once("router_w_in"), 16)
            for i in range(TT):
                for c in range(CT):
                    ins = t.matmul(m_ps[:, 0, i * E:(i + 1) * E], nx_t[:, c, i * P:(i + 1) * P],
                                   router_w[:, c], start=(c == 0), stop=(c == CT - 1))
            ins.then_inc(once("logits"), 1)
            pe.wait_ge(once("gates"), 1)
            for i in range(TT):
                ins = t.transpose(m_ps[0:E, 1, i * P:(i + 1) * P], rt[:, 5, i], ident[:])
            ins.then_inc(once("gates_turned"), 1)
            pe.wait_ge(once("gate_split"), 1)
            for e in range(E):
                for part in range(2):
                    ins = t.matmul(f_ps[:, e // 2, (e % 2) * TOK:(e % 2 + 1) * TOK],
                                   pick[:, e:e + 1].to_broadcast([E, P]), gate_parts[:, part],
                                   start=(part == 0), stop=(part == 1))
                if e % 4 == 3:
                    ins.then_inc(once("gates_spread"), 1)
            pe.wait_ge(once("gate_t_made"), 1)
            pe.wait_ge(once("down_b_in"), 16)
            for i in range(TT):
                t.matmul(y_ps[:, i], gate_t[:, i * P:(i + 1) * P], down_b[:], start=True, stop=True)
            pe.wait_ge(once("gates_copied"), 2)

            def moments(half, what):
                step, norm = what or (None, None)
                k0 = NORMS.index(norm) if norm else 0
                if step == "mean":
                    pe.wait_ge(pre_summed, half * 2 + (k0 + 1))
                    t.matmul(m_ps[:, 0, 0:TOK], mean_w[:], sums[:, 0], start=True, stop=True)\
                        .then_inc(mean_made, 1)
                if step == "variance":
                    for k in range(4):
                        pe.wait_ge(sq_summed, half * 8 + (4 * k0 + k + 1))
                        ins = t.matmul(m_ps[:, 1, 0:TOK], mean_w[:], sums[:, 1 + k], start=(k == 0),
                                       stop=(k == 3))
                    ins.then_inc(var_made, 1)

            with pe.Fori(0, HALVES) as half:
                for name, kind, kt, src, dst, e, last in LAYERS:
                    s_hi, s_lo = hid[src]
                    per = OUT_TILES[name] // layer_chunks(name, kt)
                    if src == "xn":
                        pe.wait_ge(once("xn_split"), 1)

                    def source(k):
                        if src != "xn":
                            made = STAGE_BASE[SOURCE[name]] + k + 1 + 4
                            pe.wait_ge(h_made, half * TILES_HALF + made)

                    for q in quads(pe, name, kt):
                        for i in range(4):
                            pe.wait_ge(w_lo_made, at(half, CHUNKS_HALF, q, 4, CHUNK_BASE[name] + i + 1))
                            if kind == "down":
                                hi, lo = (w[i][:].rearrange("p (f n) -> p f n", f=4) for w in (w_hi, w_lo))
                                for j in range(4):
                                    source(4 * i + j)
                                    for tt in range(TT):
                                        rows_ = slice(tt * P, (tt + 1) * P)
                                        for l, w in ((s_hi, hi), (s_lo, hi), (s_hi, lo)):
                                            ins = t.matmul(y_ps[:, tt], l[:, 4 * i + j, rows_], w[:, j],
                                                           start=False, stop=False, skip_group_check=True)
                            for j in range(per):
                                n = i * per + j
                                slot = n % 4
                                pe.wait_ge(f_read, at(half, TILES_HALF, q, 4 * per, FILL_BASE[name] + n + 1))
                                hi, lo = (w[i][:].rearrange("p (k n) -> p k n", k=kt) for w in (w_hi, w_lo))
                                cols = slice(j * P, (j + 1) * P)
                                for k in range(kt):
                                    if i == 0 and j == 0:
                                        source(k)
                                    for m, (w, r) in enumerate(((hi, s_hi), (hi, s_lo), (lo, s_hi))):
                                        ins = t.matmul(f_ps[:, slot, 0:TOK], w[:, k, cols], r[:, k],
                                                       start=(k == 0 and m == 0),
                                                       stop=(k == kt - 1 and m == 2))
                                if j < per - 1:
                                    ins.then_inc(f_made, 1)
                            ins.then_inc(w_used, 1)
                            if i == 1:
                                moments(half, STEPS.get((name, "second")))
                        if isinstance(q, int) and q == 0:
                            moments(half, STEPS.get((name, "four")))
                    moments(half, STEPS.get((name, "end")))


def kernel(**inputs):
    import numpy as np
    import concourse.bacc as bacc
    from concourse.bass_utils import run_bass_kernel_spmd as run

    i = {k: np.asarray(v) for k, v in inputs.items()}
    f = {k[len("L0_ffn_"):]: v for k, v in i.items() if k.startswith("L0_ffn_")}
    xa = {k[len("L0_xattn_"):]: v for k, v in i.items() if k.startswith("L0_xattn_")}

    def chunks(w):
        return w.reshape(-1, P, w.shape[1]).transpose(1, 0, 2)

    def stream(w, name):
        k, n = w.shape
        if name == "down":
            return w.reshape(E // HALVES, 4, P, n).transpose(0, 2, 1, 3).reshape(-1, P, CHUNK)
        kt = k // P
        return w.reshape(kt, P, -1, CHUNK // kt).transpose(2, 1, 0, 3).reshape(-1, P, CHUNK)

    def columns(v):
        return v.reshape(-1, P).T

    spec = {"spec0": "spec0_W", "spec1a": "spec1a_W", "spec1b": "spec1b_W", "spec2": "spec2_W"}
    w = []
    for half in range(HALVES):
        for name, kind, kt, src, dst, e, last in LAYERS:
            if name.startswith("up"):
                w.append(stream(f["up_W"][half * 4 + e], "up"))
            elif kind == "down":
                w.append(stream(f["down_W"][half * 4 + e], "down"))
            else:
                w.append(stream(f[spec[name]][half], name))
    arrays = {
        "x": chunks(i["x"][0]),
        "ctx": i["ctx_1024"][0].reshape(KT, P, CT, P).transpose(0, 3, 2, 1).reshape(KT, P, C),
        "wq": chunks(xa["Wq"].T),
        "wk": chunks(xa["Wk"]),
        "wv": chunks(xa["Wv"].T),
        "wp": chunks(xa["Wp"].T),
        "head_vecs": np.broadcast_to(np.stack([xa["gq"], xa["bq"], xa["gk"], xa["bk"]]), (P, 4, D)),
        "bias_rows": np.broadcast_to(
            np.concatenate([xa["bp"], i["L0_attn_out_b"], i["L0_attn_qkv_b"]]).reshape(5, C), (P, 5, C)),
        "qkv_w": chunks(i["L0_attn_qkv_w"]),
        "out_w": chunks(i["L0_attn_out_w"]),
        "ln_rows": np.broadcast_to(np.stack([f["ln_g"], f["ln_b"]]), (P, 2, C)),
        "router_w": chunks(f["router_w"]),
        "down_b": f["down_b"],
        "bias_cols": np.concatenate([columns(f[n]) for n in (
            "up_b", "spec0_b", "ln0_g", "ln0_b", "spec1a_b", "spec1b_b", "ln1_g", "ln1_b", "spec2_b")],
            axis=1),
        "w": np.concatenate(w),
    }
    arrays = {k: np.ascontiguousarray(v) for k, v in arrays.items()}
    nc = bacc.Bacc("TRN2", target_bir_lowering=False, num_devices=1,
                   dynamic_dma_scratch_size=1024)
    given = {k: nc.dram_tensor(k + "_dram", v.shape, mybir.dt.from_np(v.dtype), kind="ExternalInput").ap()
             for k, v in arrays.items()}
    out = nc.dram_tensor("out_dram", (P, TT, C), mybir.dt.float32, kind="ExternalOutput").ap()
    perceiver_block(nc, given, out)
    r = run(nc, [{k + "_dram": v for k, v in arrays.items()}], core_ids=[0])
    return r.results[0]["out_dram"].transpose(1, 0, 2).reshape(1, TOK, C)
```
